# Optimizing a Trainium2 kernel written in Bass

```python
import numpy as np
import jax
import jax.numpy as jnp

def _softmax(x, axis=-1):
    return jax.nn.softmax(x, axis=axis)

def _gelu(x):
    return jax.nn.gelu(x, approximate=True)

def _silu(x):
    return jax.nn.silu(x)

def _sigmoid(x):
    return jax.nn.sigmoid(x)

def _layernorm(x, axis=-1, eps=1e-05):
    m = jnp.mean(x, axis=axis, keepdims=True)
    v = jnp.var(x, axis=axis, keepdims=True)
    return (x - m) / jnp.sqrt(v + eps)

def _scatter_add(tgt, idx, src, axis=0):
    return tgt.at[idx].add(src)

def _segment_sum(src, seg, n):
    return jax.ops.segment_sum(src, seg, n)
kernel_name = 'mk_xattn_ffn_d2_seqx_r4_f6ba7a'

def setup_inputs(seed: int=0):
    np.random.seed(seed)
    _w = jnp.asarray

    def _rec_inputs():
        import jax
        import jax.numpy as jnp
        _rk = jax.random.key(seed)
        x = 7.22e-05 + 1 * jax.random.normal(jax.random.fold_in(_rk, 1), (2, 1024, 256), jnp.float32)
        _lenS = 1024 - jax.random.randint(jax.random.fold_in(_rk, 7), (2,), 0, max(1, 1024 // 4) + 1, jnp.int32)
        _lenS2 = 64 - jax.random.randint(jax.random.fold_in(_rk, 8), (2,), 0, max(1, 64 // 4) + 1, jnp.int32)
        _ctx_1024P = jax.random.normal(jax.random.fold_in(_rk, 11), (2, 16, 256), jnp.float32)
        _ctx_1024c = jax.random.dirichlet(jax.random.fold_in(_rk, 511), 0.3 * jnp.ones((16,), jnp.float32), (2, 64))
        _ctx_1024t = jnp.einsum('bsk,bkd->bsd', _ctx_1024c, _ctx_1024P)
        _ctx_1024t = _ctx_1024t * jax.lax.rsqrt(jnp.mean(jnp.square(_ctx_1024t)) + 1e-12) * 0.953939
        ctx_1024 = 4.13588e-05 + 0.999923 * (_ctx_1024t + 0.3 * jax.random.normal(jax.random.fold_in(_rk, 611), (2, 64, 256), jnp.float32))
        _validS = jnp.arange(1024)[None, :] < _lenS[:, None]
        _validS2 = jnp.arange(64)[None, :] < _lenS2[:, None]
        _causal = jnp.tril(jnp.ones((1024, 1024), dtype=bool))
        mask_Bx1xSxS2_ff0 = jnp.where(jnp.ones((2, 1, 1024, 64), dtype=bool), 0.0, -1000000000.0).astype(jnp.float32)
        return (x, ctx_1024, mask_Bx1xSxS2_ff0)
    x, ctx_1024, mask_Bx1xSxS2_ff0 = _rec_inputs()

    def _L0_xattn_setup():
        import jax, jax.numpy as jnp
        import numpy as np
        H = 16
        DK = 64
        D_MODEL = 256
        key = jax.random.key(seed)
        ks = jax.random.split(key, 9)
        B, T, D = (4, 512, D_MODEL)
        scale = 1.0 / np.sqrt(D)
        return {'Q': jax.random.normal(ks[0], (B, T, D), dtype=jnp.float32), 'K': jax.random.normal(ks[1], (B, T, D), dtype=jnp.float32), 'V': jax.random.normal(ks[2], (B, T, D), dtype=jnp.float32), 'Wq': jax.random.normal(ks[3], (D, D), dtype=jnp.float32) * scale, 'bq': jax.random.normal(ks[4], (D,), dtype=jnp.float32) * scale, 'Wk': jax.random.normal(ks[5], (D, D), dtype=jnp.float32) * scale, 'bk': jax.random.normal(ks[6], (D,), dtype=jnp.float32) * scale, 'Wv': jax.random.normal(ks[7], (D, D), dtype=jnp.float32) * scale, 'bv': jax.random.normal(ks[8], (D,), dtype=jnp.float32) * scale}
    _L0_xattn_all = _L0_xattn_setup()
    _L0_xattn_in = {k: v for k, v in _L0_xattn_all.items() if k in ('Wq', 'bq', 'Wk', 'bk', 'Wv', 'bv')}
    del _L0_xattn_all

    def _L0_ffn_setup():
        import jax, jax.numpy as jnp
        import numpy as np
        E = 32
        K = 4
        H = 256
        F = 256
        LIMIT = 7.0
        ALPHA = 1.702
        EPS = 1e-05

        def _rmsnorm(x, scale):
            t = x * jax.lax.rsqrt(jnp.mean(x * x, axis=-1, keepdims=True) + EPS)
            return t * scale

        def _swiglu(h):
            glu = jnp.minimum(h[..., ::2], LIMIT)
            lin = jnp.clip(h[..., 1::2], -LIMIT, LIMIT)
            return glu * jax.nn.sigmoid(ALPHA * glu) * (lin + 1.0)
        key = jax.random.key(seed)
        ks = jax.random.split(key, 8)
        B, S = (1, 256)
        x = jax.random.normal(ks[0], (B, S, H), dtype=jnp.float32)
        norm_scale = jnp.ones((H,), dtype=jnp.float32)
        gate_w = jax.random.normal(ks[1], (E, H), dtype=jnp.float32) * 0.02
        gate_b = jnp.zeros((E,), dtype=jnp.float32)
        w1 = jax.random.normal(ks[2], (E, 2 * F, H), dtype=jnp.float32) * 0.02
        b1 = jnp.zeros((E, 2 * F), dtype=jnp.float32)
        w2 = jax.random.normal(ks[3], (E, H, F), dtype=jnp.float32) * 0.02
        b2 = jnp.zeros((E, H), dtype=jnp.float32)
        return {'x': x, 'norm_scale': norm_scale, 'gate_w': gate_w, 'gate_b': gate_b, 'w1': w1, 'b1': b1, 'w2': w2, 'b2': b2}
    _L0_ffn_all = _L0_ffn_setup()
    _L0_ffn_in = {k: v for k, v in _L0_ffn_all.items() if k in ('norm_scale', 'gate_w', 'gate_b', 'w1', 'b1', 'w2', 'b2')}
    del _L0_ffn_all

    def _L1_xattn_setup():
        import jax, jax.numpy as jnp
        import numpy as np
        DEPTH = 64
        key = jax.random.key(seed)
        ks = jax.random.split(key, 7)
        B, F, T, H = (2, 512, 512, 256)
        N, D = (16, 64)
        s = 1.0 / np.sqrt(H)
        return {'query_input': jax.random.normal(ks[0], (B, F, H), jnp.float32), 'source_input': jax.random.normal(ks[1], (B, T, H), jnp.float32), 'bias': jnp.zeros((B, 1, F, T), jnp.float32), 'wq': jax.random.normal(ks[2], (H, N, D), jnp.float32) * s, 'wk': jax.random.normal(ks[3], (H, N, D), jnp.float32) * s, 'wv': jax.random.normal(ks[4], (H, N, D), jnp.float32) * s, 'wo': jax.random.normal(ks[5], (N, D, H), jnp.float32) * s}
    _L1_xattn_all = _L1_xattn_setup()
    _L1_xattn_in = {k: v for k, v in _L1_xattn_all.items() if k in ('wq', 'wk', 'wv', 'wo')}
    del _L1_xattn_all

    def _L1_ffn_setup():
        import jax, jax.numpy as jnp
        import numpy as np
        H, I, E_ROUTED, TOP_K = (256, 704, 7, 2)
        B, S = (4, 512)

        def _expert(h, g, u, d):
            return jnp.einsum('...i,hi->...h', jax.nn.silu(h @ g.T) * (h @ u.T), d)
        key = jax.random.key(seed)
        ks = jax.random.split(key, 10)
        sc = 0.02
        return {'x': jax.random.normal(ks[0], (B, S, H), dtype=jnp.float32), 'sg': jax.random.normal(ks[1], (I, H), dtype=jnp.float32) * sc, 'su': jax.random.normal(ks[2], (I, H), dtype=jnp.float32) * sc, 'sd': jax.random.normal(ks[3], (H, I), dtype=jnp.float32) * sc, 'rg': jax.random.normal(ks[4], (E_ROUTED, I, H), dtype=jnp.float32) * sc, 'ru': jax.random.normal(ks[5], (E_ROUTED, I, H), dtype=jnp.float32) * sc, 'rd': jax.random.normal(ks[6], (E_ROUTED, H, I), dtype=jnp.float32) * sc, 'wr': jax.random.normal(ks[7], (E_ROUTED, H), dtype=jnp.float32) * sc, 'rb': jnp.zeros((E_ROUTED,), dtype=jnp.float32)}
    _L1_ffn_all = _L1_ffn_setup()
    _L1_ffn_in = {k: v for k, v in _L1_ffn_all.items() if k in ('sg', 'su', 'sd', 'rg', 'ru', 'rd', 'wr', 'rb')}
    del _L1_ffn_all
    return {'x': x, 'ctx_1024': ctx_1024, 'mask_Bx1xSxS2_ff0': mask_Bx1xSxS2_ff0, 'L0_xattn_Wq': _L0_xattn_in['Wq'], 'L0_xattn_bq': _L0_xattn_in['bq'], 'L0_xattn_Wk': _L0_xattn_in['Wk'], 'L0_xattn_bk': _L0_xattn_in['bk'], 'L0_xattn_Wv': _L0_xattn_in['Wv'], 'L0_xattn_bv': _L0_xattn_in['bv'], 'L0_ffn_norm_scale': _L0_ffn_in['norm_scale'], 'L0_ffn_gate_w': _L0_ffn_in['gate_w'], 'L0_ffn_gate_b': _L0_ffn_in['gate_b'], 'L0_ffn_w1': _L0_ffn_in['w1'], 'L0_ffn_b1': _L0_ffn_in['b1'], 'L0_ffn_w2': _L0_ffn_in['w2'], 'L0_ffn_b2': _L0_ffn_in['b2'], 'L1_xattn_wq': _L1_xattn_in['wq'], 'L1_xattn_wk': _L1_xattn_in['wk'], 'L1_xattn_wv': _L1_xattn_in['wv'], 'L1_xattn_wo': _L1_xattn_in['wo'], 'L1_ffn_sg': _L1_ffn_in['sg'], 'L1_ffn_su': _L1_ffn_in['su'], 'L1_ffn_sd': _L1_ffn_in['sd'], 'L1_ffn_rg': _L1_ffn_in['rg'], 'L1_ffn_ru': _L1_ffn_in['ru'], 'L1_ffn_rd': _L1_ffn_in['rd'], 'L1_ffn_wr': _L1_ffn_in['wr'], 'L1_ffn_rb': _L1_ffn_in['rb']}

def reference(x, ctx_1024, mask_Bx1xSxS2_ff0, L0_xattn_Wq, L0_xattn_bq, L0_xattn_Wk, L0_xattn_bk, L0_xattn_Wv, L0_xattn_bv, L0_ffn_norm_scale, L0_ffn_gate_w, L0_ffn_gate_b, L0_ffn_w1, L0_ffn_b1, L0_ffn_w2, L0_ffn_b2, L1_xattn_wq, L1_xattn_wk, L1_xattn_wv, L1_xattn_wo, L1_ffn_sg, L1_ffn_su, L1_ffn_sd, L1_ffn_rg, L1_ffn_ru, L1_ffn_rd, L1_ffn_wr, L1_ffn_rb):
    import jax
    import jax.numpy as jnp

    def _L0_xattn_ref(Q, K, V, Wq, bq, Wk, bk, Wv, bv):
        import jax, jax.numpy as jnp
        import numpy as np
        H = 16
        DK = 64
        D_MODEL = 256
        B = Q.shape[0]

        def proj(x, W, b):
            y = jnp.einsum('btd,ed->bte', x, W) + b
            return y.reshape(B, -1, H, DK).transpose(0, 2, 1, 3)
        q = proj(Q, Wq, bq)
        k = proj(K, Wk, bk)
        v = proj(V, Wv, bv)
        scores = jnp.einsum('bhqd,bhkd->bhqk', q, k) / jnp.sqrt(jnp.float32(DK))
        attn = jax.nn.softmax(scores, axis=-1)
        out = jnp.einsum('bhqk,bhkd->bhqd', attn, v)
        return out.transpose(0, 2, 1, 3).reshape(B, -1, D_MODEL)

    def _L0_ffn_ref(x, norm_scale, gate_w, gate_b, w1, b1, w2, b2):
        import jax, jax.numpy as jnp
        import numpy as np
        E = 32
        K = 4
        H = 256
        F = 256
        LIMIT = 7.0
        ALPHA = 1.702
        EPS = 1e-05

        def _rmsnorm(x, scale):
            t = x * jax.lax.rsqrt(jnp.mean(x * x, axis=-1, keepdims=True) + EPS)
            return t * scale

        def _swiglu(h):
            glu = jnp.minimum(h[..., ::2], LIMIT)
            lin = jnp.clip(h[..., 1::2], -LIMIT, LIMIT)
            return glu * jax.nn.sigmoid(ALPHA * glu) * (lin + 1.0)
        B, S, _ = x.shape
        t = _rmsnorm(x, norm_scale)
        g = t @ gate_w.T + gate_b
        tf = t.reshape(-1, H)
        gf = g.reshape(-1, E)
        T = tf.shape[0]
        vals, idx = jax.lax.top_k(gf, K)
        w = jax.nn.softmax(vals, axis=-1)
        combine = jnp.zeros((T, E), dtype=tf.dtype).at[jnp.arange(T)[:, None], idx].add(w)
        h1 = jnp.einsum('th,efh->tef', tf, w1) + b1
        h = _swiglu(h1)
        hw = h * combine[:, :, None]
        out = jnp.einsum('tef,ehf->th', hw, w2) + combine @ b2
        return x + out.reshape(B, S, H)

    def _L1_xattn_ref(query_input, source_input, bias, wq, wk, wv, wo):
        import jax, jax.numpy as jnp
        import numpy as np
        DEPTH = 64
        q = jnp.einsum('bfd,dnh->bfnh', query_input, wq)
        k = jnp.einsum('btd,dnh->btnh', source_input, wk)
        v = jnp.einsum('btd,dnh->btnh', source_input, wv)
        q = q * DEPTH ** (-0.5)
        logits = jnp.einsum('btnh,bfnh->bnft', k, q) + bias
        weights = jax.nn.softmax(logits, axis=-1)
        ctx = jnp.einsum('bnft,btnh->bfnh', weights, v)
        return jnp.einsum('bfnh,nhd->bfd', ctx, wo)

    def _L1_ffn_ref(x, sg, su, sd, rg, ru, rd, wr, rb):
        import jax, jax.numpy as jnp
        import numpy as np
        H, I, E_ROUTED, TOP_K = (256, 704, 7, 2)
        B, S = (4, 512)

        def _expert(h, g, u, d):
            return jnp.einsum('...i,hi->...h', jax.nn.silu(h @ g.T) * (h @ u.T), d)
        shared_out = _expert(x, sg, su, sd)
        logits = x @ wr.T + rb
        probs = jax.nn.softmax(logits, axis=-1)
        scores, idx = jax.lax.top_k(probs, TOP_K)
        scores = scores / scores.sum(axis=-1, keepdims=True)
        w = jnp.sum(scores[..., None] * jax.nn.one_hot(idx, E_ROUTED, dtype=x.dtype), axis=-2)
        out = shared_out
        for e in range(E_ROUTED):
            out = out + w[..., e:e + 1] * _expert(x, rg[e], ru[e], rd[e])
        return out
    x = x + _L0_xattn_ref(_layernorm(x, axis=-1), ctx_1024, ctx_1024, L0_xattn_Wq, L0_xattn_bq, L0_xattn_Wk, L0_xattn_bk, L0_xattn_Wv, L0_xattn_bv)
    x = x + _L0_ffn_ref(_layernorm(x, axis=-1), L0_ffn_norm_scale, L0_ffn_gate_w, L0_ffn_gate_b, L0_ffn_w1, L0_ffn_b1, L0_ffn_w2, L0_ffn_b2)
    x = x + _L1_xattn_ref(_layernorm(x, axis=-1), ctx_1024, mask_Bx1xSxS2_ff0, L1_xattn_wq, L1_xattn_wk, L1_xattn_wv, L1_xattn_wo)
    x = x + _L1_ffn_ref(_layernorm(x, axis=-1), L1_ffn_sg, L1_ffn_su, L1_ffn_sd, L1_ffn_rg, L1_ffn_ru, L1_ffn_rd, L1_ffn_wr, L1_ffn_rb)
    return x

_drawn_inputs = setup_inputs


def setup_inputs(seed=0):
    import zlib

    import numpy as np

    out = dict(_drawn_inputs(seed))
    spreads = {'L0_ffn_norm_scale': (1.0, 0.6),
     'L0_ffn_gate_b': (0.0, 0.525),
     'L0_ffn_b1': (0.0, 0.8),
     'L0_ffn_b2': (0.0, 0.377),
     'L1_ffn_rb': (0.0, 0.8)}
    factors = {'L0_xattn_bq': 3.804,
     'L0_xattn_bk': 8.0,
     'L0_ffn_w1': 4.465,
     'L0_ffn_w2': 4.162,
     'L1_ffn_sg': 4.876,
     'L1_ffn_su': 4.508,
     'L1_ffn_sd': 4.556,
     'L1_ffn_rg': 7.077,
     'L1_ffn_ru': 7.014,
     'L1_ffn_rd': 6.978,
     'L1_ffn_wr': 8.0}
    for name, (base, spread) in spreads.items():
        noise = np.random.default_rng([zlib.crc32(name.encode()), seed]).standard_normal(out[name].shape)
        drawn = base * np.exp(spread * noise) if base else spread * noise
        out[name] = jnp.asarray(drawn.astype(out[name].dtype))
    for name, factor in factors.items():
        out[name] = (out[name] * factor).astype(out[name].dtype)
    return out
```

```python
from contextlib import ExitStack

import numpy as np

import concourse.bass as bass
from concourse import mybir

F32 = mybir.dt.float32
BF16 = mybir.dt.bfloat16
I32 = mybir.dt.int32
U32 = mybir.dt.uint32
ALU = mybir.AluOpType
ACT = mybir.ActivationFunctionType
AX = mybir.AxisListType

P = 128
B, S, D, S2 = 2, 1024, 256, 64
FK = D // P
NT = B * S // P
NPAIR = NT // 2
J = 4
C0, KEYS0 = 4, S2 // J
DH = 64
H1, HP1 = 16, 8
EPS = 1e-5
E0, K0, F0 = 32, 4, 256
E1, K1, F1 = 7, 2, 704
EC1 = 8
LIMIT, ALPHA = 7.0, 1.702
NC1 = 2
FC1 = F1 // NC1
SUB1 = [(0, 128), (128, 128), (256, FC1 - 256)]
T0 = (NT * P * K0 + 127 * E0) // P
T0 += T0 % 2
T1 = (NT * P * K1 + 127 * E1) // P
T1 += T1 % 2
R0 = 8
W0 = FK * 2 * F0 + (F0 // P) * D
GU1 = FK * NC1 * 2 * FC1
W1 = GU1 + NC1 * 3 * D
B0 = 2 * F0 + D
EARLY = 6
SHARED_SLOTS = 2
AHEAD = 2
SHARED_A, SHARED_B = 8, 8
N1 = SHARED_A + T1 + SHARED_B
MID1 = SHARED_A + T1


def wait(eng, sem, n):
    if not (isinstance(n, int) and n <= 0):
        eng.wait_ge(sem, n)


class Tile:

    def __init__(self, m, q, u=2):
        self.m, self.q, self.u, self.t = m, q, u, u * m + q
        self.p = q % 2
        self.half = m * (u // 2) + q // 2
        self.pair = q // 2 % 2

    def plus(self, d):
        return Tile(self.m + (self.q + d) // self.u, (self.q + d) % self.u, self.u)

    def exists(self, lo, hi):
        return not isinstance(self.t, int) or lo <= self.t < hi


def over_tiles(eng, lo, hi, body, lead=2, tail=2, u=2):
    a, z = -(-(lo + lead) // u) * u, (hi - tail) // u * u
    for t in range(lo, min(a, hi)):
        body(Tile(t // u, t % u, u))
    if z > a:
        with eng.Fori(a // u, z // u) as m:
            for q in range(u):
                body(Tile(m, q, u))
    for t in range(max(a, z), hi):
        body(Tile(t // u, t % u, u))


def alone(eng, sem):
    eng.sem_inc(sem, 1)


def span(i, n=1):
    return slice(i, i + n) if isinstance(i, int) else bass.ds(i, n)


class Chain:

    def __init__(self, eng, sem):
        self.eng, self.sem, self.n, self.base = eng, sem, 0, 0

    def __call__(self, ins):
        ins.then_inc(self.sem, 1)
        self.n = self.n + 1

    def wait(self):
        self.eng.wait_ge(self.sem, self.n)

    def step(self, base, per, t):
        self.n = base + per * t
        self.base, self.per, self.now = base, per, t

    def stepped(self):
        d = self.n - (self.base + self.per * self.now)
        assert not isinstance(d, int) or d == self.per, d


def build(nc, a, out):
    ctx = ExitStack()
    with ctx:
        def sb(name, shape, dt=F32):
            return ctx.enter_context(nc.sbuf_tensor(name, shape, dt))

        def sem(name):
            return ctx.enter_context(nc.semaphore(name))

        xres = sb("xres", [P, NT, D])
        normed = sb("normed", [P, NT, D])
        big = sb("big", [P, 8 * W1])
        w1s = big[:, :].rearrange("p (e w) -> p e w", e=8)
        ring = big[:, 0:R0 * (W0 + B0)].rearrange("p (r w) -> p r w", r=R0)
        o = (R0 - SHARED_SLOTS) * (W0 + B0)
        att_in = big[:, o:o + FK * H1 * DH]
        att_in_v = att_in.rearrange("p (k n) -> p k n", k=FK)
        o += FK * H1 * DH
        att_w = big[:, o:o + HP1 * D]
        att_w_v = att_w.rearrange("p (h n) -> p h n", h=HP1)
        o += HP1 * D
        blk1 = big[:, o:o + HP1 * B * 2 * S2]
        blk1_v = blk1.rearrange("p (h b c s) -> p h b c s", h=HP1, b=B, c=2)
        o += HP1 * B * 2 * S2
        tabA0 = big[:, o:o + 3 * 512].rearrange("p (k b j c s) -> p k b j c s", k=3, b=B, j=J, c=C0)
        o += 3 * 512
        tabV0_ = big[:, o:o + B * 2 * 512]
        tabV0 = tabV0_.rearrange("p (b q j d) -> p b q j d", b=B, q=2, j=2)
        o += B * 2 * 512
        ab = big[:, o:o + 3072]
        o = 8 * W1 - B * FK * H1 * S2 - B * HP1 * D
        assert (R0 - SHARED_SLOTS) * (W0 + B0) + 3 * 2048 + 1536 + 2048 + 3072 <= o
        assert SHARED_SLOTS * (W0 + B0) <= 3 * 2048
        tabA = big[:, o:o + B * FK * H1 * S2].rearrange("p (b k n) -> p b k n", b=B, k=FK)
        o += B * FK * H1 * S2
        tabV = big[:, o:o + B * HP1 * D].rearrange("p (b h n) -> p b h n", b=B, h=HP1)
        o += B * HP1 * D
        assert o == 8 * W1

        ident = sb("ident", [P, P])
        ones_b = sb("ones_b", [P, P], BF16)
        tri_b = sb("tri_b", [P, P], BF16)
        mhalf = sb("mhalf", [P, 2])
        eps_t = sb("eps_t", [P, 2])
        stats = sb("stats", [P, 2, 6])
        mv = sb("mv", [P, 2, 2, 2])
        rs = sb("rs", [P, 2, 2])
        rms = sb("rms", [P, 2, 2])
        rtmp = sb("rtmp", [P, 1, 2])
        WORK = 5376
        work = sb("work", [P, WORK])

        def carve(parts):
            at, got = 0, []
            for n in parts:
                got.append(work[:, at:at + n])
                at += n
            assert at <= WORK, at
            return got

        (w0q_, w0k_, w0v_, kblk0_, crep_, bqb_, bvb) = carve([512, 512, 512, 512, 1024, 256, 256])
        w0q = w0q_.rearrange("p (k n) -> p k n", k=2)
        w0k = w0k_.rearrange("p (k n) -> p k n", k=2)
        w0v = w0v_.rearrange("p (k n) -> p k n", k=2)
        kblk0 = kblk0_.rearrange("p (m c n) -> p m c n", m=2, c=2)
        crep = crep_.rearrange("p (k b j c s) -> p k b j c s", k=FK, b=B, j=J, c=C0)
        bqb = bqb_.rearrange("p (m n) -> p m n", m=2)
        ctxT = sb("ctxT", [P, FK, B * S2])
        b0c = sb("b0c", [P, 2, 2])

        xn_a = ab[:, 0:1024].rearrange("p (q n) -> p q n", q=2)
        xT_a = ab[:, 1024:2048].rearrange("p (q n) -> p q n", q=2)
        sc0 = ab[:, 2048:2304].rearrange("p (q n) -> p q n", q=2)
        aT0 = ab[:, 2304:2560].rearrange("p (q n) -> p q n", q=2)
        blkmask = ab[:, 2560:2816]
        gx = sb("gx", [P, 2, 512])
        scale_b = ab[:, 2816:3072]
        gateT = sb("gateT", [P, FK, E0 + E1])
        gate_b = sb("gate_b", [P, E0 + E1])
        sm0 = sb("sm0", [P, 4, 16])

        logits = sb("logits", [P, NT, E0])
        top = sb("top", [P, NT, 8])
        topi = sb("topi", [P, NT, 8], U32)
        wexp = sb("wexp", [P, NT, K0])
        wsum = sb("wsum", [P, 2, NT])
        wgt = [sb(f"wgt{l}", [P, NT, k]) for l, k in ((0, K0), (1, K1))]
        slot_i = [sb(f"slot_i{l}", [P, k, NT], I32) for l, k in ((0, K0), (1, K1))]
        info = [sb(f"info{l}", [1, 3, n], I32) for l, n in ((0, T0), (1, N1))]
        (r_topf, r_one, r_mask, r_cum, r_slot, r_tmp, r_small) = carve([128, 1024, 256, 288, 512, 512, 1024])
        xn_r = work[:, 4320:5344].rearrange("p (q n) -> p q n", q=2)
        topf = r_topf.rearrange("p (t k) -> p t k", k=8)
        slots_f = r_small[:, 700:764].rearrange("p (k t) -> p k t", t=NT)
        cnt_f = r_small[:, 16:48]
        cnt_i = r_small[:, 48:80].bitcast(I32)
        tiles_f = r_small[:, 80:112]
        ends_f = r_small[:, 112:144]
        base_f = r_small[:, 144:176]
        ones_f = r_small[:, 176:208]
        cmp_f = r_small[:, 208:240]
        te_col = r_small[:, 240:242]
        te_row = r_small[0:1, 242:338]
        fl_row = r_small[0:1, 338:434]
        rk_row = r_small[0:1, 434:530]
        one_row = r_small[0:1, 530:626]
        pidx = r_small[:, 626:627]
        iota_e = r_small[:, 628:660]

        (xr0_, xT0_, hb_, glu_, lin_, sig_, hs_, hT_, y0_) = carve([1024, 512, 512, 256, 256, 256, 512, 512, 1024])
        xr0 = xr0_.rearrange("p (q k n) -> p q k n", q=2, k=2)
        xT0 = xT0_.rearrange("p (q k n) -> p q k n", q=2, k=2)
        hs0 = hs_.rearrange("p (q n) -> p q n", q=2)
        hT0 = hT_.rearrange("p (q k n) -> p q k n", q=2, k=2)
        y0 = y0_.rearrange("p (q k n) -> p q k n", q=2, k=2)

        (xn1_, xT1_, s1_, aT1_, g1_, mk_) = carve([512, 512, 2048, 1024, 1024, 128])
        xn1 = xn1_.rearrange("p (q n) -> p q n", q=2)
        xT1 = xT1_.rearrange("p (q k n) -> p q k n", q=2, k=2)
        sc1 = s1_.rearrange("p (q n) -> p q n", q=2)
        aT1 = aT1_.rearrange("p (h n) -> p h n", h=HP1)
        msk = mk_.rearrange("p (q n) -> p q n", q=2)
        sm1 = sb("sm1", [P, 2, 3, H1])

        (xr1_, xTe_, si_, hh_, hTe_, y1_) = carve([512, 512, 704, 704, 768, 512])
        xr1 = xr1_.rearrange("p (q n) -> p q n", q=2)
        xTe = xTe_.rearrange("p (q k n) -> p q k n", q=2, k=2)
        silu = si_.rearrange("p (q n) -> p q n", q=2)
        hh = hh_.rearrange("p (q n) -> p q n", q=2)
        hTe = hTe_.rearrange("p (q s n) -> p q s n", q=2, s=3)
        y1 = y1_.rearrange("p (q n) -> p q n", q=2)
        gat1 = big[:, W1:W1 + NT * K1 * D].rearrange("p (t k n) -> p t k n", t=NT, k=K1)
        zero = sb("zero", [P, 4 * D])
        gat0 = [g1_.rearrange("p (k n) -> p k n", k=K0), zero[:, :].rearrange("p (k n) -> p k n", k=K0)]

        ps = [ctx.enter_context(nc.psum_tensor(f"ps{i}", [P, 512], F32)) for i in range(8)]

        xs = [nc.dram_tensor(f"rows_in{l}", (n * P, D), F32, kind="Internal").ap() for l, n in ((0, T0), (1, T1))]
        ys = [nc.dram_tensor(f"rows_out{l}", (n * P, D), F32, kind="Internal").ap() for l, n in ((0, T0), (1, T1))]

        s_x = sem("x_loaded")
        s_w0 = sem("layer0_attention_weights_loaded")
        s_rt = sem("router_weights_loaded")
        s_zero = sem("zero_tile_set")
        s_fill = sem("slots_zeroed")
        s_wkq = sem("layer1_wk_wq_loaded")
        s_wv = sem("layer1_wv_loaded")
        s_wo = sem("layer1_wo_loaded")
        s_const = sem("constants_set")
        s_pool = sem("pool_chain")
        s_dve = sem("dve_chain")
        s_act = sem("act_chain")
        s_blk0z = sem("layer0_blocks_zeroed")
        s_bn = sem("row_statistics")
        s_bqb = sem("query_bias_spread")
        s_crep = sem("context_columns_repeated")
        s_p0 = sem("prep0_products")
        s_p0e = sem("prep0_evacuated")
        s_var = sem("variances_ready")
        s_rstd = sem("rstd_ready")
        s_xn = sem("pair_normalised")
        s_xt = sem("pair_transposed")
        s_xte = sem("pair_transposed_copied")
        s_sc = sem("pair_scores")
        s_scb = sem("pair_scores_shifted")
        s_exp = sem("pair_exponentials")
        s_at = sem("pair_weights")
        s_att = sem("pair_weights_transposed")
        s_atte = sem("pair_weights_transposed_copied")
        s_ao = sem("pair_attended")
        s_aoe = sem("pair_residual_added")
        s_gn = sem("router_rows_normalised")
        s_un = sem("router_rows_unscaled")
        s_xl = sem("normalised_rows_added")
        s_nc = sem("normalised_rows_kept")
        s_gt = sem("router_rows_transposed")
        s_gte = sem("router_rows_transposed_copied")
        s_gl = sem("router_logits")
        s_gle = sem("router_logits_copied")
        s_pmax = sem("router_logits_shifted")
        s_pexp = sem("router_exponentials")
        s_wd = sem("router_weight_differences")
        s_we = sem("router_weight_exponentials")
        s_mask = sem("assignment_masks")
        s_rank = sem("assignment_ranks")
        s_te = sem("tile_expert_column")
        s_ter = sem("tile_expert_row")
        s_slot = sem("slots_ready")
        s_info = sem("tile_info_ready")
        s_disp = [sem("rows_dispatched0"), sem("rows_dispatched1")]
        s_l1p = sem("layer1_table_products")
        s_l1e = sem("layer1_table_products_copied")
        s_bz = sem("layer1_blocks_zeroed")
        s_ew = [sem("expert_weights_a"), sem("expert_weights_b")]
        s_ex = [sem("expert_rows_a"), sem("expert_rows_b")]
        s_eX = sem("expert_rows_transposed")
        s_eXe = sem("expert_rows_transposed_copied")
        s_eH = sem("expert_hidden_products")
        s_ehb = sem("expert_hidden_biased")
        s_eglu = sem("expert_glu_ready")
        s_elin = sem("expert_linear_ready")
        s_egate = sem("expert_gated")
        s_esig = sem("expert_sigmoid_ready")
        s_ehs = sem("expert_hidden_ready")
        s_eHT = sem("expert_hidden_transposed")
        s_eHTe = sem("expert_hidden_transposed_copied")
        s_eO = sem("expert_out_products")
        s_ey = sem("expert_rows_out_ready")
        s_est = [sem("expert_rows_stored_a"), sem("expert_rows_stored_b")]
        s_gath = [sem("rows_gathered0_a"), sem("rows_gathered0_b")]
        s_comb4 = sem("rows_combined0")
        s_mk = [sem("mask_loaded_a"), sem("mask_loaded_b")]
        s_1n = sem("l1_tile_normalised")
        s_1t = sem("l1_tile_transposed")
        s_1te = sem("l1_tile_transposed_copied")
        s_1s = sem("l1_scores")
        s_1m = sem("l1_scores_masked")
        s_1b = sem("l1_scores_shifted")
        s_1x = sem("l1_exponentials")
        s_1w = sem("l1_weights")
        s_1wt = sem("l1_weights_transposed")
        s_1wte = sem("l1_weights_transposed_copied")
        s_1o = sem("l1_attended")
        s_1r = sem("l1_residual_added")
        s_w1 = sem("layer1_experts_loaded_a")
        s_w1b = sem("layer1_experts_loaded_b")
        s_fx = [sem("routed_rows_a"), sem("routed_rows_b")]
        s_fX = sem("ffn_rows_transposed")
        s_fXe = sem("ffn_rows_transposed_copied")
        s_fG = sem("ffn_gate_up_products")
        s_fsi = sem("ffn_silu_ready")
        s_fh = sem("ffn_hidden_ready")
        s_fHT = sem("ffn_hidden_transposed")
        s_fHTe = sem("ffn_hidden_transposed_copied")
        s_fO = sem("ffn_out_products")
        s_fy = sem("ffn_out_taken")
        s_fst = [sem("routed_rows_stored_a"), sem("routed_rows_stored_b")]
        s_g1 = [sem("rows_gathered1_a"), sem("rows_gathered1_b")]
        s_half = sem("first_routed_row_added")
        s_past = sem("waits_passed")
        s_fin = sem("tile_finished")
        s_out = sem("output_stored")

        block = ctx.enter_context(nc.Block())
        n_fill = sum(-(-n * P // 4 // P) for n in (T0, T1))
        x_rows, out_rows = (v.rearrange("b (h p j) d -> (b h) j p d", h=2, j=J) for v in (a["x"], out))
        mask_rows = a["mask"].rearrange("b (h p j) d -> (b h) j p d", h=2, j=J)

        def dram_tile(v, i):
            if isinstance(i.t, int):
                return v[i.t // 4, i.t % 4]
            return v[span(i.m // 2), span(2 * (i.m % 2) + i.q)].rearrange("a c p d -> (a c p) d")

        def ring_slot(eng, t):
            return eng.value_load(info[0][0:1, 1, span(t)], min_val=0, max_val=R0 - 1)

        @block.sync
        def _(sp):
            sp.dma_start(ctxT[:, :, :], a["ctxT"]).then_inc(s_w0, 16)
            sp.dma_start(w0k, a["Wk0T"]).then_inc(s_w0, 16)
            sp.dma_start(w0q, a["Wq0"]).then_inc(s_w0, 16)
            sp.dma_start(w0v, a["Wv0T"]).then_inc(s_w0, 16)
            sp.dma_start(b0c[:, :, :], a["bkq"]).then_inc(s_w0, 16)
            sp.dma_start(bvb, a["bv"].to_broadcast([P, D])).then_inc(s_w0, 16)
            for g in range(NT // J):
                sp.dma_start(xres[:, J * g:J * g + J, :],
                             x_rows[g].rearrange("j p d -> p j d")).then_inc(s_x, 16)
            sp.dma_start(gateT[:, :, :], a["gateT"]).then_inc(s_rt, 16)
            sp.dma_start(gate_b[:, :], a["gate_b"].to_broadcast([P, E0 + E1])).then_inc(s_rt, 16)
            sp.dma_start(scale_b, a["norm_scale"].to_broadcast([P, D])).then_inc(s_rt, 16)
            sp.dma_start(att_in_v, a["wk1"]).then_inc(s_wkq, 16)
            sp.dma_start(att_w_v, a["wq1T"]).then_inc(s_wkq, 16)
            sp.wait_ge(s_zero, 1)
            for l, n in ((0, T0), (1, T1)):
                rows4 = xs[l].rearrange("(p r) d -> p (r d)", r=4)
                for c in range(0, n * P // 4, P):
                    m = min(P, n * P // 4 - c)
                    sp.dma_start(rows4[c:c + m, :], zero[0:m, :]).then_inc(s_fill, 16)
            sp.wait_ge(s_l1p, 2)
            sp.dma_start(att_in_v, a["wv1"]).then_inc(s_wv, 16)
            sp.wait_ge(s_l1p, 10)
            sp.dma_start(att_w_v, a["wo1"]).then_inc(s_wo, 16)

            sp.wait_ge(s_info, 1)

            def weights(i):
                e = sp.value_load(info[0][0:1, 0, span(i.t)], min_val=0, max_val=E0 - 1)
                r = ring_slot(sp, i.t)
                new = sp.value_load(info[0][0:1, 2, span(i.t)], min_val=0, max_val=1)
                wait(sp, s_ey, i.t - R0 + 1)
                alone(sp, s_past)
                wait(sp, s_ew[i.p], 16 * i.half)
                sp.dma_start(ring[:, span(r), :].rearrange("p a w -> p (a w)"),
                             a["w_e0"][span(e)].rearrange("a p w -> (a p) w"),
                             cond=(new != 0)).then_inc(s_ew[i.p], 16)

            def rows0(i):
                wait(sp, s_eX, i.t - 2)
                sp.dma_start(xr0[:, i.pair], xs[0][span(i.t * P, 2 * P), :].rearrange("(k p) d -> p k d", k=2)
                             ).then_inc(s_ex[i.pair], 16)

            for t in range(AHEAD):
                weights(Tile(t // 4, t % 4, 4))
            sp.wait_ge(s_l1p, 20)
            sp.wait_ge(s_disp[0], 16 * K0 * NT)

            def step0(i):
                if i.p == 0:
                    rows0(i)
                if i.plus(AHEAD).exists(0, T0):
                    weights(i.plus(AHEAD))

            over_tiles(sp, 0, T0, step0, lead=8, tail=AHEAD, u=4)

            def mask_tile(i):
                wait(sp, s_1m, i.t - 1)
                sp.dma_start(msk[:, i.q, :], dram_tile(mask_rows, i)).then_inc(s_mk[i.q], 16)

            sp.wait_ge(s_ey, T0)
            mask_tile(Tile(0, 0))
            mask_tile(Tile(0, 1))
            for e in range(EARLY):
                sp.dma_start(w1s[:, e, :], a["w_e1"][e]).then_inc(s_w1, 16)
            over_tiles(sp, 2, NT, mask_tile)
            sp.wait_ge(s_1r, NT)
            for e in range(EARLY, 8):
                sp.dma_start(w1s[:, e, :], a["w_e1"][e]).then_inc(s_w1b, 16)

            sp.wait_ge(s_info, 2)
            sp.wait_ge(s_nc, 2 * NPAIR)

            def rows1(source):
                def body(i):
                    wait(sp, s_fX, i.t - 1)
                    sp.dma_start(xr1[:, i.q, :], source(i)).then_inc(s_fx[i.q], 16)
                return body

            def token_rows(first):
                return rows1(lambda i: normed[:, span(i.plus(first).t), :].rearrange("p a d -> p (a d)"))

            over_tiles(sp, 0, SHARED_A, token_rows(0))
            sp.wait_ge(s_disp[1], 16 * K1 * NT)
            over_tiles(sp, SHARED_A, MID1, rows1(lambda i: xs[1][span(i.plus(-SHARED_A).t * P, P), :]))
            over_tiles(sp, MID1, N1, token_rows(-T1))

            def output(i):
                sp.wait_ge(s_fin, i.t + 1)
                sp.dma_start(dram_tile(out_rows, i),
                             xres[:, span(i.t), :].rearrange("p a d -> p (a d)")).then_inc(s_out, 16)

            over_tiles(sp, 0, NT, output)
            sp.wait_ge(s_out, 16 * NT)

        @block.gpsimd
        def _(pool):
            chain = Chain(pool, s_pool)
            pool.memset(zero[:, :], 0.0).then_inc(s_zero, 1)
            chain(pool.memset(ident[:, :], 0.0))
            chain(pool.memset(tri_b[:, :], 1.0))
            chain(pool.memset(blkmask, 1.0))
            pool.memset(kblk0_, 0.0).then_inc(s_blk0z, 1)
            pool.memset(tabV0_, 0.0).then_inc(s_blk0z, 1)
            chain.wait()
            pool.affine_select(out=ident[:, :], in_=ident[:, :], compare_op=ALU.not_equal, fill=1.0, base=0,
                               pattern=[[-1, P]], channel_multiplier=1).then_inc(s_const, 1)
            pool.affine_select(out=tri_b[:, :], in_=tri_b[:, :], compare_op=ALU.is_ge, fill=0.0, base=-1,
                               pattern=[[1, P]], channel_multiplier=-1).then_inc(s_const, 1)
            halves = [blkmask[64 * h:64 * h + 64, :].rearrange("p (c d) -> p c d", c=C0) for h in range(2)]
            pool.wait_ge(s_const, 2)
            for m in halves:
                chain(pool.affine_select(out=m, in_=m, compare_op=ALU.is_ge, fill=0.0, base=0,
                                         pattern=[[-KEYS0, C0], [0, DH]], channel_multiplier=1))
                chain.wait()
            for n, m in enumerate(halves):
                pool.affine_select(out=m, in_=m, compare_op=ALU.is_ge, fill=0.0, base=KEYS0 - 1,
                                   pattern=[[KEYS0, C0], [0, DH]], channel_multiplier=-1).then_inc(s_const, 1)
                pool.wait_ge(s_const, 3 + n)
            pool.memset(ones_b[:, :], 1.0).then_inc(s_const, 1)
            pool.memset(mhalf[:, :], -0.5).then_inc(s_const, 1)
            pool.memset(eps_t[:, :], EPS).then_inc(s_const, 1)
            pool.memset(blk1, 0.0).then_inc(s_bz, 1)
            pool.wait_ge(s_const, 7)

            def factor(base, i, width, twice, cbase):
                q, w = i.q, slice(0, width)
                chain.step(cbase, 5 if twice else 1, i.t)
                pool.wait_ge(s_var, base + i.t + 1)
                v, r = mv[:, q, w, 1], rs[:, q, w]
                chain(pool.tensor_tensor(rtmp[:, 0, w], v, eps_t[:, w], ALU.add))
                chain.wait()
                if not twice:
                    pool.tensor_tensor(r, rtmp[:, 0, w], mhalf[:, w], ALU.pow).then_inc(s_rstd, 1)
                else:
                    chain(pool.tensor_tensor(r, rtmp[:, 0, w], mhalf[:, w], ALU.pow))
                    chain.wait()
                    chain(pool.tensor_tensor(rtmp[:, 0, w], v, r, ALU.mult))
                    chain.wait()
                    chain(pool.tensor_tensor(rtmp[:, 0, w], rtmp[:, 0, w], r, ALU.mult))
                    chain.wait()
                    chain(pool.tensor_tensor(rtmp[:, 0, w], rtmp[:, 0, w], eps_t[:, w], ALU.add))
                    chain.wait()
                    pool.tensor_tensor(rms[:, q, w], rtmp[:, 0, w], mhalf[:, w], ALU.pow).then_inc(s_rstd, 1)
                chain.stepped()
                pool.wait_ge(s_rstd, base + i.t + 1)

            def iotas():
                pool.iota(pidx, pattern=[[0, 1]], base=0, channel_multiplier=1,
                          allow_small_or_imprecise_dtypes=True).then_inc(s_const, 1)
                pool.iota(iota_e, pattern=[[1, E0]], base=0, channel_multiplier=0,
                          allow_small_or_imprecise_dtypes=True).then_inc(s_const, 1)

            def dispatch(l, k_n):
                pool.wait_ge(s_slot, l + 1)
                pool.wait_ge(s_nc, (l + 1) * NPAIR)

                def scatter(i):
                    for k in range(k_n):
                        pool.indirect_dma_start(
                            out=xs[l], out_offset=bass.IndirectOffsetOnAxis(
                                ap=slot_i[l][:, k, i:i + 1].bitcast(U32), axis=0),
                            in_=normed[:, i, :], in_offset=None).then_inc(s_disp[l], 16)

                for i in range(NT):
                    scatter(i)

            c0 = chain.n
            over_tiles(pool, 0, NPAIR, lambda i: factor(0, i, 2, False, c0))
            c1 = c0 + NPAIR
            over_tiles(pool, 0, NPAIR, lambda i: factor(NPAIR, i, 2, True, c1))
            c2 = c1 + 5 * NPAIR
            iotas()
            pool.wait_ge(s_fill, 16 * n_fill)
            dispatch(0, K0)

            def store0(i):
                if i.p == 0:
                    pool.wait_ge(s_ey, i.t + 2)
                    pool.dma_start(ys[0][span(i.t * P, 2 * P), :].rearrange("(k p) d -> p k d", k=2),
                                   y0[:, i.pair]).then_inc(s_est[i.pair], 16)

            over_tiles(pool, 0, T0, store0, u=4)
            for q in range(2):
                pool.wait_ge(s_est[q], 16 * T0 // 4)

            def gather0(i):
                if i >= 2:
                    pool.wait_ge(s_comb4, K0 * (i - 1))
                for k in range(K0):
                    pool.indirect_dma_start(
                        out=gat0[i % 2][:, k, :], out_offset=None, in_=ys[0],
                        in_offset=bass.IndirectOffsetOnAxis(ap=slot_i[0][:, k, i:i + 1].bitcast(U32), axis=0)
                    ).then_inc(s_gath[i % 2], 16)

            gather0(0)
            for i in range(NT):
                if i + 1 < NT:
                    gather0(i + 1)
                factor(2 * NPAIR, Tile(i // 2, i % 2), 1, False, c2)
            c3 = c2 + NT
            over_tiles(pool, 0, NPAIR, lambda i: factor(2 * NPAIR + NT, i, 2, False, c3))
            iotas()
            dispatch(1, K1)

            def store1(i):
                pool.wait_ge(s_fy, SHARED_A + i.t + 1)
                pool.dma_start(ys[1][span(i.t * P, P), :], y1[:, i.q, :]).then_inc(s_fst[i.q], 16)

            over_tiles(pool, 0, T1, store1)
            for q in range(2):
                pool.wait_ge(s_fst[q], 16 * T1 // 2)
            for i in range(NT):
                if i >= 2:
                    pool.wait_ge(s_g1[i % 2], 16 * K1 * (i // 2))
                for k in range(K1):
                    pool.indirect_dma_start(
                        out=gat1[:, i, k, :], out_offset=None, in_=ys[1],
                        in_offset=bass.IndirectOffsetOnAxis(ap=slot_i[1][:, k, i:i + 1].bitcast(U32), axis=0)
                    ).then_inc(s_g1[i % 2], 16)

        @block.scalar
        def _(act):
            def copy(out_, in_, sem_, scale=1.0):
                act.activation(out_, in_, ACT.Copy, scale=scale).then_inc(sem_, 1)

            def exps0(i):
                act.wait_ge(s_scb, i.t + 1)
                act.activation(sc0[:, i.q, :], sc0[:, i.q, :], ACT.Exp).then_inc(s_exp, 1)

            def rows_t0(i):
                act.wait_ge(s_xt, i.t + 1)
                wait(act, s_sc, i.t - 1)
                copy(xT_a[:, i.q, :], ps[i.q][:, :], s_xte)

            def weights_t0(i):
                act.wait_ge(s_att, i.t + 1)
                wait(act, s_ao, i.t - 1)
                copy(aT0[:, i.q, :], ps[4][:, 0:P], s_atte)

            rows_t0(Tile(0, 0))

            def attend0(i):
                exps0(i)
                if i.plus(1).exists(0, NPAIR):
                    rows_t0(i.plus(1))
                weights_t0(i)

            over_tiles(act, 0, NPAIR, attend0)

            def router_rows(l):
                def body(i):
                    act.wait_ge(s_gt, l * NPAIR + i.t + 1)
                    wait(act, s_gl, l * NPAIR + i.t - 1)
                    copy(gx[:, i.q, :], ps[i.q][:, :], s_gte)
                    copy(normed[:, span(2 * i.t, 2), :], xn_r[:, i.q, :].rearrange("p (a d) -> p a d", a=2), s_nc)

                over_tiles(act, 0, NPAIR, body)

            router_rows(0)

            act.wait_ge(s_wd, 1)
            act.activation(wexp[:, :, :], wexp[:, :, :], ACT.Exp).then_inc(s_we, 1)

            def blocks(base):
                for g in range(2):
                    act.wait_ge(s_l1p, base + g + 1)
                    for h in range(2):
                        r = slice(64 * h, 64 * h + 64)
                        dst = blk1_v[r, 4 * g:4 * g + 4, :, h, :]
                        src = ps[g][r, :].rearrange("p (h b s) -> p h b s", h=4, b=B)
                        ins = act.activation(dst, src, ACT.Copy, scale=DH ** -0.5 if base == 0 else 1.0)
                    ins.then_inc(s_l1e, 1)

            act.wait_ge(s_bz, 1)
            blocks(0)
            for n in range(8):
                act.wait_ge(s_l1p, 3 + n)
                k, g = n // 4, n % 4
                copy(tabA[:, :, k, 256 * g:256 * g + 256].rearrange("p b (h n) -> p h b n", h=2),
                     ps[2 + n % 2][:, :].rearrange("p (h b n) -> p h b n", h=2, b=B), s_l1e)
            blocks(10)
            for n in range(8):
                act.wait_ge(s_l1p, 13 + n)
                b, g = n // 4, n % 4
                copy(tabV[:, b, 2 * g:2 * g + 2, :], ps[2 + n % 2][:, :].rearrange("p (h n) -> p h n", h=2), s_l1e)

            act.wait_ge(s_info, 1)

            def rows_e0(i):
                act.wait_ge(s_eX, i.t + 1)
                wait(act, s_eH, i.t - 1)
                copy(xT0[:, i.p, :, :], ps[i.p][:, 0:D].rearrange("p (k n) -> p k n", k=FK), s_eXe)

            def hidden_t0(i):
                act.wait_ge(s_eHT, i.t + 1)
                wait(act, s_eO, i.t - 1)
                copy(hT0[:, i.p, :, :], ps[4][:, 0:D].rearrange("p (k n) -> p k n", k=2), s_eHTe)

            def sigmoid0(i):
                act.wait_ge(s_eglu, i.t + 1)
                wait(act, s_ehs, i.t)
                act.activation(sig_, glu_, ACT.Sigmoid, scale=ALPHA).then_inc(s_esig, 1)

            rows_e0(Tile(0, 0, 4))

            def expert0(i):
                if i.plus(-2).exists(0, T0):
                    hidden_t0(i.plus(-2))
                if i.plus(-1).exists(0, T0):
                    sigmoid0(i.plus(-1))
                if i.plus(1).exists(0, T0):
                    rows_e0(i.plus(1))

            over_tiles(act, 0, T0 + 2, expert0, lead=4, tail=4, u=4)

            def exps1(i):
                act.wait_ge(s_1b, i.t + 1)
                act.activation(sc1[:, i.q, :], sc1[:, i.q, :], ACT.Exp).then_inc(s_1x, 1)

            def rows_t1(i):
                act.wait_ge(s_1t, i.t + 1)
                wait(act, s_1s, i.t - 1)
                copy(xT1[:, i.q, :, :], ps[0][:, 0:D].rearrange("p (k n) -> p k n", k=FK), s_1te)

            def weights_t1(i):
                act.wait_ge(s_1wt, i.t + 1)
                wait(act, s_1o, i.t)
                for g in range(2):
                    ins = act.activation(aT1[:, 4 * g:4 * g + 4, :],
                                         ps[5 + g][:, :].rearrange("p (h n) -> p h n", h=4), ACT.Copy)
                ins.then_inc(s_1wte, 1)

            rows_t1(Tile(0, 0))

            def attend1(i):
                exps1(i)
                if i.plus(1).exists(0, NT):
                    rows_t1(i.plus(1))
                weights_t1(i)

            over_tiles(act, 0, NT, attend1)
            router_rows(1)
            act.wait_ge(s_pmax, 1)
            act.activation(logits[:, :, 0:E1], logits[:, :, 0:E1], ACT.Exp).then_inc(s_pexp, 1)

            act.wait_ge(s_info, 2)

            def rows_e1(i):
                act.wait_ge(s_fX, i.t + 1)
                wait(act, s_fG, 2 * (i.t - 1))
                copy(xTe[:, i.q, :, :], ps[0][:, 0:D].rearrange("p (k n) -> p k n", k=FK), s_fXe)

            def hidden_t1(i, c):
                u = 2 * i.t + c
                act.wait_ge(s_fHT, u + 1)
                wait(act, s_fO, u - 1)
                copy(hTe[:, c, :, :], ps[5][:, 0:3 * P].rearrange("p (s n) -> p s n", s=3), s_fHTe)

            def silu1(i, c):
                u = 2 * i.t + c
                act.wait_ge(s_fG, u + 1)
                wait(act, s_fh, u - 1)
                act.activation(silu[:, c, :], ps[1 + 2 * c][:, 0:FC1], ACT.Silu).then_inc(s_fsi, 1)

            rows_e1(Tile(0, 0))

            def expert1(i):
                if i.plus(-1).exists(0, N1):
                    hidden_t1(i.plus(-1), 1)
                if i.exists(0, N1):
                    silu1(i, 0)
                    hidden_t1(i, 0)
                if i.plus(1).exists(0, N1):
                    rows_e1(i.plus(1))
                if i.exists(0, N1):
                    silu1(i, 1)

            over_tiles(act, 0, N1, expert1)
            expert1(Tile(N1 // 2, 0))

        @block.vector
        def _(dve):
            chain = Chain(dve, s_dve)
            TT, TS, STT, CP = dve.tensor_tensor, dve.tensor_scalar, dve.scalar_tensor_tensor, dve.tensor_copy

            def over(ap, n):
                return ap.unsqueeze(len(ap.shape)).broadcast_to([*ap.shape, n])

            def spread(ap, n):
                return ap.unsqueeze(1).broadcast_to([ap.shape[0], n, ap.shape[1]])

            dve.wait_ge(s_w0, 16 * 6)
            for m in range(2):
                ins = CP(bqb[:, m, :], b0c[:, 1, m:m + 1].broadcast_to([P, P]))
            ins.then_inc(s_bqb, 1)
            for k in range(FK):
                for b in range(B):
                    for c in range(C0):
                        ins = CP(crep[:, k, b, :, c, :],
                                 ctxT[:, k, b * S2:b * S2 + S2].rearrange("p (s j) -> p j s", j=J))
            ins.then_inc(s_crep, 1)
            dve.wait_ge(s_p0, 1)
            dve.wait_ge(s_blk0z, 2)
            for m in range(2):
                for h in range(2):
                    r = slice(64 * h, 64 * h + 64)
                    ins = TS(kblk0[r, m, h, :], ps[0][r, m * P:m * P + P], b0c[r, 0, m:m + 1], None, ALU.add)
            ins.then_inc(s_p0e, 1)
            dve.wait_ge(s_p0, 2)
            for k in range(3):
                src = ps[1 + k][:, :].rearrange("p (c b s j) -> p b j c s", c=C0, b=B, j=J)
                for b in range(B):
                    ins = TS(tabA0[:, k, b], src[:, b], DH ** -0.5, None, ALU.mult)
            ins.then_inc(s_p0e, 1)
            dve.wait_ge(s_p0, 3)
            vals = ab[:, 0:1024].rearrange("p (n d) -> p n d", n=4)
            for n in range(4):
                chain(TT(vals[:, n, :], ps[4 + n // 2][:, 256 * (n % 2):256 * (n % 2) + 256], bvb, ALU.add))
            chain.wait()
            dve.wait_ge(s_const, 7)
            for n in range(4):
                for j in range(2):
                    r = slice(64 * j, 64 * j + 64)
                    ins = TT(tabV0[r, n // 2, n % 2, j, :], vals[r, n, :], blkmask[r, :], ALU.mult)
            ins.then_inc(s_p0e, 1)

            def statistics(base, var_base, t, q, rows):
                wait(dve, s_var, var_base + t)
                alone(dve, s_past)
                for k, x in enumerate(rows):
                    dve.bn_stats(stats[:, k, :], x).then_inc(s_bn, 1)
                dve.wait_ge(s_bn, base + len(rows) * (t + 1))
                alone(dve, s_past)
                for k in range(len(rows)):
                    ins = dve.bn_aggr(mv[:, q, k, :], stats[:, k, :])
                ins.then_inc(s_var, 1)

            def row(i, k=0):
                return xres[:, span(2 * i.t + k), :].rearrange("p a d -> p (a d)")

            def pair(v, i):
                return v[:, span(2 * i.t, 2), :]

            def pair_stats(i, base=0, var_base=0):
                statistics(base, var_base, i.t, i.q, [row(i, 0), row(i, 1)])

            dve.wait_ge(s_x, 16 * (NT // J))

            def normalise0(i):
                dve.wait_ge(s_rstd, i.t + 1)
                wait(dve, s_xt, i.t - 1)
                for k in range(2):
                    ins = TS(xn_a[:, i.q, k * D:k * D + D], row(i, k), mv[:, i.q, k, 0:1],
                             rs[:, i.q, k:k + 1], ALU.subtract, ALU.mult)
                ins.then_inc(s_xn, 1)

            def shift0(i):
                s = sc0[:, i.q, :]
                sg = s.rearrange("p (g n) -> p g n", n=KEYS0)
                dve.wait_ge(s_sc, i.t + 1)
                bias = tabA0[:, 2].rearrange("p b j c s -> p b (j c s)")[:, span(i.m // 2), P * i.q:P * i.q + P]
                chain(TT(s, ps[2 + i.q][:, 0:P], bias.rearrange("p a n -> p (a n)"), ALU.add))
                chain.wait()
                chain(dve.tensor_reduce(sm0[:, 0, 0:8], sg, AX.X, ALU.max))
                chain.wait()
                TT(sg, sg, over(sm0[:, 0, 0:8], KEYS0), ALU.subtract).then_inc(s_scb, 1)

            def weights0(i):
                sg = sc0[:, i.q, :].rearrange("p (g n) -> p g n", n=KEYS0)
                dve.wait_ge(s_exp, i.t + 1)
                chain(dve.tensor_reduce(sm0[:, 1, 0:8], sg, AX.X, ALU.add))
                chain.wait()
                chain(dve.reciprocal(sm0[:, 2, 0:8], sm0[:, 1, 0:8]))
                chain.wait()
                TT(sg, sg, over(sm0[:, 2, 0:8], KEYS0), ALU.mult).then_inc(s_at, 1)

            def residual0(i):
                dve.wait_ge(s_ao, i.t + 1)
                TT(pair(xres, i), pair(xres, i), ps[5 + i.q][:, :].rearrange("p (a d) -> p a d", a=2),
                   ALU.add).then_inc(s_aoe, 1)

            pair_stats(Tile(0, 0))
            dve.wait_ge(s_p0e, 2)
            normalise0(Tile(0, 0))
            c0 = chain.n

            def attend0(i):
                chain.step(c0, 4, i.t)
                if i.plus(1).exists(0, NPAIR):
                    pair_stats(i.plus(1))
                shift0(i)
                if i.plus(1).exists(0, NPAIR):
                    normalise0(i.plus(1))
                weights0(i)
                chain.stepped()
                if i.plus(-1).exists(0, NPAIR):
                    residual0(i.plus(-1))

            over_tiles(dve, 0, NPAIR, attend0)
            residual0(Tile(NPAIR // 2 - 1, 1))

            def router_rows(l, bn_base, var_base, columns, bias):
                def normalise(i):
                    dve.wait_ge(s_rstd, var_base + i.t + 1)
                    wait(dve, s_gt, l * NPAIR + i.t - 1)
                    wait(dve, s_nc, l * NPAIR + i.t - 1)
                    u = xn_r if l else xn_a
                    for k in range(2):
                        ins = TS(u[:, i.q, k * D:k * D + D], row(i, k), mv[:, i.q, k, 0:1],
                                 rs[:, i.q, k:k + 1], ALU.subtract, ALU.mult)
                    if l == 0:
                        ins.then_inc(s_un, 1)
                        dve.wait_ge(s_un, i.t + 1)
                        for k in range(2):
                            ins = STT(out=xn_r[:, i.q, k * D:k * D + D], in0=xn_a[:, i.q, k * D:k * D + D],
                                      scalar=rms[:, i.q, k:k + 1], in1=scale_b, op0=ALU.mult, op1=ALU.mult)
                        TT(pair(xres, i), pair(xres, i), xn_a[:, i.q, :].rearrange("p (a d) -> p a d", a=2),
                           ALU.add).then_inc(s_xl, 1)
                    ins.then_inc(s_gn, 1)

                def take(i):
                    dve.wait_ge(s_gl, l * NPAIR + i.t + 1)
                    TT(logits[:, span(2 * i.t, 2), 0:columns],
                       ps[2 + i.q][:, 0:2 * columns].rearrange("p (a e) -> p a e", a=2),
                       spread(bias, 2), ALU.add).then_inc(s_gle, 1)

                def body(i):
                    if i.plus(1).exists(0, NPAIR):
                        pair_stats(i.plus(1), bn_base, var_base)
                    normalise(i)
                    if i.plus(-1).exists(0, NPAIR):
                        take(i.plus(-1))

                pair_stats(Tile(0, 0), bn_base, var_base)
                over_tiles(dve, 0, NPAIR, body)
                take(Tile(NPAIR // 2 - 1, 1))
                dve.wait_ge(s_gle, (l + 1) * NPAIR)

            def ranks_to_slots(l, columns, real, chosen, tiles):
                one = r_one.bitcast(BF16)[:, 0:chosen * NT * columns].rearrange(
                    "p (k t e) -> p k t e", k=chosen, t=NT)
                mask = r_mask.bitcast(BF16)[:, 0:NT * columns].rearrange("p (t e) -> p t e", t=NT)
                slot = r_slot[:, 0:NT * columns].rearrange("p (t e) -> p t e", t=NT)
                tmp = r_tmp[:, 0:NT * columns].rearrange("p (t e) -> p t e", t=NT)
                E = slice(0, columns)
                dve.wait_ge(s_const, 9 + 2 * l)
                chain.wait()
                chain(CP(topf, topi[:, :, :]))
                chain.wait()
                for k in range(chosen):
                    chain(TT(one[:, k], spread(iota_e[:, E], NT), over(topf[:, :, k], columns), ALU.is_equal))
                chain.wait()
                for k in range(1, chosen):
                    ins = TT(mask, one[:, 0] if k == 1 else mask, one[:, k], ALU.add)
                    if k < chosen - 1:
                        chain(ins)
                        chain.wait()
                ins.then_inc(s_mask, 1)
                dve.wait_ge(s_rank, l + 1)
                chain(TS(cnt_i[:, E], ps[5][:, E], float(P - 1), None, ALU.add))
                chain.wait()
                chain(TS(cnt_i[:, E], cnt_i[:, E], 7, None, ALU.logical_shift_right))
                chain(dve.memset(ones_f[:, E], 1.0))
                chain.wait()
                chain(CP(tiles_f[:, E], cnt_i[:, E]))
                chain.wait()
                chain(dve.tensor_tensor_scan(ends_f[:, E], ones_f[:, E], tiles_f[:, E], 0.0, ALU.mult, ALU.add))
                chain.wait()
                chain(TT(base_f[:, E], ends_f[:, E], tiles_f[:, E], ALU.subtract))
                chain.wait()
                chain(TS(base_f[:, E], base_f[:, E], float(P), None, ALU.mult))
                chain.wait()
                chain(TT(slot, ps[4][:, 0:NT * columns].rearrange("p (t e) -> p t e", t=NT),
                         spread(base_f[:, E], NT), ALU.add))
                chain.wait()
                for k in range(chosen):
                    chain.wait()
                    chain(TT(tmp, one[:, k], slot, ALU.mult))
                    chain.wait()
                    chain(dve.tensor_reduce(slots_f[:, k, :], tmp, AX.X, ALU.add))
                chain.wait()
                CP(slot_i[l][:, :, :], slots_f[:, 0:chosen, :]).then_inc(s_slot, 1)
                chain(TS(cmp_f[0:tiles, E], ends_f[0:tiles, E], pidx[0:tiles, :], None, ALU.is_le))
                chain.wait()
                chain(dve.tensor_reduce(te_col[0:tiles, 0:1], cmp_f[0:tiles, E], AX.X, ALU.add))
                chain.wait()
                TS(te_col[0:tiles, 0:1], te_col[0:tiles, 0:1], float(real - 1), None, ALU.min).then_inc(s_te, 1)
                te, fl, rk, on = (v[:, 0:tiles] for v in (te_row, fl_row, rk_row, one_row))
                chain(dve.memset(fl[:, 0:1], 1.0))
                chain(dve.memset(on, 1.0))
                dve.wait_ge(s_ter, l + 1)
                chain(CP(te, ps[6][0:1, 0:tiles]))
                chain.wait()
                chain(TT(fl[:, 1:tiles], te[:, 1:tiles], te[:, 0:tiles - 1], ALU.not_equal))
                chain.wait()
                chain(dve.tensor_tensor_scan(rk, on, fl, -1.0, ALU.mult, ALU.add))
                if l == 1:
                    chain(dve.memset(info[1][:, :, :], 0))
                    chain.wait()
                    TS(info[1][:, 0, SHARED_A:MID1], te, 1.0, None, ALU.add).then_inc(s_info, 1)
                else:
                    chain(CP(info[0][:, 0, :], te))
                    chain(CP(info[0][:, 2, :], fl))
                    chain.wait()
                    chain(CP(info[0][:, 1, :], rk))
                    chain.wait()
                    TS(info[0][:, 1, :], info[0][:, 1, :], R0 - 1, None, ALU.bitwise_and).then_inc(s_info, 1)

            dve.wait_ge(s_rt, 16 * 3)
            router_rows(0, 2 * NPAIR, NPAIR, E0, gate_b[:, 0:E0])
            chain.n = c0 + 4 * NPAIR

            def choose(columns):
                for i in range(NT):
                    chain(dve.max(top[:, i, :], logits[:, i, 0:columns]))
                chain.wait()
                for i in range(NT):
                    chain(dve.max_index(topi[:, i, :], top[:, i, :], logits[:, i, 0:columns]))

            choose(E0)
            TT(wexp[:, :, :], top[:, :, 0:K0], over(top[:, :, 0], K0), ALU.subtract).then_inc(s_wd, 1)
            ranks_to_slots(0, E0, E0, K0, T0)
            dve.wait_ge(s_we, 1)
            chain(dve.tensor_reduce(wsum[:, 0, :], wexp[:, :, :], AX.X, ALU.add))
            chain.wait()
            chain(dve.reciprocal(wsum[:, 1, :], wsum[:, 0, :]))
            chain.wait()
            chain(TT(wgt[0][:, :, :], wexp[:, :, :], over(wsum[:, 1, :], K0), ALU.mult))

            def biases(i, lo, n):
                return ring[:, span(ring_slot(dve, i.t)), W0 + lo:W0 + lo + n].rearrange("p a n -> p (a n)")

            def bias_hidden0(i):
                dve.wait_ge(s_eH, i.t + 1)
                TT(hb_, ps[2 + i.p][:, :], biases(i, 0, 2 * F0), ALU.add).then_inc(s_ehb, 1)
                dve.wait_ge(s_ehb, i.t + 1)
                TS(glu_, hb_[:, 0:F0], LIMIT, None, ALU.min).then_inc(s_eglu, 1)
                TS(lin_, hb_[:, F0:2 * F0], LIMIT, -LIMIT, ALU.min, ALU.max).then_inc(s_elin, 1)

            def gate_hidden0(i):
                dve.wait_ge(s_elin, i.t + 1)
                STT(out=lin_, in0=lin_, scalar=1.0, in1=glu_, op0=ALU.add, op1=ALU.mult).then_inc(s_egate, 1)
                dve.wait_ge(s_egate, i.t + 1)
                dve.wait_ge(s_esig, i.t + 1)
                wait(dve, s_eHT, i.t - 1)
                TT(hs0[:, i.p, :], lin_, sig_, ALU.mult).then_inc(s_ehs, 1)

            def rows_out0(i):
                bias = biases(i, 2 * F0, D)
                dve.wait_ge(s_eO, i.t + 1)
                wait(dve, s_est[i.pair], 16 * i.m)
                TT(y0[:, i.pair, i.p, :], ps[5 + i.p][:, 0:D], bias, ALU.add).then_inc(s_ey, 1)

            def expert0(i):
                if i.plus(-1).exists(0, T0):
                    gate_hidden0(i.plus(-1))
                if i.exists(0, T0):
                    bias_hidden0(i)
                if i.plus(-2).exists(0, T0):
                    rows_out0(i.plus(-2))

            over_tiles(dve, 0, T0 + 2, expert0, lead=4, tail=4, u=4)

            c1 = chain.n
            BN1 = 4 * NPAIR

            def row1(i):
                return xres[:, span(i.t), :].rearrange("p a d -> p (a d)")

            def combine0(i):
                dve.wait_ge(s_gath[i.q], 16 * K0 * (i.m + 1))
                for k in range(K0):
                    w = wgt[0][:, span(i.t), k:k + 1].rearrange("p a k -> p (a k)")
                    ins = STT(out=row1(i), in0=gat0[i.q][:, k, :], scalar=w, in1=row1(i),
                              op0=ALU.mult, op1=ALU.add)
                    ins.then_inc(s_comb4, 1)
                    dve.wait_ge(s_comb4, K0 * i.t + k + 1)
                statistics(BN1, 2 * NPAIR, i.t, i.q, [row1(i)])

            def normalise1(i):
                dve.wait_ge(s_rstd, 2 * NPAIR + i.t + 1)
                wait(dve, s_1t, i.t - 1)
                TS(xn1[:, i.q, :], row1(i), mv[:, i.q, 0, 0:1], rs[:, i.q, 0:1],
                   ALU.subtract, ALU.mult).then_inc(s_1n, 1)

            def shift1(i):
                s = sc1[:, i.q, :].rearrange("p (h n) -> p h n", h=H1)
                dve.wait_ge(s_1s, i.t + 1)
                dve.wait_ge(s_mk[i.q], 16 * (i.m + 1))
                for g in range(2):
                    ins = TT(s[:, 8 * g:8 * g + 8, :], ps[1 + 2 * i.q + g][:, :].rearrange("p (h n) -> p h n", h=8),
                             spread(msk[:, i.q, :], 8), ALU.add)
                ins.then_inc(s_1m, 1)
                dve.wait_ge(s_1m, i.t + 1)
                chain(dve.tensor_reduce(sm1[:, i.q, 0, :], s, AX.X, ALU.max))
                chain.wait()
                TT(s, s, over(sm1[:, i.q, 0, :], S2), ALU.subtract).then_inc(s_1b, 1)

            def weights1(i):
                s = sc1[:, i.q, :].rearrange("p (h n) -> p h n", h=H1)
                dve.wait_ge(s_1x, i.t + 1)
                chain(dve.tensor_reduce(sm1[:, i.q, 1, :], s, AX.X, ALU.add))
                chain.wait()
                chain(dve.reciprocal(sm1[:, i.q, 2, :], sm1[:, i.q, 1, :]))
                chain.wait()
                TT(s, s, over(sm1[:, i.q, 2, :], S2), ALU.mult).then_inc(s_1w, 1)

            def residual1(i):
                dve.wait_ge(s_1o, i.t + 1)
                TT(row1(i), row1(i), ps[7][:, 0:D], ALU.add).then_inc(s_1r, 1)

            def attend1(i):
                chain.step(c1, 3, i.t)
                if i.plus(1).exists(0, NT):
                    combine0(i.plus(1))
                shift1(i)
                if i.plus(1).exists(0, NT):
                    normalise1(i.plus(1))
                weights1(i)
                chain.stepped()
                if i.plus(-1).exists(0, NT):
                    residual1(i.plus(-1))

            combine0(Tile(0, 0))
            normalise1(Tile(0, 0))
            over_tiles(dve, 0, NT, attend1)
            residual1(Tile(NT // 2 - 1, 1))
            dve.wait_ge(s_1r, NT)

            router_rows(1, BN1 + NT, 2 * NPAIR + NT, E1, gate_b[:, E0:E0 + E1])
            chain.n = c1 + 3 * NT
            lg = logits[:, :, 0:E1]
            chain(dve.tensor_reduce(wsum[:, 0, :], lg, AX.X, ALU.max))
            chain.wait()
            TT(lg, lg, over(wsum[:, 0, :], E1), ALU.subtract).then_inc(s_pmax, 1)
            chain(dve.memset(logits[:, :, E1:EC1], -1.0))
            dve.wait_ge(s_pexp, 1)
            chain(dve.tensor_reduce(wsum[:, 0, :], lg, AX.X, ALU.add))
            chain.wait()
            chain(dve.reciprocal(wsum[:, 1, :], wsum[:, 0, :]))
            chain.wait()
            chain(TT(lg, lg, over(wsum[:, 1, :], E1), ALU.mult))
            chain.wait()
            choose(EC1)
            chain(dve.tensor_reduce(wsum[:, 0, :], top[:, :, 0:K1], AX.X, ALU.add))
            chain.wait()
            chain(dve.reciprocal(wsum[:, 1, :], wsum[:, 0, :]))
            chain.wait()
            chain(TT(wgt[1][:, :, :], top[:, :, 0:K1], over(wsum[:, 1, :], K1), ALU.mult))
            ranks_to_slots(1, EC1, E1, K1, T1)

            def hidden1(i, c):
                u = 2 * i.t + c
                dve.wait_ge(s_fsi, u + 1)
                wait(dve, s_fHT, u - 1)
                TT(hh[:, c, :], silu[:, c, :], ps[2 + 2 * c][:, 0:FC1], ALU.mult).then_inc(s_fh, 1)

            def take1(i, kind):
                dve.wait_ge(s_fO, 2 * i.t + 2)
                o = ps[6 + i.q][:, 0:D]
                if kind == "routed":
                    j = i.plus(-SHARED_A)
                    wait(dve, s_fst[i.q], 16 * j.m)
                    CP(y1[:, i.q, :], o).then_inc(s_fy, 1)
                else:
                    j = i if kind == "first" else i.plus(-T1)
                    TT(row1(j), row1(j), o, ALU.add).then_inc(s_fy, 1)

            def finish(i):
                dve.wait_ge(s_g1[i.q], 16 * K1 * (i.m + 1))
                for k in range(K1):
                    w = wgt[1][:, span(i.t), k:k + 1].rearrange("p a k -> p (a k)")
                    g = gat1[:, span(i.t), k, :].rearrange("p a d -> p (a d)")
                    STT(out=row1(i), in0=g, scalar=w, in1=row1(i), op0=ALU.mult, op1=ALU.add)                        .then_inc(s_half if k == 0 else s_fin, 1)
                    if k == 0:
                        dve.wait_ge(s_half, i.t + 1)

            def expert1(i, before):
                hidden1(i, 0)
                if i.plus(-1).exists(0, N1):
                    take1(i.plus(-1), before)
                hidden1(i, 1)

            def segment(lo, hi, kind, before):
                def body(i):
                    first = isinstance(i.t, int) and i.t == lo
                    expert1(i, before if first else kind)
                    if kind == "last" and not first:
                        finish(i.plus(-MID1 - 1))
                over_tiles(dve, lo, hi, body)

            segment(0, SHARED_A, "first", None)
            segment(SHARED_A, MID1, "routed", "first")
            dve.wait_ge(s_fy, SHARED_A)
            segment(MID1, N1, "last", "routed")
            take1(Tile(N1 // 2 - 1, 1), "last")
            dve.wait_ge(s_fy, N1)
            finish(Tile((SHARED_B - 1) // 2, (SHARED_B - 1) % 2))
            over_tiles(dve, SHARED_B, NT, finish)

        @block.tensor
        def _(pe):
            MM = pe.matmul

            def transposes(dst, rows, n):
                for k in range(n):
                    ins = pe.transpose(dst[:, k * P:k * P + P], rows[:, k * P:k * P + P], ident[:, :])
                return ins

            pe.wait_ge(s_w0, 16 * 6)
            for m in range(2):
                for k in range(FK):
                    ins = MM(ps[0][:, m * P:m * P + P], w0k[:, k, m * P:m * P + P], ctxT[:, k, :],
                             start=(k == 0), stop=(k == FK - 1))
            ins.then_inc(s_p0, 1)
            pe.wait_ge(s_p0e, 1)
            pe.wait_ge(s_bqb, 1)
            for k in range(3):
                for m in range(2):
                    w = w0q[:, m, k * P:k * P + P] if k < FK else bqb[:, m, :]
                    ins = MM(ps[1 + k][:, m * 256:m * 256 + 256], w,
                             kblk0[:, m, :, :].rearrange("p c n -> p (c n)"), start=True, stop=True)
            ins.then_inc(s_p0, 1)
            pe.wait_ge(s_crep, 1)
            for n in range(4):
                for k in range(FK):
                    c = crep[:, k, n // 2].rearrange("p j c s -> p (j c s)")
                    ins = MM(ps[4 + n // 2][:, 256 * (n % 2):256 * (n % 2) + 256],
                             c[:, P * (n % 2):P * (n % 2) + P], w0v[:, k, :],
                             start=(k == 0), stop=(k == FK - 1))
            ins.then_inc(s_p0, 1)

            def rows_t0(i):
                pe.wait_ge(s_xn, i.t + 1)
                wait(pe, s_xte, i.t - 1)
                transposes(ps[i.q], xn_a[:, i.q, :], 4).then_inc(s_xt, 1)

            def scores0(i):
                pe.wait_ge(s_xte, i.t + 1)
                wait(pe, s_scb, i.t - 1)
                for j in range(2):
                    for k in range(FK):
                        tab = tabA0[:, k].rearrange("p b j c s -> p b (j c s)")[
                            :, span(i.m // 2), P * i.q + 64 * j:P * i.q + 64 * j + 64]
                        ins = MM(ps[2 + i.q][:, 64 * j:64 * j + 64],
                                 xT_a[:, i.q, (2 * j + k) * P:(2 * j + k) * P + P],
                                 tab.rearrange("p a n -> p (a n)"), start=(k == 0), stop=(k == FK - 1))
                ins.then_inc(s_sc, 1)

            def weights_t0(i):
                pe.wait_ge(s_at, i.t + 1)
                wait(pe, s_atte, i.t)
                transposes(ps[4], sc0[:, i.q, :], 1).then_inc(s_att, 1)

            def values0(i):
                pe.wait_ge(s_atte, i.t + 1)
                wait(pe, s_aoe, i.t - 1)
                tab = tabV0.rearrange("p b q j d -> p b q (j d)")[:, span(i.m // 2), i.q, :]
                MM(ps[5 + i.q][:, :], aT0[:, i.q, :], tab.rearrange("p a n -> p (a n)"),
                   start=True, stop=True).then_inc(s_ao, 1)

            pe.wait_ge(s_const, 7)
            pe.wait_ge(s_p0e, 3)
            rows_t0(Tile(0, 0))
            scores0(Tile(0, 0))

            def attend0(i):
                if i.plus(1).exists(0, NPAIR):
                    rows_t0(i.plus(1))
                    scores0(i.plus(1))
                weights_t0(i)
                values0(i)

            over_tiles(pe, 0, NPAIR, attend0)

            def router_rows(l, w, columns):
                def rows(i):
                    pe.wait_ge(s_gn, l * NPAIR + i.t + 1)
                    wait(pe, s_gte, l * NPAIR + i.t - 1)
                    transposes(ps[i.q], xn_r[:, i.q, :], 4).then_inc(s_gt, 1)

                def logits_of(i):
                    pe.wait_ge(s_gte, l * NPAIR + i.t + 1)
                    wait(pe, s_gle, l * NPAIR + i.t - 1)
                    for j in range(2):
                        for k in range(FK):
                            n = 2 * j + k
                            ins = MM(ps[2 + i.q][:, columns * j:columns * j + columns],
                                     gx[:, i.q, n * P:n * P + P], w[:, k, :], start=(k == 0), stop=(k == FK - 1))
                    ins.then_inc(s_gl, 1)

                def body(i):
                    if i.plus(1).exists(0, NPAIR):
                        rows(i.plus(1))
                    logits_of(i)

                rows(Tile(0, 0))
                over_tiles(pe, 0, NPAIR, body)

            def ranks(l, columns, tiles):
                mask = r_mask.bitcast(BF16)
                pe.wait_ge(s_mask, l + 1)
                MM(ps[4][:, 0:NT * columns], tri_b[:, :], mask[:, 0:NT * columns],
                   start=True, stop=False, skip_group_check=True)
                for n in range(1, NT):
                    MM(ps[4][:, n * columns:NT * columns], ones_b[:, :], mask[:, 0:(NT - n) * columns],
                       start=False, stop=(n == NT - 1), skip_group_check=True)
                for n in range(NT):
                    ins = MM(ps[5][:, 0:columns], ones_b[:, :], mask[:, n * columns:(n + 1) * columns],
                             start=(n == 0), stop=(n == NT - 1))
                ins.then_inc(s_rank, 1)

            def expert_row(l, tiles):
                pe.wait_ge(s_te, l + 1)
                MM(ps[6][0:1, 0:tiles], te_col[0:tiles, 0:1], ident[0:tiles, 0:tiles],
                   start=True, stop=True).then_inc(s_ter, 1)

            pe.wait_ge(s_rt, 16 * 3)
            router_rows(0, gateT[:, :, 0:E0], E0)
            ranks(0, E0, T0)

            pe.wait_ge(s_gte, NPAIR)
            pe.wait_ge(s_gle, NPAIR)
            pe.wait_ge(s_wkq, 16 * 2)

            def blocks(base):
                for hp in range(HP1):
                    g = hp // 4
                    if hp % 4 == 0 and base:
                        pe.wait_ge(s_l1e, 10)
                    for k in range(FK):
                        ins = MM(ps[g][:, (hp % 4) * P:(hp % 4) * P + P], att_in_v[:, k, hp * P:hp * P + P],
                                 ctxT[:, k, :], start=(k == 0), stop=(k == FK - 1))
                    if hp % 4 == 3:
                        ins.then_inc(s_l1p, 1)

            blocks(0)
            for n in range(8):
                k, g = n // 4, n % 4
                pe.wait_ge(s_l1e, max(2, n + 1))
                for h in range(2):
                    hp = 2 * g + h
                    ins = MM(ps[2 + n % 2][:, 256 * h:256 * h + 256], att_w_v[:, hp, k * P:k * P + P],
                             blk1_v[:, hp].rearrange("p b c s -> p (b c s)"), start=True, stop=True)
                ins.then_inc(s_l1p, 1)
            expert_row(0, T0)
            pe.wait_ge(s_wv, 16)
            blocks(10)
            pe.wait_ge(s_wo, 16)
            for n in range(8):
                b, g = n // 4, n % 4
                pe.wait_ge(s_l1e, max(12, n + 11))
                for h in range(2):
                    hp = 2 * g + h
                    ins = MM(ps[2 + n % 2][:, 256 * h:256 * h + 256],
                             blk1_v[:, hp, b].rearrange("p c s -> p (c s)"), att_w_v[:, hp, :],
                             start=True, stop=True)
                ins.then_inc(s_l1p, 1)
            pe.wait_ge(s_l1e, 20)

            pe.wait_ge(s_info, 1)

            def rows_e0(i):
                if i.p == 0:
                    pe.wait_ge(s_ex[i.pair], 16 * (i.m + 1))
                wait(pe, s_eXe, i.t - 1)
                transposes(ps[i.p], xr0[:, i.pair, i.p, :], FK).then_inc(s_eX, 1)

            def hidden0(i):
                r = ring_slot(pe, i.t)
                pe.wait_ge(s_eXe, i.t + 1)
                pe.wait_ge(s_ew[i.p], 16 * (i.half + 1))
                wait(pe, s_ehb, i.t - 1)
                for k in range(FK):
                    w = ring[:, span(r), k * 2 * F0:(k + 1) * 2 * F0].rearrange("p a n -> p (a n)")
                    ins = MM(ps[2 + i.p][:, :], xT0[:, i.p, k, :], w, start=(k == 0), stop=(k == FK - 1))
                ins.then_inc(s_eH, 1)

            def hidden_t0(i):
                pe.wait_ge(s_ehs, i.t + 1)
                wait(pe, s_eHTe, i.t)
                transposes(ps[4], hs0[:, i.p, :], F0 // P).then_inc(s_eHT, 1)

            def out0(i):
                r = ring_slot(pe, i.t)
                pe.wait_ge(s_eHTe, i.t + 1)
                wait(pe, s_ey, i.t - 1)
                for k in range(F0 // P):
                    lo = FK * 2 * F0 + k * D
                    w = ring[:, span(r), lo:lo + D].rearrange("p a n -> p (a n)")
                    ins = MM(ps[5 + i.p][:, 0:D], hT0[:, i.p, k, :], w, start=(k == 0), stop=(k == F0 // P - 1))
                ins.then_inc(s_eO, 1)

            def expert0(i):
                if i.plus(-2).exists(0, T0):
                    hidden_t0(i.plus(-2))
                if i.plus(1).exists(0, T0):
                    rows_e0(i.plus(1))
                if i.exists(0, T0):
                    hidden0(i)
                if i.plus(-2).exists(0, T0):
                    out0(i.plus(-2))

            rows_e0(Tile(0, 0, 4))
            over_tiles(pe, 0, T0 + 2, expert0, lead=4, tail=4, u=4)

            def rows_t1(i):
                pe.wait_ge(s_1n, i.t + 1)
                wait(pe, s_1te, i.t)
                transposes(ps[0], xn1[:, i.q, :], FK).then_inc(s_1t, 1)

            def scores1(i):
                pe.wait_ge(s_1te, i.t + 1)
                wait(pe, s_1m, i.t - 1)
                b = i.m // 4
                for g in range(2):
                    for k in range(FK):
                        tab = tabA[:, span(b), k, 512 * g:512 * g + 512].rearrange("p a n -> p (a n)")
                        ins = MM(ps[1 + 2 * i.q + g][:, :], xT1[:, i.q, k, :], tab,
                                 start=(k == 0), stop=(k == FK - 1))
                ins.then_inc(s_1s, 1)

            def weights_t1(i):
                pe.wait_ge(s_1w, i.t + 1)
                wait(pe, s_1wte, i.t)
                transposes(ps[5], sc1[:, i.q, 0:512], 4)
                transposes(ps[6], sc1[:, i.q, 512:1024], 4).then_inc(s_1wt, 1)

            def values1(i):
                pe.wait_ge(s_1wte, i.t + 1)
                wait(pe, s_1r, i.t)
                b = i.m // 4
                for hp in range(HP1):
                    tab = tabV[:, span(b), hp, :].rearrange("p a n -> p (a n)")
                    ins = MM(ps[7][:, 0:D], aT1[:, hp, :], tab, start=(hp == 0), stop=(hp == HP1 - 1))
                ins.then_inc(s_1o, 1)

            def attend1(i):
                if i.plus(1).exists(0, NT):
                    rows_t1(i.plus(1))
                    scores1(i.plus(1))
                weights_t1(i)
                values1(i)

            rows_t1(Tile(0, 0))
            scores1(Tile(0, 0))
            over_tiles(pe, 0, NT, attend1)

            router_rows(1, gateT[:, :, E0:E0 + E1], E1)
            ranks(1, EC1, T1)
            expert_row(1, T1)

            pe.wait_ge(s_info, 2)
            pe.wait_ge(s_w1, 16 * EARLY)
            pe.wait_ge(s_w1b, 16 * (8 - EARLY))

            def rows_e1(i):
                pe.wait_ge(s_fx[i.q], 16 * (i.m + 1))
                wait(pe, s_fXe, i.t)
                transposes(ps[0], xr1[:, i.q, :], FK).then_inc(s_fX, 1)

            def place(i):
                return pe.value_load(info[1][0:1, 0, span(i.t)], min_val=0, max_val=E1)

            def gate_up(i, c):
                e = place(i)
                u = 2 * i.t + c
                if c == 0:
                    pe.wait_ge(s_fXe, i.t + 1)
                wait(pe, s_fh, u - 1)
                for g in range(2):
                    for k in range(FK):
                        lo = ((k * NC1 + c) * 2 + g) * FC1
                        w = w1s[:, span(e), lo:lo + FC1].rearrange("p a n -> p (a n)")
                        ins = MM(ps[1 + 2 * c + g][:, 0:FC1], xTe[:, i.q, k, :], w,
                                 start=(k == 0), stop=(k == FK - 1))
                ins.then_inc(s_fG, 1)

            def hidden_t1(i, c):
                u = 2 * i.t + c
                pe.wait_ge(s_fh, u + 1)
                wait(pe, s_fHTe, u)
                for n, (lo, width) in enumerate(SUB1):
                    ins = pe.transpose(ps[5][0:width, n * P:n * P + P], hh[:, c, lo:lo + width], ident[:, :])
                ins.then_inc(s_fHT, 1)

            def out1(i, c):
                e = place(i)
                u = 2 * i.t + c
                pe.wait_ge(s_fHTe, u + 1)
                if c == 0:
                    wait(pe, s_fy, i.t - 1)
                for n, (_, width) in enumerate(SUB1):
                    lo = GU1 + (c * 3 + n) * D
                    w = w1s[0:width, span(e), lo:lo + D].rearrange("p a n -> p (a n)")
                    ins = MM(ps[6 + i.q][:, 0:D], hTe[0:width, c, n, :], w,
                             start=(c == 0 and n == 0), stop=(c == 1 and n == 2))
                ins.then_inc(s_fO, 1)

            def expert1(i):
                if i.plus(-1).exists(0, N1):
                    hidden_t1(i.plus(-1), 1)
                if i.exists(0, N1):
                    gate_up(i, 0)
                if i.plus(-1).exists(0, N1):
                    out1(i.plus(-1), 1)
                if i.exists(0, N1):
                    hidden_t1(i, 0)
                    if i.plus(1).exists(0, N1):
                        rows_e1(i.plus(1))
                    gate_up(i, 1)
                    out1(i, 0)

            rows_e1(Tile(0, 0))
            over_tiles(pe, 0, N1, expert1)
            expert1(Tile(N1 // 2, 0))


_NAMES = ["x", "mask", "ctxT", "Wk0T", "Wq0", "Wv0T", "bkq", "bv", "gateT", "gate_b", "norm_scale",
          "wk1", "wq1T", "wv1", "wo1", "w_e0", "w_e1"]


def arrange(i):
    f = {k: np.asarray(v) for k, v in i.items()}

    def by_part(w):
        return w.reshape(-1, P, w.shape[-1]).transpose(1, 0, 2)

    r = {"x": f["x"], "mask": f["mask_Bx1xSxS2_ff0"][:, 0]}
    r["ctxT"] = by_part(f["ctx_1024"].reshape(B * S2, D).T)
    r["Wk0T"], r["Wv0T"] = by_part(f["L0_xattn_Wk"].T), by_part(f["L0_xattn_Wv"].T)
    r["Wq0"] = by_part(f["L0_xattn_Wq"])
    r["bkq"] = np.stack([f["L0_xattn_bk"].reshape(2, P), f["L0_xattn_bq"].reshape(2, P)]).transpose(2, 0, 1)
    r["bv"] = f["L0_xattn_bv"][None]
    r["gateT"] = by_part(np.concatenate([f["L0_ffn_gate_w"], f["L1_ffn_wr"]]).T)
    r["gate_b"] = np.concatenate([f["L0_ffn_gate_b"], f["L1_ffn_rb"]])[None]
    r["norm_scale"] = f["L0_ffn_norm_scale"][None]
    r["wk1"], r["wv1"] = (by_part(f[k].reshape(D, H1 * DH)) for k in ("L1_xattn_wk", "L1_xattn_wv"))
    r["wq1T"] = by_part(f["L1_xattn_wq"].reshape(D, H1 * DH).T)
    r["wo1"] = by_part(f["L1_xattn_wo"].reshape(H1 * DH, D))
    w1 = f["L0_ffn_w1"].reshape(E0, F0, 2, FK, P).transpose(0, 4, 3, 2, 1).reshape(E0, P, FK * 2 * F0)
    w2 = f["L0_ffn_w2"].reshape(E0, D, F0 // P, P).transpose(0, 3, 2, 1).reshape(E0, P, (F0 // P) * D)
    b1 = f["L0_ffn_b1"].reshape(E0, F0, 2).transpose(0, 2, 1).reshape(E0, 2 * F0)
    b = np.concatenate([b1, f["L0_ffn_b2"]], axis=1)
    r["w_e0"] = np.concatenate([w1, w2, np.broadcast_to(b[:, None], (E0, P, B0))], axis=2)
    g, u, d = (np.concatenate([f["L1_ffn_s" + k][None], f["L1_ffn_r" + k]]) for k in "gud")
    gu = np.stack([g, u]).reshape(2, 8, NC1, FC1, FK, P).transpose(1, 5, 4, 2, 0, 3).reshape(8, P, GU1)
    d = d.reshape(8, D, NC1, FC1).transpose(0, 2, 3, 1)
    dd = np.zeros((8, NC1, 3 * P, D), np.float32)
    dd[:, :, :FC1] = d
    dd = dd.reshape(8, NC1, 3, P, D).transpose(0, 3, 1, 2, 4).reshape(8, P, NC1 * 3 * D)
    r["w_e1"] = np.concatenate([gu, dd], axis=2)
    return {k: np.ascontiguousarray(r[k]) for k in _NAMES}


def kernel(**inputs):
    import concourse.bacc as _bacc
    from concourse.bass_utils import run_bass_kernel_spmd as _run

    nc = _bacc.Bacc("TRN2", target_bir_lowering=False, num_devices=1)
    arrays = arrange(inputs)
    aps = {k: nc.dram_tensor("in_" + k, v.shape, F32, kind="ExternalInput").ap() for k, v in arrays.items()}
    out = nc.dram_tensor("out", (B, S, D), F32, kind="ExternalOutput").ap()
    build(nc, aps, out)
    r = _run(nc, [{"in_" + k: v for k, v in arrays.items()}], core_ids=[0])
    return r.results[0]["out"]
```

```python
from contextlib import ExitStack

import numpy as np

import concourse.bass as bass
from concourse import mybir

F32 = mybir.dt.float32
BF16 = mybir.dt.bfloat16
F16 = mybir.dt.float16
I32 = mybir.dt.int32
U32 = mybir.dt.uint32
ALU = mybir.AluOpType
ACT = mybir.ActivationFunctionType
AX = mybir.AxisListType

P = 128
B, S, D, S2 = 2, 1024, 256, 64
FK = D // P
NT = B * S // P
NPAIR = NT // 2
J = 4
C0, KEYS0 = 4, S2 // J
DH = 64
H1, HP1 = 16, 8
EPS = 1e-5
E0, K0, F0 = 32, 4, 256
E1, K1, F1 = 7, 2, 704
EC1 = 8
LIMIT, ALPHA = 7.0, 1.702
NC1 = 2
FC1 = F1 // NC1
SUB1 = [(0, 128), (128, 128), (256, FC1 - 256)]
T0 = (NT * P * K0 + 127 * E0) // P
T0 += T0 % 2
T1 = (NT * P * K1 + 127 * E1) // P
T1 += T1 % 2
R0 = 8
W0 = FK * 2 * F0 + (F0 // P) * D
GU1 = FK * NC1 * 2 * FC1
W1 = GU1 + NC1 * 3 * D
B0 = 2 * F0 + D
EARLY = 6
SHARED_SLOTS = 2
LAG0, LAG1 = 8, 4
LAGR = 5
AHEAD = 2
SHARED_A, SHARED_B = 8, 8
N1 = SHARED_A + T1 + SHARED_B
MID1 = SHARED_A + T1


def wait(eng, sem, n):
    if not (isinstance(n, int) and n <= 0):
        eng.wait_ge(sem, n)


class Tile:

    def __init__(self, m, q, u=2, place=None):
        self.m, self.q, self.u, self.t = m, q, u, u * m + q
        self.place = q if place is None else place
        self.p = q % 2
        self.half = m * (u // 2) + q // 2
        self.pair = q // 2 % 2

    def plus(self, d):
        return Tile(self.m + (self.q + d) // self.u, (self.q + d) % self.u, self.u, self.place + d)

    def exists(self, lo, hi):
        return not isinstance(self.t, int) or lo <= self.t < hi


def over_tiles(eng, lo, hi, body, lead=2, tail=2, u=2):
    a, z = -(-(lo + lead) // u) * u, (hi - tail) // u * u
    for t in range(lo, min(a, hi)):
        body(Tile(t // u, t % u, u))
    if z > a:
        with eng.Fori(a // u, z // u) as m:
            for q in range(u):
                body(Tile(m, q, u))
    for t in range(max(a, z), hi):
        body(Tile(t // u, t % u, u))


def at_most(t, n):
    return min(t, n) if isinstance(t, int) else t


def alone(eng, sem):
    eng.sem_inc(sem, 1)


def span(i, n=1):
    return slice(i, i + n) if isinstance(i, int) else bass.ds(i, n)


class Registers:

    def __init__(self, load_value):
        self.load_value, self.held = load_value, {}

    def begin(self, i):
        if i.q == 0 or isinstance(i.t, int):
            self.held = {}
            self.m = i.m

    def key(self, i):
        return i.t if isinstance(i.t, int) else i.place

    def load(self, i):
        if self.key(i) not in self.held:
            self.held[self.key(i)] = self.load_value(i.t)

    def __getitem__(self, i):
        return self.held[self.key(i)]


class Chain:

    def __init__(self, eng, sem):
        self.eng, self.sem, self.n, self.base = eng, sem, 0, 0

    def __call__(self, ins):
        ins.then_inc(self.sem, 1)
        self.n = self.n + 1

    def wait(self):
        self.eng.wait_ge(self.sem, self.n)

    def step(self, base, per, t):
        self.n = base + per * t
        self.base, self.per, self.now = base, per, t

    def stepped(self):
        d = self.n - (self.base + self.per * self.now)
        assert not isinstance(d, int) or d == self.per, d


def build(nc, a, out):
    ctx = ExitStack()
    with ctx:
        def sb(name, shape, dt=F32):
            return ctx.enter_context(nc.sbuf_tensor(name, shape, dt))

        def sem(name):
            return ctx.enter_context(nc.semaphore(name))

        xres = sb("xres", [P, NT, D])
        normed = sb("normed", [P, NT, D])
        big = sb("big", [P, 8 * W1])
        w1s = big[:, :].rearrange("p (e w) -> p e w", e=8)
        ring = big[:, 0:R0 * (W0 + B0)].rearrange("p (r w) -> p r w", r=R0)
        o = (R0 - SHARED_SLOTS) * (W0 + B0)
        att_in = big[:, o:o + FK * H1 * DH]
        att_in_v = att_in.rearrange("p (k n) -> p k n", k=FK)
        o += FK * H1 * DH
        att_w = big[:, o:o + HP1 * D]
        att_w_v = att_w.rearrange("p (h n) -> p h n", h=HP1)
        o += HP1 * D
        blk1 = big[:, o:o + HP1 * B * 2 * S2]
        blk1_v = blk1.rearrange("p (h b c s) -> p h b c s", h=HP1, b=B, c=2)
        o += HP1 * B * 2 * S2
        tabA0 = big[:, o:o + 3 * 512].rearrange("p (k b j c s) -> p k b j c s", k=3, b=B, j=J, c=C0)
        o += 3 * 512
        tabV0_ = big[:, o:o + B * 2 * 512]
        tabV0 = tabV0_.rearrange("p (b q j d) -> p b q j d", b=B, q=2, j=2)
        o += B * 2 * 512
        ab = big[:, o:o + 3072]
        o = 8 * W1 - B * FK * H1 * S2 - B * HP1 * D
        assert (R0 - SHARED_SLOTS) * (W0 + B0) + 3 * 2048 + 1536 + 2048 + 3072 <= o
        assert SHARED_SLOTS * (W0 + B0) <= 3 * 2048
        tabA = big[:, o:o + B * FK * H1 * S2].rearrange("p (b k n) -> p b k n", b=B, k=FK)
        o += B * FK * H1 * S2
        tabV = big[:, o:o + B * HP1 * D].rearrange("p (b h n) -> p b h n", b=B, h=HP1)
        o += B * HP1 * D
        assert o == 8 * W1

        ident = sb("ident", [P, P])
        ones_b = sb("ones_b", [P, P], BF16)
        tri_b = sb("tri_b", [P, P], BF16)
        mhalf = sb("mhalf", [P, 2])
        eps_t = sb("eps_t", [P, 2])
        stats = sb("stats", [P, 2, 6])
        mv = sb("mv", [P, 2, 2, 2])
        rs = sb("rs", [P, 2, 2])
        rms = sb("rms", [P, 2, 2])
        rtmp = sb("rtmp", [P, 1, 2])
        WORK = 5376
        work = sb("work", [P, WORK])

        def carve(parts):
            at, got = 0, []
            for n in parts:
                got.append(work[:, at:at + n])
                at += n
            assert at <= WORK, at
            return got

        (w0q_, w0k_, w0v_, kblk0_, crep_, bqb_, bvb) = carve([512, 512, 512, 512, 1024, 256, 256])
        w0q = w0q_.rearrange("p (k n) -> p k n", k=2)
        w0k = w0k_.rearrange("p (k n) -> p k n", k=2)
        w0v = w0v_.rearrange("p (k n) -> p k n", k=2)
        kblk0 = kblk0_.rearrange("p (m c n) -> p m c n", m=2, c=2)
        crep = crep_.rearrange("p (k b j c s) -> p k b j c s", k=FK, b=B, j=J, c=C0)
        bqb = bqb_.rearrange("p (m n) -> p m n", m=2)
        ctxT = sb("ctxT", [P, FK, B * S2])
        b0c = sb("b0c", [P, 2, 2])

        xn_a = ab[:, 0:1024].rearrange("p (q n) -> p q n", q=2)
        xT_a = ab[:, 1024:2048].rearrange("p (q n) -> p q n", q=2)
        sc0 = ab[:, 2048:2304].rearrange("p (q n) -> p q n", q=2)
        aT0 = ab[:, 2304:2560].rearrange("p (q n) -> p q n", q=2)
        blkmask = ab[:, 2560:2816]
        gx = sb("gx", [P, 2, 512])
        scale_b = ab[:, 2816:3072]
        gateT = sb("gateT", [P, FK, E0 + E1])
        gate_b = sb("gate_b", [P, E0 + E1])
        sm0 = sb("sm0", [P, 4, 16])

        logits = sb("logits", [P, NT, E0])
        top = sb("top", [P, NT, 8])
        topi = sb("topi", [P, NT, 8], U32)
        wexp = sb("wexp", [P, NT, K0])
        wsum = sb("wsum", [P, 2, NT])
        wgt = [sb(f"wgt{l}", [P, NT, k]) for l, k in ((0, K0), (1, K1))]
        slot_i = [sb(f"slot_i{l}", [P, k, NT], I32) for l, k in ((0, K0), (1, K1))]
        info = [sb(f"info{l}", [1, 3, n], I32) for l, n in ((0, T0), (1, N1))]
        (r_topf, r_one, r_mask, r_cum, r_slot, r_tmp, r_small) = carve([128, 1024, 256, 288, 512, 512, 1024])
        xn_r = work[:, 4320:5344].rearrange("p (q n) -> p q n", q=2)
        topf = r_topf.rearrange("p (t k) -> p t k", k=8)
        slots_f = r_small[:, 700:764].rearrange("p (k t) -> p k t", t=NT)
        cnt_f = r_small[:, 16:48]
        cnt_i = r_small[:, 48:80].bitcast(I32)
        tiles_f = r_small[:, 80:112]
        ends_f = r_small[:, 112:144]
        base_f = r_small[:, 144:176]
        ones_f = r_small[:, 176:208]
        cmp_f = r_small[:, 208:240]
        te_col = r_small[:, 240:242]
        te_row = r_small[0:1, 242:338]
        fl_row = r_small[0:1, 338:434]
        rk_row = r_small[0:1, 434:530]
        one_row = r_small[0:1, 530:626]
        pidx = r_small[:, 626:627]
        iota_e = r_small[:, 628:660]
        slot_hi, slot_lo = (r_small[:, 770 + 64 * n:834 + 64 * n] for n in range(2))
        slot_sh = r_small[:, 898:962].bitcast(I32)
        iota_p = sb("iota_p", [P, P])
        token_id = sb("token_id", [P, NT])
        token_col = sb("token_col", [P, 4], I32)
        slot_token = [sb(f"slot_token{l}", [P, n], I32) for l, n in ((0, T0), (1, T1))]
        o = 2 * (W0 + B0)
        hot_hi = [big[:, o:o + K0 * NT * T0 // 2].bitcast(F16).rearrange("p (c n) -> p c n", n=T0)]
        o += K0 * NT * T0 // 2
        hot_lo = [[v.bitcast(F16).rearrange("p (c n) -> p c n", n=P)
                   for v in [big[:, o + k * NT * P // 2:o + (k + 1) * NT * P // 2] for k in range(K0)]]]
        assert o + K0 * NT * P // 2 <= (R0 - SHARED_SLOTS) * (W0 + B0)

        (xr0_, xT0_, hb_, hs_, hT_, y0_) = carve([1024, 512, 512, 512, 512, 1024])
        xr0 = xr0_.rearrange("p (q n) -> p q n", q=4)
        xT0 = xT0_.rearrange("p (q k n) -> p q k n", q=2, k=2)
        hs0 = hs_.rearrange("p (q n) -> p q n", q=2)
        hT0 = hT_.rearrange("p (q k n) -> p q k n", q=2, k=2)
        y0 = y0_.rearrange("p (q k n) -> p q k n", q=2, k=2)

        (xn1_, xT1_, s1_, aT1_, g1_, mk_) = carve([512, 512, 2048, 1024, 1024, 128])
        xn1 = xn1_.rearrange("p (q n) -> p q n", q=2)
        xT1 = xT1_.rearrange("p (q k n) -> p q k n", q=2, k=2)
        sc1 = s1_.rearrange("p (q n) -> p q n", q=2)
        aT1 = aT1_.rearrange("p (h n) -> p h n", h=HP1)
        msk = mk_.rearrange("p (q n) -> p q n", q=2)
        sm1 = sb("sm1", [P, 2, 3, H1])
        xn_f = gx[:, :, D:2 * D]

        (xr1_, xTe_, si_, hh_, hTe_, y1_) = carve([512, 512, 704, 704, 768, 512])
        xr1 = xr1_.rearrange("p (q n) -> p q n", q=2)
        xTe = xTe_.rearrange("p (q k n) -> p q k n", q=2, k=2)
        silu = si_.rearrange("p (q n) -> p q n", q=2)
        hh = hh_.rearrange("p (q n) -> p q n", q=2)
        hTe = hTe_.rearrange("p (q s n) -> p q s n", q=2, s=3)
        y1 = y1_.rearrange("p (q n) -> p q n", q=2)
        gat1 = big[:, W1:W1 + NT * K1 * D].rearrange("p (t k n) -> p t k n", t=NT, k=K1)
        gat_b = sb("gat_b", [P, 4 * D])
        gat0 = [g1_.rearrange("p (k n) -> p k n", k=K0), gat_b[:, :].rearrange("p (k n) -> p k n", k=K0)]

        hot_hi.append(work[:, 3744:3744 + K1 * NT * T1 // 2].bitcast(F16).rearrange("p (c n) -> p c n", n=T1))
        hot_lo.append([v.bitcast(F16).rearrange("p (c n) -> p c n", n=P)
                       for v in (gat_b[:, :], gx[:, :, :].rearrange("p q n -> p (q n)"))])

        glu, lin, sig = (v.rearrange("p (q n) -> p q n", q=2)
                         for v in (gat_b[:, 0:2 * F0], gat_b[:, 2 * F0:4 * F0], gx[:, 0, 0:2 * F0]))

        ps = [ctx.enter_context(nc.psum_tensor(f"ps{i}", [P, 512], F32)) for i in range(8)]

        xs = [nc.dram_tensor(f"rows_in{l}", (NT * P, D), F32, kind="Internal").ap() for l in range(2)]
        ys = [nc.dram_tensor(f"rows_out{l}", (n * P, D), F32, kind="Internal").ap() for l, n in ((0, T0), (1, T1))]

        s_x = sem("x_loaded")
        s_w0 = sem("layer0_attention_weights_loaded")
        s_rt = sem("router_weights_loaded")
        s_iota = sem("token_numbers_set")
        s_wkq = sem("layer1_wk_wq_loaded")
        s_wv = sem("layer1_wv_loaded")
        s_wo = sem("layer1_wo_loaded")
        s_const = sem("constants_set")
        s_pool = sem("pool_chain")
        s_dve = sem("dve_chain")
        s_act = sem("act_chain")
        s_blk0z = sem("layer0_blocks_zeroed")
        s_bn = sem("row_statistics")
        s_bqb = sem("query_bias_spread")
        s_crep = sem("context_columns_repeated")
        s_p0 = sem("prep0_products")
        s_p0e = sem("prep0_evacuated")
        s_var = sem("variances_ready")
        s_rstd = sem("rstd_ready")
        s_xn = sem("pair_normalised")
        s_xt = sem("pair_transposed")
        s_xte = sem("pair_transposed_copied")
        s_sc = sem("pair_scores")
        s_scb = sem("pair_scores_shifted")
        s_exp = sem("pair_exponentials")
        s_at = sem("pair_weights")
        s_att = sem("pair_weights_transposed")
        s_atte = sem("pair_weights_transposed_copied")
        s_ao = sem("pair_attended")
        s_aoe = sem("pair_residual_added")
        s_gn = sem("router_rows_normalised")
        s_un = sem("router_rows_unscaled")
        s_xl = sem("normalised_rows_added")
        s_nc = sem("normalised_rows_kept")
        s_gt = sem("router_rows_transposed")
        s_gte = sem("router_rows_transposed_copied")
        s_gl = sem("router_logits")
        s_gle = sem("router_logits_copied")
        s_rvar = sem("l1_router_variances")
        s_rbn = sem("l1_router_row_statistics")
        s_rrstd = sem("l1_router_rstd_ready")
        s_rn = sem("l1_router_rows_normalised")
        s_rk = sem("l1_router_rows_kept")
        s_rtr = sem("l1_router_rows_transposed")
        s_rte = sem("l1_router_rows_transposed_copied")
        s_rl = sem("l1_router_logits")
        s_rle = sem("l1_router_logits_copied")
        s_pmax = sem("router_logits_shifted")
        s_pexp = sem("router_exponentials")
        s_wd = sem("router_weight_differences")
        s_we = sem("router_weight_exponentials")
        s_mask = sem("assignment_masks")
        s_rank = sem("assignment_ranks")
        s_te = sem("tile_expert_column")
        s_ter = sem("tile_expert_row")
        s_slot = sem("slots_ready")
        s_info = sem("tile_info_ready")
        s_rows = [sem("token_rows_stored0"), sem("token_rows_stored1")]
        s_hot = sem("slots_one_hot")
        s_inv = sem("slot_tokens_summed")
        s_fr = [sem("routed_rows_gathered_a"), sem("routed_rows_gathered_b")]
        s_col = sem("slot_tokens_in_place")
        s_tok = sem("slot_tokens_ready")
        s_l1p = sem("layer1_table_products")
        s_l1e = sem("layer1_table_products_copied")
        s_bz = sem("layer1_blocks_zeroed")
        s_ew = [sem("expert_weights_a"), sem("expert_weights_b")]
        s_ex = [sem(f"expert_rows_{q}") for q in range(4)]
        s_eX = sem("expert_rows_transposed")
        s_eXe = sem("expert_rows_transposed_copied")
        s_eH = sem("expert_hidden_products")
        s_ehb = sem("expert_hidden_biased")
        s_eglu = sem("expert_glu_ready")
        s_elin = sem("expert_linear_ready")
        s_egate = sem("expert_gated")
        s_esig = sem("expert_sigmoid_ready")
        s_ehs = sem("expert_hidden_ready")
        s_eHT = sem("expert_hidden_transposed")
        s_eHTe = sem("expert_hidden_transposed_copied")
        s_eO = sem("expert_out_products")
        s_ey = sem("expert_rows_out_ready")
        s_est = [sem("expert_rows_stored_a"), sem("expert_rows_stored_b")]
        s_gath = [sem("rows_gathered0_a"), sem("rows_gathered0_b")]
        s_comb4 = sem("rows_combined0")
        s_mk = [sem("mask_loaded_a"), sem("mask_loaded_b")]
        s_1n = sem("l1_tile_normalised")
        s_1t = sem("l1_tile_transposed")
        s_1te = sem("l1_tile_transposed_copied")
        s_1s = sem("l1_scores")
        s_1m = sem("l1_scores_masked")
        s_1b = sem("l1_scores_shifted")
        s_1x = sem("l1_exponentials")
        s_1w = sem("l1_weights")
        s_1wt = sem("l1_weights_transposed")
        s_1wte = sem("l1_weights_transposed_copied")
        s_1o = sem("l1_attended")
        s_1r = sem("l1_residual_added")
        s_w1 = sem("layer1_experts_loaded_a")
        s_w1b = sem("layer1_experts_loaded_b")
        s_fx = [sem("routed_rows_a"), sem("routed_rows_b")]
        s_fX = sem("ffn_rows_transposed")
        s_fXe = sem("ffn_rows_transposed_copied")
        s_fG = sem("ffn_gate_up_products")
        s_fsi = sem("ffn_silu_ready")
        s_fh = sem("ffn_hidden_ready")
        s_fHT = sem("ffn_hidden_transposed")
        s_fHTe = sem("ffn_hidden_transposed_copied")
        s_fO = sem("ffn_out_products")
        s_fy = sem("ffn_out_taken")
        s_fst = [sem("routed_rows_stored_a"), sem("routed_rows_stored_b")]
        s_g1 = [sem("rows_gathered1_a"), sem("rows_gathered1_b")]
        s_half = sem("first_routed_row_added")
        s_past = sem("waits_passed")
        s_fin = sem("tile_finished")
        s_out = sem("output_stored")

        block = ctx.enter_context(nc.Block())

        x_rows, out_rows = (v.rearrange("b (h p j) d -> (b h) j p d", h=2, j=J) for v in (a["x"], out))
        mask_rows = a["mask"].rearrange("b (h p j) d -> (b h) j p d", h=2, j=J)

        def dram_tile(v, i):
            if isinstance(i.t, int):
                return v[i.t // 4, i.t % 4]
            return v[span(i.m // 2), span(2 * (i.m % 2) + i.q)].rearrange("a c p d -> (a c p) d")

        def ring_slot(eng, t):
            return eng.value_load(info[0][0:1, 1, span(t)], min_val=0, max_val=R0 - 1)

        @block.sync
        def _(sp):
            sp.dma_start(ctxT[:, :, :], a["ctxT"]).then_inc(s_w0, 16)
            sp.dma_start(w0k, a["Wk0T"]).then_inc(s_w0, 16)
            sp.dma_start(w0q, a["Wq0"]).then_inc(s_w0, 16)
            sp.dma_start(w0v, a["Wv0T"]).then_inc(s_w0, 16)
            sp.dma_start(b0c[:, :, :], a["bkq"]).then_inc(s_w0, 16)
            sp.dma_start(bvb, a["bv"].to_broadcast([P, D])).then_inc(s_w0, 16)
            for g in range(NT // J):
                sp.dma_start(xres[:, J * g:J * g + J, :],
                             x_rows[g].rearrange("j p d -> p j d")).then_inc(s_x, 16)
            sp.dma_start(gateT[:, :, :], a["gateT"]).then_inc(s_rt, 16)
            sp.dma_start(gate_b[:, :], a["gate_b"].to_broadcast([P, E0 + E1])).then_inc(s_rt, 16)
            sp.dma_start(scale_b, a["norm_scale"].to_broadcast([P, D])).then_inc(s_rt, 16)
            sp.dma_start(att_in_v, a["wk1"]).then_inc(s_wkq, 16)
            sp.dma_start(att_w_v, a["wq1T"]).then_inc(s_wkq, 16)

            def keep_rows(l, kept, each):
                rows = xs[l].rearrange("(t p) d -> p t d", p=P)

                def keep(i):
                    sp.wait_ge(kept, each * (i.t + 1))
                    sp.dma_start(rows[:, span(2 * i.t, 2), :], normed[:, span(2 * i.t, 2), :]
                                 ).then_inc(s_rows[l], 16)

                over_tiles(sp, 0, NPAIR, keep)

            keep_rows(0, s_nc, 1)
            sp.wait_ge(s_l1p, 2)
            sp.dma_start(att_in_v, a["wv1"]).then_inc(s_wv, 16)
            sp.wait_ge(s_l1p, 10)
            sp.dma_start(att_w_v, a["wo1"]).then_inc(s_wo, 16)

            sp.wait_ge(s_info, 1)

            def weights(i):
                e = sp.value_load(info[0][0:1, 0, span(i.t)], min_val=0, max_val=E0 - 1)
                r = ring_slot(sp, i.t)
                new = sp.value_load(info[0][0:1, 2, span(i.t)], min_val=0, max_val=1)
                wait(sp, s_ey, i.t - R0 + 1)
                alone(sp, s_past)
                wait(sp, s_ew[i.p], 16 * i.half)
                sp.dma_start(ring[:, span(r), :].rearrange("p a w -> p (a w)"),
                             a["w_e0"][span(e)].rearrange("a p w -> (a p) w"),
                             cond=(new != 0)).then_inc(s_ew[i.p], 16)

            for t in range(AHEAD):
                weights(Tile(t // 4, t % 4, 4))
            sp.wait_ge(s_l1p, 20)
            sp.wait_ge(s_inv, 1)
            over_tiles(sp, AHEAD, T0, weights, lead=R0, tail=0, u=4)

            def mask_tile(i):
                wait(sp, s_1m, i.t - 1)
                sp.dma_start(msk[:, i.q, :], dram_tile(mask_rows, i)).then_inc(s_mk[i.q], 16)

            sp.wait_ge(s_ey, T0)
            mask_tile(Tile(0, 0))
            mask_tile(Tile(0, 1))
            for t in range(2, NT):
                mask_tile(Tile(t // 2, t % 2))
                if t - 2 < EARLY:
                    sp.dma_start(w1s[:, t - 2, :], a["w_e1"][t - 2]).then_inc(s_w1, 16)
            keep_rows(1, s_rk, 2)
            sp.wait_ge(s_1r, NT)
            for e in range(EARLY, 8):
                sp.dma_start(w1s[:, e, :], a["w_e1"][e]).then_inc(s_w1b, 16)

            sp.wait_ge(s_info, 2)

            def rows1(source):
                def body(i):
                    wait(sp, s_fX, i.t - 1)
                    sp.dma_start(xr1[:, i.q, :], source(i)).then_inc(s_fx[i.q], 16)
                return body

            def token_rows(first):
                return rows1(lambda i: normed[:, span(i.plus(first).t), :].rearrange("p a d -> p (a d)"))

            over_tiles(sp, 0, SHARED_A, token_rows(0))
            over_tiles(sp, MID1, N1, token_rows(-T1))

            def output(i):
                sp.wait_ge(s_fin, i.t + 1)
                sp.dma_start(dram_tile(out_rows, i),
                             xres[:, span(i.t), :].rearrange("p a d -> p (a d)")).then_inc(s_out, 16)

            over_tiles(sp, 0, NT, output)
            sp.wait_ge(s_out, 16 * NT)

        @block.gpsimd
        def _(pool):
            chain = Chain(pool, s_pool)
            chain(pool.memset(ident[:, :], 0.0))
            chain(pool.memset(tri_b[:, :], 1.0))
            chain(pool.memset(blkmask, 1.0))
            pool.memset(kblk0_, 0.0).then_inc(s_blk0z, 1)
            pool.memset(tabV0_, 0.0).then_inc(s_blk0z, 1)
            chain.wait()
            pool.affine_select(out=ident[:, :], in_=ident[:, :], compare_op=ALU.not_equal, fill=1.0, base=0,
                               pattern=[[-1, P]], channel_multiplier=1).then_inc(s_const, 1)
            pool.affine_select(out=tri_b[:, :], in_=tri_b[:, :], compare_op=ALU.is_ge, fill=0.0, base=-1,
                               pattern=[[1, P]], channel_multiplier=-1).then_inc(s_const, 1)
            halves = [blkmask[64 * h:64 * h + 64, :].rearrange("p (c d) -> p c d", c=C0) for h in range(2)]
            pool.wait_ge(s_const, 2)
            for m in halves:
                chain(pool.affine_select(out=m, in_=m, compare_op=ALU.is_ge, fill=0.0, base=0,
                                         pattern=[[-KEYS0, C0], [0, DH]], channel_multiplier=1))
                chain.wait()
            for n, m in enumerate(halves):
                pool.affine_select(out=m, in_=m, compare_op=ALU.is_ge, fill=0.0, base=KEYS0 - 1,
                                   pattern=[[KEYS0, C0], [0, DH]], channel_multiplier=-1).then_inc(s_const, 1)
                pool.wait_ge(s_const, 3 + n)
            pool.memset(ones_b[:, :], 1.0).then_inc(s_const, 1)
            pool.memset(mhalf[:, :], -0.5).then_inc(s_const, 1)
            pool.memset(eps_t[:, :], EPS).then_inc(s_const, 1)
            pool.memset(blk1, 0.0).then_inc(s_bz, 1)
            pool.iota(iota_p[:, :], pattern=[[1, P]], base=0, channel_multiplier=0,
                      allow_small_or_imprecise_dtypes=True).then_inc(s_iota, 1)
            pool.iota(token_id[:, :], pattern=[[P, NT]], base=0, channel_multiplier=1,
                      allow_small_or_imprecise_dtypes=True).then_inc(s_iota, 1)
            pool.wait_ge(s_const, 7)

            def factor(base, i, width, twice, cbase):
                q, w = i.q, slice(0, width)
                chain.step(cbase, 5 if twice else 1, i.t)
                pool.wait_ge(s_var, base + i.t + 1)
                v, r = mv[:, q, w, 1], rs[:, q, w]
                chain(pool.tensor_tensor(rtmp[:, 0, w], v, eps_t[:, w], ALU.add))
                chain.wait()
                if not twice:
                    pool.tensor_tensor(r, rtmp[:, 0, w], mhalf[:, w], ALU.pow).then_inc(s_rstd, 1)
                else:
                    chain(pool.tensor_tensor(r, rtmp[:, 0, w], mhalf[:, w], ALU.pow))
                    chain.wait()
                    chain(pool.tensor_tensor(rtmp[:, 0, w], v, r, ALU.mult))
                    chain.wait()
                    chain(pool.tensor_tensor(rtmp[:, 0, w], rtmp[:, 0, w], r, ALU.mult))
                    chain.wait()
                    chain(pool.tensor_tensor(rtmp[:, 0, w], rtmp[:, 0, w], eps_t[:, w], ALU.add))
                    chain.wait()
                    pool.tensor_tensor(rms[:, q, w], rtmp[:, 0, w], mhalf[:, w], ALU.pow).then_inc(s_rstd, 1)
                chain.stepped()
                pool.wait_ge(s_rstd, base + i.t + 1)

            def iotas():
                pool.iota(pidx, pattern=[[0, 1]], base=0, channel_multiplier=1,
                          allow_small_or_imprecise_dtypes=True).then_inc(s_const, 1)
                pool.iota(iota_e, pattern=[[1, E0]], base=0, channel_multiplier=0,
                          allow_small_or_imprecise_dtypes=True).then_inc(s_const, 1)

            def gather_rows(l, sem_, buf, i):
                place = token_col[:, i.q:i.q + 1]
                pool.tensor_copy(out=place, in_=slot_token[l][:, span(i.t)]).then_inc(s_col, 1)
                pool.wait_ge(s_col, l * T0 + i.t + 1)
                alone(pool, s_past)
                pool.indirect_dma_start(
                    out=buf, out_offset=None, in_=xs[l],
                    in_offset=bass.IndirectOffsetOnAxis(ap=place.bitcast(U32), axis=0)).then_inc(sem_, 16)

            c0 = chain.n
            over_tiles(pool, 0, NPAIR, lambda i: factor(0, i, 2, False, c0))
            c1 = c0 + NPAIR
            over_tiles(pool, 0, NPAIR, lambda i: factor(NPAIR, i, 2, True, c1))
            c2 = c1 + 5 * NPAIR
            iotas()
            pool.wait_ge(s_tok, 1)
            pool.wait_ge(s_rows[0], 16 * NPAIR)

            def rows0(i):
                if i.exists(0, T0):
                    wait(pool, s_eX, i.t - 3)
                    gather_rows(0, s_ex[i.q], xr0[:, i.q, :], i)
                j = i.plus(-LAG0)
                if j.exists(0, T0) and j.p == 0:
                    pool.wait_ge(s_ey, j.t + 2)
                    pool.dma_start(ys[0][span(j.t * P, 2 * P), :].rearrange("(k p) d -> p k d", k=2),
                                   y0[:, j.pair]).then_inc(s_est[j.pair], 16)

            over_tiles(pool, 0, T0 + LAG0, rows0, lead=LAG0, tail=LAG0, u=4)
            for q in range(2):
                pool.wait_ge(s_est[q], 16 * T0 // 4)

            def gather0(i):
                if i >= 2:
                    pool.wait_ge(s_comb4, K0 * (i - 1))
                for k in range(K0):
                    pool.indirect_dma_start(
                        out=gat0[i % 2][:, k, :], out_offset=None, in_=ys[0],
                        in_offset=bass.IndirectOffsetOnAxis(ap=slot_i[0][:, k, i:i + 1].bitcast(U32), axis=0)
                    ).then_inc(s_gath[i % 2], 16)

            def router_factor(i):
                q = i % 2
                pool.wait_ge(s_rvar, i + 1)
                chain(pool.tensor_tensor(rtmp[:, 0, 1:2], mv[:, q, 1, 1:2], eps_t[:, 1:2], ALU.add))
                chain.wait()
                pool.tensor_tensor(rs[:, q, 1:2], rtmp[:, 0, 1:2], mhalf[:, 1:2], ALU.pow).then_inc(s_rrstd, 1)
                pool.wait_ge(s_rrstd, i + 1)

            chain.n = c2
            gather0(0)
            for i in range(NT):
                if i + 1 < NT:
                    gather0(i + 1)
                factor(2 * NPAIR, Tile(i // 2, i % 2), 1, False, chain.n - i)
                if i >= LAGR:
                    router_factor(i - LAGR)
            for i in range(NT - LAGR, NT):
                router_factor(i)
            iotas()
            pool.wait_ge(s_tok, 2)
            pool.wait_ge(s_rows[1], 16 * NPAIR)

            def rows1(i):
                if i.exists(0, T1):
                    pool.wait_ge(s_fX, SHARED_A + i.t - 1)
                    gather_rows(1, s_fr[i.q], xr1[:, i.q, :], i)
                j = i.plus(-LAG1)
                if j.exists(0, T1):
                    pool.wait_ge(s_fy, SHARED_A + j.t + 1)
                    pool.dma_start(ys[1][span(j.t * P, P), :], y1[:, j.q, :]).then_inc(s_fst[j.q], 16)

            over_tiles(pool, 0, T1 + LAG1, rows1, lead=LAG1, tail=LAG1)
            for q in range(2):
                pool.wait_ge(s_fst[q], 16 * T1 // 2)
            for i in range(NT):
                if i >= 2:
                    pool.wait_ge(s_g1[i % 2], 16 * K1 * (i // 2))
                for k in range(K1):
                    pool.indirect_dma_start(
                        out=gat1[:, i, k, :], out_offset=None, in_=ys[1],
                        in_offset=bass.IndirectOffsetOnAxis(ap=slot_i[1][:, k, i:i + 1].bitcast(U32), axis=0)
                    ).then_inc(s_g1[i % 2], 16)

        @block.scalar
        def _(act):
            def copy(out_, in_, sem_, scale=1.0):
                act.activation(out_, in_, ACT.Copy, scale=scale).then_inc(sem_, 1)

            def exps0(i):
                act.wait_ge(s_scb, i.t + 1)
                act.activation(sc0[:, i.q, :], sc0[:, i.q, :], ACT.Exp).then_inc(s_exp, 1)

            def rows_t0(i):
                act.wait_ge(s_xt, i.t + 1)
                wait(act, s_sc, i.t - 1)
                copy(xT_a[:, i.q, :], ps[i.q][:, :], s_xte)

            def weights_t0(i):
                act.wait_ge(s_att, i.t + 1)
                wait(act, s_ao, i.t - 1)
                copy(aT0[:, i.q, :], ps[4][:, 0:P], s_atte)

            rows_t0(Tile(0, 0))

            def attend0(i):
                exps0(i)
                if i.plus(1).exists(0, NPAIR):
                    rows_t0(i.plus(1))
                weights_t0(i)

            over_tiles(act, 0, NPAIR, attend0)

            def router_rows(l):
                def body(i):
                    act.wait_ge(s_gt, l * NPAIR + i.t + 1)
                    wait(act, s_gl, l * NPAIR + i.t - 1)
                    copy(gx[:, i.q, :], ps[i.q][:, :], s_gte)
                    copy(normed[:, span(2 * i.t, 2), :], xn_r[:, i.q, :].rearrange("p (a d) -> p a d", a=2), s_nc)

                over_tiles(act, 0, NPAIR, body)

            router_rows(0)

            act.wait_ge(s_wd, 1)
            act.activation(wexp[:, :, :], wexp[:, :, :], ACT.Exp).then_inc(s_we, 1)

            def blocks(base):
                for g in range(2):
                    act.wait_ge(s_l1p, base + g + 1)
                    for h in range(2):
                        r = slice(64 * h, 64 * h + 64)
                        dst = blk1_v[r, 4 * g:4 * g + 4, :, h, :]
                        src = ps[g][r, :].rearrange("p (h b s) -> p h b s", h=4, b=B)
                        ins = act.activation(dst, src, ACT.Copy, scale=DH ** -0.5 if base == 0 else 1.0)
                    ins.then_inc(s_l1e, 1)

            act.wait_ge(s_bz, 1)
            blocks(0)
            for n in range(8):
                act.wait_ge(s_l1p, 3 + n)
                k, g = n // 4, n % 4
                copy(tabA[:, :, k, 256 * g:256 * g + 256].rearrange("p b (h n) -> p h b n", h=2),
                     ps[2 + n % 2][:, :].rearrange("p (h b n) -> p h b n", h=2, b=B), s_l1e)
            blocks(10)
            for n in range(8):
                act.wait_ge(s_l1p, 13 + n)
                b, g = n // 4, n % 4
                copy(tabV[:, b, 2 * g:2 * g + 2, :], ps[2 + n % 2][:, :].rearrange("p (h n) -> p h n", h=2), s_l1e)

            act.wait_ge(s_info, 1)

            def rows_e0(i):
                act.wait_ge(s_eX, i.t + 1)
                wait(act, s_eH, i.t - 1)
                copy(xT0[:, i.p, :, :], ps[i.p][:, 0:D].rearrange("p (k n) -> p k n", k=FK), s_eXe)

            def hidden_t0(i):
                act.wait_ge(s_eHT, i.t + 1)
                wait(act, s_eO, i.t - 1)
                copy(hT0[:, i.p, :, :], ps[4][:, 0:D].rearrange("p (k n) -> p k n", k=2), s_eHTe)

            def sigmoid0(i):
                act.wait_ge(s_eglu, i.t + 1)
                wait(act, s_ehs, i.t - 1)
                act.activation(sig[:, i.p], glu[:, i.p], ACT.Sigmoid, scale=ALPHA).then_inc(s_esig, 1)

            rows_e0(Tile(0, 0, 4))

            def expert0(i):
                if i.plus(-2).exists(0, T0):
                    hidden_t0(i.plus(-2))
                if i.plus(-1).exists(0, T0):
                    sigmoid0(i.plus(-1))
                if i.plus(1).exists(0, T0):
                    rows_e0(i.plus(1))

            over_tiles(act, 0, T0 + 2, expert0, lead=4, tail=4, u=4)

            def exps1(i, first, last):
                act.wait_ge(s_1b, i.t + 1)
                for h in range(first, last):
                    s = sc1[:, i.q, h * S2:h * S2 + S2]
                    ins = act.activation(s, s, ACT.Exp, bias=sm1[:, i.q, 0, h:h + 1],
                                         accum_out=sm1[:, i.q, 1, h:h + 1])
                if last == H1:
                    ins.then_inc(s_1x, 1)

            def rows_t1(i):
                act.wait_ge(s_1t, i.t + 1)
                wait(act, s_1s, i.t - 1)
                copy(xT1[:, i.q, :, :], ps[0][:, 0:D].rearrange("p (k n) -> p k n", k=FK), s_1te)

            def weights_t1(i):
                act.wait_ge(s_1wt, i.t + 1)
                wait(act, s_1o, i.t)
                for g in range(2):
                    ins = act.activation(aT1[:, 4 * g:4 * g + 4, :],
                                         ps[5 + g][:, :].rearrange("p (h n) -> p h n", h=4), ACT.Copy)
                ins.then_inc(s_1wte, 1)

            def router1(i):
                act.wait_ge(s_rtr, i.t + 1)
                wait(act, s_rl, i.t - 1)
                copy(gx[:, i.q, 0:D], ps[0][:, D:2 * D], s_rte)
                copy(normed[:, span(i.t), :].rearrange("p a d -> p (a d)"), xn_f[:, i.q, :], s_rk)

            def attend1(i):
                if i.plus(2).exists(0, NT):
                    rows_t1(i.plus(2))
                if i.plus(-2).exists(0, NT):
                    router1(i.plus(-2))
                if i.plus(1).exists(0, NT):
                    exps1(i.plus(1), 0, H1 // 2)
                if i.exists(0, NT):
                    weights_t1(i)
                if i.plus(1).exists(0, NT):
                    exps1(i.plus(1), H1 // 2, H1)

            rows_t1(Tile(0, 0))
            attend1(Tile(-1, 1))
            over_tiles(act, 0, NT + 2, attend1, lead=4, tail=4)
            act.wait_ge(s_pmax, 1)
            act.activation(logits[:, :, 0:E1], logits[:, :, 0:E1], ACT.Exp).then_inc(s_pexp, 1)

            act.wait_ge(s_info, 2)

            def rows_e1(i):
                act.wait_ge(s_fX, i.t + 1)
                wait(act, s_fG, 2 * (i.t - 1))
                copy(xTe[:, i.q, :, :], ps[0][:, 0:D].rearrange("p (k n) -> p k n", k=FK), s_fXe)

            def hidden_t1(i, c):
                u = 2 * i.t + c
                act.wait_ge(s_fHT, u + 1)
                wait(act, s_fO, u - 1)
                copy(hTe[:, c, :, :], ps[5][:, 0:3 * P].rearrange("p (s n) -> p s n", s=3), s_fHTe)

            def silu1(i, c):
                u = 2 * i.t + c
                act.wait_ge(s_fG, u + 1)
                wait(act, s_fh, u - 1)
                act.activation(silu[:, c, :], ps[1 + 2 * c][:, 0:FC1], ACT.Silu).then_inc(s_fsi, 1)

            rows_e1(Tile(0, 0))

            def expert1(i):
                if i.exists(0, N1):
                    silu1(i, 0)
                if i.plus(-1).exists(0, N1):
                    hidden_t1(i.plus(-1), 1)
                if i.plus(1).exists(0, N1):
                    rows_e1(i.plus(1))
                if i.exists(0, N1):
                    silu1(i, 1)
                    hidden_t1(i, 0)

            over_tiles(act, 0, N1, expert1)
            expert1(Tile(N1 // 2, 0))

        @block.vector
        def _(dve):
            chain = Chain(dve, s_dve)
            TT, TS, STT, CP = dve.tensor_tensor, dve.tensor_scalar, dve.scalar_tensor_tensor, dve.tensor_copy

            def over(ap, n):
                return ap.unsqueeze(len(ap.shape)).broadcast_to([*ap.shape, n])

            def spread(ap, n):
                return ap.unsqueeze(1).broadcast_to([ap.shape[0], n, ap.shape[1]])

            dve.wait_ge(s_w0, 16 * 6)
            for m in range(2):
                ins = CP(bqb[:, m, :], b0c[:, 1, m:m + 1].broadcast_to([P, P]))
            ins.then_inc(s_bqb, 1)
            for k in range(FK):
                for b in range(B):
                    for c in range(C0):
                        ins = CP(crep[:, k, b, :, c, :],
                                 ctxT[:, k, b * S2:b * S2 + S2].rearrange("p (s j) -> p j s", j=J))
            ins.then_inc(s_crep, 1)
            dve.wait_ge(s_p0, 1)
            dve.wait_ge(s_blk0z, 2)
            for m in range(2):
                for h in range(2):
                    r = slice(64 * h, 64 * h + 64)
                    ins = TS(kblk0[r, m, h, :], ps[0][r, m * P:m * P + P], b0c[r, 0, m:m + 1], None, ALU.add)
            ins.then_inc(s_p0e, 1)
            dve.wait_ge(s_p0, 2)
            for k in range(3):
                src = ps[1 + k][:, :].rearrange("p (c b s j) -> p b j c s", c=C0, b=B, j=J)
                for b in range(B):
                    ins = TS(tabA0[:, k, b], src[:, b], DH ** -0.5, None, ALU.mult)
            ins.then_inc(s_p0e, 1)
            dve.wait_ge(s_p0, 3)
            vals = ab[:, 0:1024].rearrange("p (n d) -> p n d", n=4)
            for n in range(4):
                chain(TT(vals[:, n, :], ps[4 + n // 2][:, 256 * (n % 2):256 * (n % 2) + 256], bvb, ALU.add))
            chain.wait()
            dve.wait_ge(s_const, 7)
            for n in range(4):
                for j in range(2):
                    r = slice(64 * j, 64 * j + 64)
                    ins = TT(tabV0[r, n // 2, n % 2, j, :], vals[r, n, :], blkmask[r, :], ALU.mult)
            ins.then_inc(s_p0e, 1)

            def statistics(base, var_base, t, q, rows):
                wait(dve, s_var, var_base + t)
                alone(dve, s_past)
                for k, x in enumerate(rows):
                    dve.bn_stats(stats[:, k, :], x).then_inc(s_bn, 1)
                dve.wait_ge(s_bn, base + len(rows) * (t + 1))
                alone(dve, s_past)
                for k in range(len(rows)):
                    ins = dve.bn_aggr(mv[:, q, k, :], stats[:, k, :])
                ins.then_inc(s_var, 1)

            def row(i, k=0):
                return xres[:, span(2 * i.t + k), :].rearrange("p a d -> p (a d)")

            def pair(v, i):
                return v[:, span(2 * i.t, 2), :]

            def pair_stats(i, base=0, var_base=0):
                statistics(base, var_base, i.t, i.q, [row(i, 0), row(i, 1)])

            dve.wait_ge(s_x, 16 * (NT // J))

            def normalise0(i):
                dve.wait_ge(s_rstd, i.t + 1)
                wait(dve, s_xt, i.t - 1)
                for k in range(2):
                    ins = TS(xn_a[:, i.q, k * D:k * D + D], row(i, k), mv[:, i.q, k, 0:1],
                             rs[:, i.q, k:k + 1], ALU.subtract, ALU.mult)
                ins.then_inc(s_xn, 1)

            def shift0(i):
                s = sc0[:, i.q, :]
                sg = s.rearrange("p (g n) -> p g n", n=KEYS0)
                dve.wait_ge(s_sc, i.t + 1)
                bias = tabA0[:, 2].rearrange("p b j c s -> p b (j c s)")[:, span(i.m // 2), P * i.q:P * i.q + P]
                chain(TT(s, ps[2 + i.q][:, 0:P], bias.rearrange("p a n -> p (a n)"), ALU.add))
                chain.wait()
                chain(dve.tensor_reduce(sm0[:, 0, 0:8], sg, AX.X, ALU.max))
                chain.wait()
                TT(sg, sg, over(sm0[:, 0, 0:8], KEYS0), ALU.subtract).then_inc(s_scb, 1)

            def weights0(i):
                sg = sc0[:, i.q, :].rearrange("p (g n) -> p g n", n=KEYS0)
                dve.wait_ge(s_exp, i.t + 1)
                chain(dve.tensor_reduce(sm0[:, 1, 0:8], sg, AX.X, ALU.add))
                chain.wait()
                chain(dve.reciprocal(sm0[:, 2, 0:8], sm0[:, 1, 0:8]))
                chain.wait()
                TT(sg, sg, over(sm0[:, 2, 0:8], KEYS0), ALU.mult).then_inc(s_at, 1)

            def residual0(i):
                dve.wait_ge(s_ao, i.t + 1)
                TT(pair(xres, i), pair(xres, i), ps[5 + i.q][:, :].rearrange("p (a d) -> p a d", a=2),
                   ALU.add).then_inc(s_aoe, 1)

            pair_stats(Tile(0, 0))
            dve.wait_ge(s_p0e, 2)
            normalise0(Tile(0, 0))
            c0 = chain.n

            def attend0(i):
                chain.step(c0, 4, i.t)
                if i.plus(1).exists(0, NPAIR):
                    pair_stats(i.plus(1))
                shift0(i)
                if i.plus(1).exists(0, NPAIR):
                    normalise0(i.plus(1))
                weights0(i)
                chain.stepped()
                if i.plus(-1).exists(0, NPAIR):
                    residual0(i.plus(-1))

            over_tiles(dve, 0, NPAIR, attend0)
            residual0(Tile(NPAIR // 2 - 1, 1))

            def router_rows(l, bn_base, var_base, columns, bias):
                def normalise(i):
                    dve.wait_ge(s_rstd, var_base + i.t + 1)
                    wait(dve, s_gt, l * NPAIR + i.t - 1)
                    wait(dve, s_nc, l * NPAIR + i.t - 1)
                    u = xn_r if l else xn_a
                    for k in range(2):
                        ins = TS(u[:, i.q, k * D:k * D + D], row(i, k), mv[:, i.q, k, 0:1],
                                 rs[:, i.q, k:k + 1], ALU.subtract, ALU.mult)
                    if l == 0:
                        ins.then_inc(s_un, 1)
                        dve.wait_ge(s_un, i.t + 1)
                        for k in range(2):
                            ins = STT(out=xn_r[:, i.q, k * D:k * D + D], in0=xn_a[:, i.q, k * D:k * D + D],
                                      scalar=rms[:, i.q, k:k + 1], in1=scale_b, op0=ALU.mult, op1=ALU.mult)
                        TT(pair(xres, i), pair(xres, i), xn_a[:, i.q, :].rearrange("p (a d) -> p a d", a=2),
                           ALU.add).then_inc(s_xl, 1)
                    ins.then_inc(s_gn, 1)

                def take(i):
                    dve.wait_ge(s_gl, l * NPAIR + i.t + 1)
                    TT(logits[:, span(2 * i.t, 2), 0:columns],
                       ps[2 + i.q][:, 0:2 * columns].rearrange("p (a e) -> p a e", a=2),
                       spread(bias, 2), ALU.add).then_inc(s_gle, 1)

                def body(i):
                    if i.plus(1).exists(0, NPAIR):
                        pair_stats(i.plus(1), bn_base, var_base)
                    normalise(i)
                    if i.plus(-1).exists(0, NPAIR):
                        take(i.plus(-1))

                pair_stats(Tile(0, 0), bn_base, var_base)
                over_tiles(dve, 0, NPAIR, body)
                take(Tile(NPAIR // 2 - 1, 1))
                dve.wait_ge(s_gle, (l + 1) * NPAIR)

            def ranks_to_slots(l, columns, real, chosen, tiles):
                one = r_one.bitcast(BF16)[:, 0:chosen * NT * columns].rearrange(
                    "p (k t e) -> p k t e", k=chosen, t=NT)
                mask = r_mask.bitcast(BF16)[:, 0:NT * columns].rearrange("p (t e) -> p t e", t=NT)
                slot = r_slot[:, 0:NT * columns].rearrange("p (t e) -> p t e", t=NT)
                tmp = r_tmp[:, 0:NT * columns].rearrange("p (t e) -> p t e", t=NT)
                E = slice(0, columns)
                dve.wait_ge(s_const, 9 + 2 * l)
                chain.wait()
                chain(CP(topf, topi[:, :, :]))
                chain.wait()
                for k in range(chosen):
                    chain(TT(one[:, k], spread(iota_e[:, E], NT), over(topf[:, :, k], columns), ALU.is_equal))
                chain.wait()
                for k in range(1, chosen):
                    ins = TT(mask, one[:, 0] if k == 1 else mask, one[:, k], ALU.add)
                    if k < chosen - 1:
                        chain(ins)
                        chain.wait()
                ins.then_inc(s_mask, 1)
                dve.wait_ge(s_rank, l + 1)
                chain(TS(cnt_i[:, E], ps[5][:, E], float(P - 1), None, ALU.add))
                chain.wait()
                chain(TS(cnt_i[:, E], cnt_i[:, E], 7, None, ALU.logical_shift_right))
                chain(dve.memset(ones_f[:, E], 1.0))
                chain.wait()
                chain(CP(tiles_f[:, E], cnt_i[:, E]))
                chain.wait()
                chain(dve.tensor_tensor_scan(ends_f[:, E], ones_f[:, E], tiles_f[:, E], 0.0, ALU.mult, ALU.add))
                chain.wait()
                chain(TT(base_f[:, E], ends_f[:, E], tiles_f[:, E], ALU.subtract))
                chain.wait()
                chain(TS(base_f[:, E], base_f[:, E], float(P), None, ALU.mult))
                chain.wait()
                chain(TT(slot, ps[4][:, 0:NT * columns].rearrange("p (t e) -> p t e", t=NT),
                         spread(base_f[:, E], NT), ALU.add))
                chain.wait()
                for k in range(chosen):
                    chain.wait()
                    chain(TT(tmp, one[:, k], slot, ALU.mult))
                    chain.wait()
                    chain(dve.tensor_reduce(slots_f[:, k, :], tmp, AX.X, ALU.add))
                chain.wait()
                chain(CP(slot_i[l][:, :, :], slots_f[:, 0:chosen, :]))
                chain(TS(cmp_f[0:tiles, E], ends_f[0:tiles, E], pidx[0:tiles, :], None, ALU.is_le))
                chain.wait()
                chain(dve.tensor_reduce(te_col[0:tiles, 0:1], cmp_f[0:tiles, E], AX.X, ALU.add))
                chain.wait()
                TS(te_col[0:tiles, 0:1], te_col[0:tiles, 0:1], float(real - 1), None, ALU.min).then_inc(s_te, 1)
                te, fl, rk, on = (v[:, 0:tiles] for v in (te_row, fl_row, rk_row, one_row))
                chain(dve.memset(fl[:, 0:1], 1.0))
                chain(dve.memset(on, 1.0))
                dve.wait_ge(s_ter, l + 1)
                chain(CP(te, ps[6][0:1, 0:tiles]))
                chain.wait()
                chain(TT(fl[:, 1:tiles], te[:, 1:tiles], te[:, 0:tiles - 1], ALU.not_equal))
                chain.wait()
                chain(dve.tensor_tensor_scan(rk, on, fl, -1.0, ALU.mult, ALU.add))
                if l == 1:
                    chain(dve.memset(info[1][:, :, :], 0))
                    chain.wait()
                    TS(info[1][:, 0, SHARED_A:MID1], te, 1.0, None, ALU.add).then_inc(s_info, 1)
                else:
                    chain(CP(info[0][:, 0, :], te))
                    chain(CP(info[0][:, 2, :], fl))
                    chain.wait()
                    chain(CP(info[0][:, 1, :], rk))
                    chain.wait()
                    TS(info[0][:, 1, :], info[0][:, 1, :], R0 - 1, None, ALU.bitwise_and).then_inc(s_info, 1)
                n = chosen * NT
                flat = slot_i[l][:, :, :].rearrange("p k t -> p (k t)")
                chain(TS(slot_sh[:, 0:n], flat, 7, None, ALU.logical_shift_right))
                chain.wait()
                chain(CP(slot_hi[:, 0:n], slot_sh[:, 0:n]))
                chain.wait()
                chain(TS(slot_sh[:, 0:n], flat, P - 1, None, ALU.bitwise_and))
                chain.wait()
                chain(CP(slot_lo[:, 0:n], slot_sh[:, 0:n]))
                chain.wait()
                dve.wait_ge(s_iota, 2)
                for c in range(n):
                    TS(hot_hi[l][:, c, :], iota_p[:, 0:tiles], slot_hi[:, c:c + 1],
                       token_id[:, c % NT:c % NT + 1], ALU.is_equal, ALU.mult)
                    TS(hot_lo[l][c // NT][:, c % NT, :], iota_p[:, :], slot_lo[:, c:c + 1], None,
                       ALU.is_equal).then_inc(s_hot, 1)
                dve.wait_ge(s_inv, l + 1)
                CP(slot_token[l][:, :], ps[7][:, 0:tiles]).then_inc(s_tok, 1)

            dve.wait_ge(s_rt, 16 * 3)
            router_rows(0, 2 * NPAIR, NPAIR, E0, gate_b[:, 0:E0])
            chain.n = c0 + 4 * NPAIR

            def choose(columns):
                for i in range(NT):
                    chain(dve.max(top[:, i, :], logits[:, i, 0:columns]))
                chain.wait()
                for i in range(NT):
                    chain(dve.max_index(topi[:, i, :], top[:, i, :], logits[:, i, 0:columns]))

            choose(E0)
            TT(wexp[:, :, :], top[:, :, 0:K0], over(top[:, :, 0], K0), ALU.subtract).then_inc(s_wd, 1)
            ranks_to_slots(0, E0, E0, K0, T0)
            dve.wait_ge(s_we, 1)
            chain(dve.tensor_reduce(wsum[:, 0, :], wexp[:, :, :], AX.X, ALU.add))
            chain.wait()
            chain(dve.reciprocal(wsum[:, 1, :], wsum[:, 0, :]))
            chain.wait()
            chain(TT(wgt[0][:, :, :], wexp[:, :, :], over(wsum[:, 1, :], K0), ALU.mult))

            slot_at = Registers(lambda t: ring_slot(dve, t))

            def biases(i, lo, n):
                return ring[:, span(slot_at[i]), W0 + lo:W0 + lo + n].rearrange("p a n -> p (a n)")

            def bias0(i):
                dve.wait_ge(s_eH, i.t + 1)
                TT(hb_, ps[2 + i.p][:, :], biases(i, 0, 2 * F0), ALU.add).then_inc(s_ehb, 1)

            def clip0(i):
                dve.wait_ge(s_ehb, i.t + 1)
                wait(dve, s_ehs, i.t - 1)
                TS(glu[:, i.p], hb_[:, 0:F0], LIMIT, None, ALU.min).then_inc(s_eglu, 1)
                TS(lin[:, i.p], hb_[:, F0:2 * F0], LIMIT, -LIMIT, ALU.min, ALU.max).then_inc(s_elin, 1)

            def gate0(i):
                dve.wait_ge(s_elin, i.t + 1)
                STT(out=lin[:, i.p], in0=lin[:, i.p], scalar=1.0, in1=glu[:, i.p], op0=ALU.add,
                    op1=ALU.mult).then_inc(s_egate, 1)

            def hidden0(i):
                dve.wait_ge(s_egate, i.t + 1)
                dve.wait_ge(s_esig, i.t + 1)
                wait(dve, s_eHT, i.t - 1)
                TT(hs0[:, i.p, :], lin[:, i.p], sig[:, i.p], ALU.mult).then_inc(s_ehs, 1)

            def rows_out0(i):
                bias = biases(i, 2 * F0, D)
                dve.wait_ge(s_eO, i.t + 1)
                wait(dve, s_est[i.pair], 16 * i.m)
                TT(y0[:, i.pair, i.p, :], ps[5 + i.p][:, 0:D], bias, ALU.add).then_inc(s_ey, 1)

            def expert0(i):
                slot_at.begin(i)
                last = i.plus(-1)
                if last.exists(0, T0):
                    gate0(last)
                if i.exists(0, T0):
                    slot_at.load(i)
                if last.exists(0, T0):
                    hidden0(last)
                if i.exists(0, T0):
                    bias0(i)
                if i.plus(-2).exists(0, T0):
                    slot_at.load(i.plus(-2))
                if i.exists(0, T0):
                    clip0(i)
                if i.plus(-2).exists(0, T0):
                    rows_out0(i.plus(-2))

            over_tiles(dve, 0, T0 + 2, expert0, lead=4, tail=4, u=4)

            c1 = chain.n
            BN1 = 4 * NPAIR

            def row1(i):
                return xres[:, span(i.t), :].rearrange("p a d -> p (a d)")

            def combine0(i):
                dve.wait_ge(s_gath[i.q], 16 * K0 * (i.m + 1))
                for k in range(K0):
                    w = wgt[0][:, span(i.t), k:k + 1].rearrange("p a k -> p (a k)")
                    ins = STT(out=row1(i), in0=gat0[i.q][:, k, :], scalar=w, in1=row1(i),
                              op0=ALU.mult, op1=ALU.add)
                    ins.then_inc(s_comb4, 1)
                    dve.wait_ge(s_comb4, K0 * i.t + k + 1)
                statistics(BN1, 2 * NPAIR, i.t, i.q, [row1(i)])

            def normalise1(i):
                dve.wait_ge(s_rstd, 2 * NPAIR + i.t + 1)
                wait(dve, s_1t, i.t - 1)
                TS(xn1[:, i.q, :], row1(i), mv[:, i.q, 0, 0:1], rs[:, i.q, 0:1],
                   ALU.subtract, ALU.mult).then_inc(s_1n, 1)

            def shift1(i):
                s = sc1[:, i.q, :].rearrange("p (h n) -> p h n", h=H1)
                dve.wait_ge(s_1s, i.t + 1)
                dve.wait_ge(s_mk[i.q], 16 * (i.m + 1))
                for g in range(2):
                    ins = TT(s[:, 8 * g:8 * g + 8, :], ps[1 + 2 * i.q + g][:, :].rearrange("p (h n) -> p h n", h=8),
                             spread(msk[:, i.q, :], 8), ALU.add)
                ins.then_inc(s_1m, 1)
                dve.wait_ge(s_1m, i.t + 1)
                dve.tensor_reduce(sm1[:, i.q, 0, :], s, AX.X, ALU.max, negate=True).then_inc(s_1b, 1)

            def weights1(i):
                s = sc1[:, i.q, :].rearrange("p (h n) -> p h n", h=H1)
                dve.wait_ge(s_1x, i.t + 1)
                chain(dve.reciprocal(sm1[:, i.q, 2, :], sm1[:, i.q, 1, :]))
                chain.wait()
                TT(s, s, over(sm1[:, i.q, 2, :], S2), ALU.mult).then_inc(s_1w, 1)

            def residual1(i):
                dve.wait_ge(s_1o, i.t + 1)
                TT(row1(i), row1(i), ps[7][:, 0:D], ALU.add).then_inc(s_1r, 1)

            def router_statistics(i):
                dve.wait_ge(s_1r, i.t + 1)
                wait(dve, s_rvar, i.t)
                alone(dve, s_past)
                dve.bn_stats(stats[:, 1, :], row1(i)).then_inc(s_rbn, 1)
                dve.wait_ge(s_rbn, i.t + 1)
                alone(dve, s_past)
                dve.bn_aggr(mv[:, i.q, 1, :], stats[:, 1, :]).then_inc(s_rvar, 1)

            def router_normalise(i):
                dve.wait_ge(s_rrstd, i.t + 1)
                wait(dve, s_rtr, i.t - 1)
                wait(dve, s_rk, i.t - 1)
                TS(xn_f[:, i.q, :], row1(i), mv[:, i.q, 1, 0:1], rs[:, i.q, 1:2],
                   ALU.subtract, ALU.mult).then_inc(s_rn, 1)

            def router_logits(i):
                dve.wait_ge(s_rl, i.t + 1)
                TT(logits[:, span(i.t), 0:E1].rearrange("p a e -> p (a e)"), ps[7][:, D:D + E1],
                   gate_b[:, E0:E0 + E1], ALU.add).then_inc(s_rle, 1)

            def attend1(i):
                chain.step(c1, 1, i.t)
                if i.plus(2).exists(0, NT):
                    normalise1(i.plus(2))
                if i.plus(-2).exists(0, NT):
                    router_normalise(i.plus(-2))
                if i.plus(1).exists(0, NT):
                    shift1(i.plus(1))
                if i.exists(0, NT):
                    weights1(i)
                    chain.stepped()
                if i.plus(4).exists(0, NT):
                    combine0(i.plus(4))
                if i.plus(-1).exists(0, NT):
                    residual1(i.plus(-1))
                    router_statistics(i.plus(-1))
                if i.plus(-3).exists(0, NT):
                    router_logits(i.plus(-3))

            combine0(Tile(0, 0))
            normalise1(Tile(0, 0))
            combine0(Tile(0, 1))
            normalise1(Tile(0, 1))
            combine0(Tile(1, 0))
            shift1(Tile(0, 0))
            combine0(Tile(1, 1))
            over_tiles(dve, 0, NT + 4, attend1, lead=4, tail=8)

            dve.wait_ge(s_rle, NT)
            chain.n = c1 + NT
            lg = logits[:, :, 0:E1]
            chain(dve.tensor_reduce(wsum[:, 0, :], lg, AX.X, ALU.max))
            chain.wait()
            TT(lg, lg, over(wsum[:, 0, :], E1), ALU.subtract).then_inc(s_pmax, 1)
            chain(dve.memset(logits[:, :, E1:EC1], -1.0))
            dve.wait_ge(s_pexp, 1)
            chain(dve.tensor_reduce(wsum[:, 0, :], lg, AX.X, ALU.add))
            chain.wait()
            chain(dve.reciprocal(wsum[:, 1, :], wsum[:, 0, :]))
            chain.wait()
            chain(TT(lg, lg, over(wsum[:, 1, :], E1), ALU.mult))
            chain.wait()
            choose(EC1)
            chain(dve.tensor_reduce(wsum[:, 0, :], top[:, :, 0:K1], AX.X, ALU.add))
            chain.wait()
            chain(dve.reciprocal(wsum[:, 1, :], wsum[:, 0, :]))
            chain.wait()
            chain(TT(wgt[1][:, :, :], top[:, :, 0:K1], over(wsum[:, 1, :], K1), ALU.mult))
            ranks_to_slots(1, EC1, E1, K1, T1)

            def hidden1(i, c):
                u = 2 * i.t + c
                dve.wait_ge(s_fsi, u + 1)
                wait(dve, s_fHT, u - 1)
                TT(hh[:, c, :], silu[:, c, :], ps[2 + 2 * c][:, 0:FC1], ALU.mult).then_inc(s_fh, 1)

            def take1(i, kind):
                dve.wait_ge(s_fO, 2 * i.t + 2)
                o = ps[6 + i.q][:, 0:D]
                if kind == "routed":
                    j = i.plus(-SHARED_A)
                    wait(dve, s_fst[i.q], 16 * j.m)
                    CP(y1[:, i.q, :], o).then_inc(s_fy, 1)
                else:
                    j = i if kind == "first" else i.plus(-T1)
                    TT(row1(j), row1(j), o, ALU.add).then_inc(s_fy, 1)

            def finish(i):
                dve.wait_ge(s_g1[i.q], 16 * K1 * (i.m + 1))
                for k in range(K1):
                    w = wgt[1][:, span(i.t), k:k + 1].rearrange("p a k -> p (a k)")
                    g = gat1[:, span(i.t), k, :].rearrange("p a d -> p (a d)")
                    STT(out=row1(i), in0=g, scalar=w, in1=row1(i), op0=ALU.mult, op1=ALU.add)                        .then_inc(s_half if k == 0 else s_fin, 1)
                    if k == 0:
                        dve.wait_ge(s_half, i.t + 1)

            def expert1(i, before):
                hidden1(i, 0)
                hidden1(i, 1)
                if i.plus(-1).exists(0, N1):
                    take1(i.plus(-1), before)

            def segment(lo, hi, kind, before):
                def body(i):
                    first = isinstance(i.t, int) and i.t == lo
                    expert1(i, before if first else kind)
                    if kind == "last" and not first:
                        finish(i.plus(-MID1 - 1))
                over_tiles(dve, lo, hi, body)

            segment(0, SHARED_A, "first", None)
            segment(SHARED_A, MID1, "routed", "first")
            dve.wait_ge(s_fy, SHARED_A)
            segment(MID1, N1, "last", "routed")
            take1(Tile(N1 // 2 - 1, 1), "last")
            dve.wait_ge(s_fy, N1)
            finish(Tile((SHARED_B - 1) // 2, (SHARED_B - 1) % 2))
            over_tiles(dve, SHARED_B, NT, finish)

        @block.tensor
        def _(pe):
            MM = pe.matmul

            def transposes(dst, rows, n):
                for k in range(n):
                    ins = pe.transpose(dst[:, k * P:k * P + P], rows[:, k * P:k * P + P], ident[:, :])
                return ins

            pe.wait_ge(s_w0, 16 * 6)
            for m in range(2):
                for k in range(FK):
                    ins = MM(ps[0][:, m * P:m * P + P], w0k[:, k, m * P:m * P + P], ctxT[:, k, :],
                             start=(k == 0), stop=(k == FK - 1))
            ins.then_inc(s_p0, 1)
            pe.wait_ge(s_p0e, 1)
            pe.wait_ge(s_bqb, 1)
            for k in range(3):
                for m in range(2):
                    w = w0q[:, m, k * P:k * P + P] if k < FK else bqb[:, m, :]
                    ins = MM(ps[1 + k][:, m * 256:m * 256 + 256], w,
                             kblk0[:, m, :, :].rearrange("p c n -> p (c n)"), start=True, stop=True)
            ins.then_inc(s_p0, 1)
            pe.wait_ge(s_crep, 1)
            for n in range(4):
                for k in range(FK):
                    c = crep[:, k, n // 2].rearrange("p j c s -> p (j c s)")
                    ins = MM(ps[4 + n // 2][:, 256 * (n % 2):256 * (n % 2) + 256],
                             c[:, P * (n % 2):P * (n % 2) + P], w0v[:, k, :],
                             start=(k == 0), stop=(k == FK - 1))
            ins.then_inc(s_p0, 1)

            def rows_t0(i):
                pe.wait_ge(s_xn, i.t + 1)
                wait(pe, s_xte, i.t - 1)
                transposes(ps[i.q], xn_a[:, i.q, :], 4).then_inc(s_xt, 1)

            def scores0(i):
                pe.wait_ge(s_xte, i.t + 1)
                wait(pe, s_scb, i.t - 1)
                for j in range(2):
                    for k in range(FK):
                        tab = tabA0[:, k].rearrange("p b j c s -> p b (j c s)")[
                            :, span(i.m // 2), P * i.q + 64 * j:P * i.q + 64 * j + 64]
                        ins = MM(ps[2 + i.q][:, 64 * j:64 * j + 64],
                                 xT_a[:, i.q, (2 * j + k) * P:(2 * j + k) * P + P],
                                 tab.rearrange("p a n -> p (a n)"), start=(k == 0), stop=(k == FK - 1))
                ins.then_inc(s_sc, 1)

            def weights_t0(i):
                pe.wait_ge(s_at, i.t + 1)
                wait(pe, s_atte, i.t)
                transposes(ps[4], sc0[:, i.q, :], 1).then_inc(s_att, 1)

            def values0(i):
                pe.wait_ge(s_atte, i.t + 1)
                wait(pe, s_aoe, i.t - 1)
                tab = tabV0.rearrange("p b q j d -> p b q (j d)")[:, span(i.m // 2), i.q, :]
                MM(ps[5 + i.q][:, :], aT0[:, i.q, :], tab.rearrange("p a n -> p (a n)"),
                   start=True, stop=True).then_inc(s_ao, 1)

            pe.wait_ge(s_const, 7)
            pe.wait_ge(s_p0e, 3)
            rows_t0(Tile(0, 0))
            scores0(Tile(0, 0))

            def attend0(i):
                if i.plus(1).exists(0, NPAIR):
                    rows_t0(i.plus(1))
                    scores0(i.plus(1))
                weights_t0(i)
                values0(i)

            over_tiles(pe, 0, NPAIR, attend0)

            def router_rows(l, w, columns):
                def rows(i):
                    pe.wait_ge(s_gn, l * NPAIR + i.t + 1)
                    wait(pe, s_gte, l * NPAIR + i.t - 1)
                    transposes(ps[i.q], xn_r[:, i.q, :], 4).then_inc(s_gt, 1)

                def logits_of(i):
                    pe.wait_ge(s_gte, l * NPAIR + i.t + 1)
                    wait(pe, s_gle, l * NPAIR + i.t - 1)
                    for j in range(2):
                        for k in range(FK):
                            n = 2 * j + k
                            ins = MM(ps[2 + i.q][:, columns * j:columns * j + columns],
                                     gx[:, i.q, n * P:n * P + P], w[:, k, :], start=(k == 0), stop=(k == FK - 1))
                    ins.then_inc(s_gl, 1)

                def body(i):
                    if i.plus(1).exists(0, NPAIR):
                        rows(i.plus(1))
                    logits_of(i)

                rows(Tile(0, 0))
                over_tiles(pe, 0, NPAIR, body)

            def ranks(l, columns, tiles):
                mask = r_mask.bitcast(BF16)
                pe.wait_ge(s_mask, l + 1)
                MM(ps[4][:, 0:NT * columns], tri_b[:, :], mask[:, 0:NT * columns],
                   start=True, stop=False, skip_group_check=True)
                for n in range(1, NT):
                    MM(ps[4][:, n * columns:NT * columns], ones_b[:, :], mask[:, 0:(NT - n) * columns],
                       start=False, stop=(n == NT - 1), skip_group_check=True)
                for n in range(NT):
                    ins = MM(ps[5][:, 0:columns], ones_b[:, :], mask[:, n * columns:(n + 1) * columns],
                             start=(n == 0), stop=(n == NT - 1))
                ins.then_inc(s_rank, 1)

            def expert_row(l, tiles):
                pe.wait_ge(s_te, l + 1)
                MM(ps[6][0:1, 0:tiles], te_col[0:tiles, 0:1], ident[0:tiles, 0:tiles],
                   start=True, stop=True).then_inc(s_ter, 1)

            def slot_tokens(l, chosen, tiles):
                for c in range(chosen * NT):
                    pe.wait_ge(s_hot, l * K0 * NT + c + 1)
                    ins = MM(ps[7][:, 0:tiles], hot_lo[l][c // NT][:, c % NT, :], hot_hi[l][:, c, :],
                             start=(c == 0), stop=(c == chosen * NT - 1))
                ins.then_inc(s_inv, 1)

            pe.wait_ge(s_rt, 16 * 3)
            router_rows(0, gateT[:, :, 0:E0], E0)
            ranks(0, E0, T0)

            pe.wait_ge(s_gte, NPAIR)
            pe.wait_ge(s_gle, NPAIR)
            pe.wait_ge(s_wkq, 16 * 2)

            def blocks(base):
                for hp in range(HP1):
                    g = hp // 4
                    if hp % 4 == 0 and base:
                        pe.wait_ge(s_l1e, 10)
                    for k in range(FK):
                        ins = MM(ps[g][:, (hp % 4) * P:(hp % 4) * P + P], att_in_v[:, k, hp * P:hp * P + P],
                                 ctxT[:, k, :], start=(k == 0), stop=(k == FK - 1))
                    if hp % 4 == 3:
                        ins.then_inc(s_l1p, 1)

            blocks(0)
            for n in range(8):
                k, g = n // 4, n % 4
                pe.wait_ge(s_l1e, max(2, n + 1))
                for h in range(2):
                    hp = 2 * g + h
                    ins = MM(ps[2 + n % 2][:, 256 * h:256 * h + 256], att_w_v[:, hp, k * P:k * P + P],
                             blk1_v[:, hp].rearrange("p b c s -> p (b c s)"), start=True, stop=True)
                ins.then_inc(s_l1p, 1)
            expert_row(0, T0)
            pe.wait_ge(s_wv, 16)
            blocks(10)
            pe.wait_ge(s_wo, 16)
            for n in range(8):
                b, g = n // 4, n % 4
                pe.wait_ge(s_l1e, max(12, n + 11))
                for h in range(2):
                    hp = 2 * g + h
                    ins = MM(ps[2 + n % 2][:, 256 * h:256 * h + 256],
                             blk1_v[:, hp, b].rearrange("p c s -> p (c s)"), att_w_v[:, hp, :],
                             start=True, stop=True)
                ins.then_inc(s_l1p, 1)
            pe.wait_ge(s_l1e, 20)
            slot_tokens(0, K0, T0)

            pe.wait_ge(s_info, 1)

            def rows_e0(i):
                pe.wait_ge(s_ex[i.q], 16 * (i.m + 1))
                wait(pe, s_eXe, i.t - 1)
                transposes(ps[i.p], xr0[:, i.q, :], FK).then_inc(s_eX, 1)

            slot_at = Registers(lambda t: ring_slot(pe, t))

            def hidden0(i):
                r = slot_at[i]
                pe.wait_ge(s_eXe, i.t + 1)
                pe.wait_ge(s_ew[i.p], 16 * (i.half + 1))
                wait(pe, s_ehb, i.t - 1)
                for k in range(FK):
                    w = ring[:, span(r), k * 2 * F0:(k + 1) * 2 * F0].rearrange("p a n -> p (a n)")
                    ins = MM(ps[2 + i.p][:, :], xT0[:, i.p, k, :], w, start=(k == 0), stop=(k == FK - 1))
                ins.then_inc(s_eH, 1)

            def hidden_t0(i):
                pe.wait_ge(s_ehs, i.t + 1)
                wait(pe, s_eHTe, i.t)
                transposes(ps[4], hs0[:, i.p, :], F0 // P).then_inc(s_eHT, 1)

            def out0(i):
                r = slot_at[i]
                pe.wait_ge(s_eHTe, i.t + 1)
                wait(pe, s_ey, i.t - 1)
                for k in range(F0 // P):
                    lo = FK * 2 * F0 + k * D
                    w = ring[:, span(r), lo:lo + D].rearrange("p a n -> p (a n)")
                    ins = MM(ps[5 + i.p][:, 0:D], hT0[:, i.p, k, :], w, start=(k == 0), stop=(k == F0 // P - 1))
                ins.then_inc(s_eO, 1)

            def expert0(i):
                slot_at.begin(i)
                for j in (i.plus(-2), i):
                    if j.exists(0, T0):
                        slot_at.load(j)
                if i.plus(-2).exists(0, T0):
                    hidden_t0(i.plus(-2))
                if i.plus(1).exists(0, T0):
                    rows_e0(i.plus(1))
                if i.exists(0, T0):
                    hidden0(i)
                if i.plus(-2).exists(0, T0):
                    out0(i.plus(-2))

            rows_e0(Tile(0, 0, 4))
            over_tiles(pe, 0, T0 + 2, expert0, lead=4, tail=4, u=4)

            def rows_t1(i):
                pe.wait_ge(s_1n, i.t + 1)
                wait(pe, s_1te, i.t)
                transposes(ps[0], xn1[:, i.q, :], FK).then_inc(s_1t, 1)

            def scores1(i):
                pe.wait_ge(s_1te, i.t + 1)
                wait(pe, s_1m, i.t - 1)
                b = i.m // 4
                for g in range(2):
                    for k in range(FK):
                        tab = tabA[:, span(b), k, 512 * g:512 * g + 512].rearrange("p a n -> p (a n)")
                        ins = MM(ps[1 + 2 * i.q + g][:, :], xT1[:, i.q, k, :], tab,
                                 start=(k == 0), stop=(k == FK - 1))
                ins.then_inc(s_1s, 1)

            def weights_t1(i):
                pe.wait_ge(s_1w, i.t + 1)
                wait(pe, s_1wte, i.t)
                transposes(ps[5], sc1[:, i.q, 0:512], 4)
                transposes(ps[6], sc1[:, i.q, 512:1024], 4).then_inc(s_1wt, 1)

            def values1(i):
                pe.wait_ge(s_1wte, i.t + 1)
                wait(pe, s_1r, i.t)
                b = i.m // 4
                for hp in range(HP1):
                    tab = tabV[:, span(b), hp, :].rearrange("p a n -> p (a n)")
                    ins = MM(ps[7][:, 0:D], aT1[:, hp, :], tab, start=(hp == 0), stop=(hp == HP1 - 1))
                ins.then_inc(s_1o, 1)

            def router_rows1(i):
                pe.wait_ge(s_rn, i.t + 1)
                wait(pe, s_rte, i.t)
                pe.wait_ge(s_1te, at_most(i.t + 4, NT))
                transposes(ps[0][:, D:2 * D], xn_f[:, i.q, :], FK).then_inc(s_rtr, 1)

            def router_logits1(i):
                pe.wait_ge(s_rte, i.t + 1)
                wait(pe, s_rle, i.t)
                pe.wait_ge(s_1r, at_most(i.t + 2, NT))
                for k in range(FK):
                    ins = MM(ps[7][:, D:D + E1], gx[:, i.q, k * P:k * P + P], gateT[:, k, E0:E0 + E1],
                             start=(k == 0), stop=(k == FK - 1))
                ins.then_inc(s_rl, 1)

            def attend1(i):
                if i.plus(1).exists(0, NT):
                    scores1(i.plus(1))
                if i.plus(-2).exists(0, NT):
                    router_rows1(i.plus(-2))
                if i.plus(2).exists(0, NT):
                    rows_t1(i.plus(2))
                if i.plus(-3).exists(0, NT):
                    router_logits1(i.plus(-3))
                if i.plus(-1).exists(0, NT):
                    values1(i.plus(-1))
                if i.exists(0, NT):
                    weights_t1(i)

            rows_t1(Tile(0, 0))
            attend1(Tile(-1, 1))
            over_tiles(pe, 0, NT + 4, attend1, lead=4, tail=6)

            ranks(1, EC1, T1)
            expert_row(1, T1)
            slot_tokens(1, K1, T1)

            pe.wait_ge(s_info, 2)
            pe.wait_ge(s_w1, 16 * EARLY)
            pe.wait_ge(s_w1b, 16 * (8 - EARLY))

            def rows_e1(i, kind):
                if kind == "routed":
                    pe.wait_ge(s_fr[i.q], 16 * (i.plus(-SHARED_A).m + 1))
                else:
                    pe.wait_ge(s_fx[i.q], 16 * ((i if kind == "first" else i.plus(-T1)).m + 1))
                wait(pe, s_fXe, i.t)
                transposes(ps[0], xr1[:, i.q, :], FK).then_inc(s_fX, 1)

            place = Registers(lambda t: pe.value_load(info[1][0:1, 0, span(t)], min_val=0, max_val=E1))

            def gate_up(i, c):
                e = place[i]
                u = 2 * i.t + c
                if c == 0:
                    pe.wait_ge(s_fXe, i.t + 1)
                wait(pe, s_fh, u - 1)
                for g in range(2):
                    for k in range(FK):
                        lo = ((k * NC1 + c) * 2 + g) * FC1
                        w = w1s[:, span(e), lo:lo + FC1].rearrange("p a n -> p (a n)")
                        ins = MM(ps[1 + 2 * c + g][:, 0:FC1], xTe[:, i.q, k, :], w,
                                 start=(k == 0), stop=(k == FK - 1))
                ins.then_inc(s_fG, 1)

            def hidden_t1(i, c):
                u = 2 * i.t + c
                pe.wait_ge(s_fh, u + 1)
                wait(pe, s_fHTe, u)
                for n, (lo, width) in enumerate(SUB1):
                    ins = pe.transpose(ps[5][0:width, n * P:n * P + P], hh[:, c, lo:lo + width], ident[:, :])
                ins.then_inc(s_fHT, 1)

            def out1(i, c):
                e = place[i]
                u = 2 * i.t + c
                pe.wait_ge(s_fHTe, u + 1)
                if c == 0:
                    wait(pe, s_fy, i.t - 1)
                for n, (_, width) in enumerate(SUB1):
                    lo = GU1 + (c * 3 + n) * D
                    w = w1s[0:width, span(e), lo:lo + D].rearrange("p a n -> p (a n)")
                    ins = MM(ps[6 + i.q][:, 0:D], hTe[0:width, c, n, :], w,
                             start=(c == 0 and n == 0), stop=(c == 1 and n == 2))
                ins.then_inc(s_fO, 1)

            def expert1(i, kind_next):
                last = i.plus(-1)
                place.begin(i)
                for j in (last, i):
                    if j.exists(0, N1):
                        place.load(j)
                if i.exists(0, N1):
                    gate_up(i, 0)
                if last.exists(0, N1):
                    out1(last, 0)
                    hidden_t1(last, 1)
                if i.plus(1).exists(0, N1):
                    rows_e1(i.plus(1), kind_next)
                if i.exists(0, N1):
                    gate_up(i, 1)
                if last.exists(0, N1):
                    out1(last, 1)
                if i.exists(0, N1):
                    hidden_t1(i, 0)

            def segment(lo, hi, kind, after):
                def body(i):
                    last = isinstance(i.t, int) and i.t == hi - 1
                    expert1(i, after if last else kind)
                over_tiles(pe, lo, hi, body)

            rows_e1(Tile(0, 0), "first")
            segment(0, SHARED_A, "first", "routed")
            segment(SHARED_A, MID1, "routed", "last")
            segment(MID1, N1, "last", None)
            expert1(Tile(N1 // 2, 0), None)


_NAMES = ["x", "mask", "ctxT", "Wk0T", "Wq0", "Wv0T", "bkq", "bv", "gateT", "gate_b", "norm_scale",
          "wk1", "wq1T", "wv1", "wo1", "w_e0", "w_e1"]


def arrange(i):
    f = {k: np.asarray(v) for k, v in i.items()}

    def by_part(w):
        return w.reshape(-1, P, w.shape[-1]).transpose(1, 0, 2)

    r = {"x": f["x"], "mask": f["mask_Bx1xSxS2_ff0"][:, 0]}
    r["ctxT"] = by_part(f["ctx_1024"].reshape(B * S2, D).T)
    r["Wk0T"], r["Wv0T"] = by_part(f["L0_xattn_Wk"].T), by_part(f["L0_xattn_Wv"].T)
    r["Wq0"] = by_part(f["L0_xattn_Wq"])
    r["bkq"] = np.stack([f["L0_xattn_bk"].reshape(2, P), f["L0_xattn_bq"].reshape(2, P)]).transpose(2, 0, 1)
    r["bv"] = f["L0_xattn_bv"][None]
    r["gateT"] = by_part(np.concatenate([f["L0_ffn_gate_w"], f["L1_ffn_wr"]]).T)
    r["gate_b"] = np.concatenate([f["L0_ffn_gate_b"], f["L1_ffn_rb"]])[None]
    r["norm_scale"] = f["L0_ffn_norm_scale"][None]
    r["wk1"], r["wv1"] = (by_part(f[k].reshape(D, H1 * DH)) for k in ("L1_xattn_wk", "L1_xattn_wv"))
    r["wq1T"] = by_part(f["L1_xattn_wq"].reshape(D, H1 * DH).T)
    r["wo1"] = by_part(f["L1_xattn_wo"].reshape(H1 * DH, D))
    w1 = f["L0_ffn_w1"].reshape(E0, F0, 2, FK, P).transpose(0, 4, 3, 2, 1).reshape(E0, P, FK * 2 * F0)
    w2 = f["L0_ffn_w2"].reshape(E0, D, F0 // P, P).transpose(0, 3, 2, 1).reshape(E0, P, (F0 // P) * D)
    b1 = f["L0_ffn_b1"].reshape(E0, F0, 2).transpose(0, 2, 1).reshape(E0, 2 * F0)
    b = np.concatenate([b1, f["L0_ffn_b2"]], axis=1)
    r["w_e0"] = np.concatenate([w1, w2, np.broadcast_to(b[:, None], (E0, P, B0))], axis=2)
    g, u, d = (np.concatenate([f["L1_ffn_s" + k][None], f["L1_ffn_r" + k]]) for k in "gud")
    gu = np.stack([g, u]).reshape(2, 8, NC1, FC1, FK, P).transpose(1, 5, 4, 2, 0, 3).reshape(8, P, GU1)
    d = d.reshape(8, D, NC1, FC1).transpose(0, 2, 3, 1)
    dd = np.zeros((8, NC1, 3 * P, D), np.float32)
    dd[:, :, :FC1] = d
    dd = dd.reshape(8, NC1, 3, P, D).transpose(0, 3, 1, 2, 4).reshape(8, P, NC1 * 3 * D)
    r["w_e1"] = np.concatenate([gu, dd], axis=2)
    return {k: np.ascontiguousarray(r[k]) for k in _NAMES}


def kernel(**inputs):
    import concourse.bacc as _bacc
    from concourse.bass_utils import run_bass_kernel_spmd as _run

    nc = _bacc.Bacc("TRN2", target_bir_lowering=False, num_devices=1)
    arrays = arrange(inputs)
    aps = {k: nc.dram_tensor("in_" + k, v.shape, F32, kind="ExternalInput").ap() for k, v in arrays.items()}
    out = nc.dram_tensor("out", (B, S, D), F32, kind="ExternalOutput").ap()
    build(nc, aps, out)
    r = _run(nc, [{"in_" + k: v for k, v in arrays.items()}], core_ids=[0])
    return r.results[0]["out"]
```

```python
from contextlib import ExitStack

import numpy as np

import concourse.bass as bass
from concourse import mybir

F32 = mybir.dt.float32
BF16 = mybir.dt.bfloat16
F16 = mybir.dt.float16
I32 = mybir.dt.int32
U32 = mybir.dt.uint32
ALU = mybir.AluOpType
ACT = mybir.ActivationFunctionType
AX = mybir.AxisListType

P = 128
B, S, D, S2 = 2, 1024, 256, 64
FK = D // P
NT = B * S // P
NPAIR = NT // 2
J = 4
C0, KEYS0 = 4, S2 // J
DH = 64
H1, HP1 = 16, 8
EPS = 1e-5
E0, K0, F0 = 32, 4, 256
E1, K1, F1 = 7, 2, 704
EC1 = 8
LIMIT, ALPHA = 7.0, 1.702
NC1 = 2
FC1 = F1 // NC1
SUB1 = [(0, 128), (128, 128), (256, FC1 - 256)]
T0 = (NT * P * K0 + 127 * E0) // P
T0 += T0 % 2
T1 = (NT * P * K1 + 127 * E1) // P
T1 += T1 % 2
R0 = 8
W0 = FK * 2 * F0 + (F0 // P) * D
GU1 = FK * NC1 * 2 * FC1
W1 = GU1 + NC1 * 3 * D
B0 = 2 * F0 + D
EARLY = 6
SHARED_SLOTS = 2
LAG0, LAG1 = 8, 4
LAGR = 5
AHEAD = 2
SHARED_A, SHARED_B = 10, 6
N1 = SHARED_A + T1 + SHARED_B
MID1 = SHARED_A + T1


def wait(eng, sem, n):
    if not (isinstance(n, int) and n <= 0):
        eng.wait_ge(sem, n)


class Tile:

    def __init__(self, m, q, u=2, place=None):
        self.m, self.q, self.u, self.t = m, q, u, u * m + q
        self.place = q if place is None else place
        self.p = q % 2
        self.half = m * (u // 2) + q // 2
        self.pair = q // 2 % 2

    def plus(self, d):
        return Tile(self.m + (self.q + d) // self.u, (self.q + d) % self.u, self.u, self.place + d)

    def exists(self, lo, hi):
        return not isinstance(self.t, int) or lo <= self.t < hi


def over_tiles(eng, lo, hi, body, lead=2, tail=2, u=2):
    a, z = -(-(lo + lead) // u) * u, (hi - tail) // u * u
    for t in range(lo, min(a, hi)):
        body(Tile(t // u, t % u, u))
    if z > a:
        with eng.Fori(a // u, z // u) as m:
            for q in range(u):
                body(Tile(m, q, u))
    for t in range(max(a, z), hi):
        body(Tile(t // u, t % u, u))


def at_most(t, n):
    return min(t, n) if isinstance(t, int) else t


def alone(eng, sem):
    eng.sem_inc(sem, 1)


def span(i, n=1):
    return slice(i, i + n) if isinstance(i, int) else bass.ds(i, n)


class Registers:

    def __init__(self, load_value):
        self.load_value, self.held = load_value, {}

    def begin(self, i):
        if i.q == 0 or isinstance(i.t, int):
            self.held = {}
            self.m = i.m

    def key(self, i):
        return i.t if isinstance(i.t, int) else i.place

    def load(self, i):
        if self.key(i) not in self.held:
            self.held[self.key(i)] = self.load_value(i.t)

    def __getitem__(self, i):
        return self.held[self.key(i)]


class Chain:

    def __init__(self, eng, sem):
        self.eng, self.sem, self.n, self.base = eng, sem, 0, 0

    def __call__(self, ins):
        ins.then_inc(self.sem, 1)
        self.n = self.n + 1

    def wait(self):
        self.eng.wait_ge(self.sem, self.n)

    def step(self, base, per, t):
        self.n = base + per * t
        self.base, self.per, self.now = base, per, t

    def stepped(self):
        d = self.n - (self.base + self.per * self.now)
        assert not isinstance(d, int) or d == self.per, d


def build(nc, a, out):
    ctx = ExitStack()
    with ctx:
        def sb(name, shape, dt=F32):
            return ctx.enter_context(nc.sbuf_tensor(name, shape, dt))

        def sem(name):
            return ctx.enter_context(nc.semaphore(name))

        xres = sb("xres", [P, NT, D])
        normed = sb("normed", [P, NT, D])
        big = sb("big", [P, 8 * W1])
        w1s = big[:, :].rearrange("p (e w) -> p e w", e=8)
        ring = big[:, 0:R0 * (W0 + B0)].rearrange("p (r w) -> p r w", r=R0)
        o = (R0 - SHARED_SLOTS) * (W0 + B0)
        att_in = big[:, o:o + FK * H1 * DH]
        att_in_v = att_in.rearrange("p (k n) -> p k n", k=FK)
        o += FK * H1 * DH
        att_w = big[:, o:o + HP1 * D]
        att_w_v = att_w.rearrange("p (h n) -> p h n", h=HP1)
        o += HP1 * D
        blk1 = big[:, o:o + HP1 * B * 2 * S2]
        blk1_v = blk1.rearrange("p (h b c s) -> p h b c s", h=HP1, b=B, c=2)
        o += HP1 * B * 2 * S2
        tabA0 = big[:, o:o + 3 * 512].rearrange("p (k b j c s) -> p k b j c s", k=3, b=B, j=J, c=C0)
        o += 3 * 512
        tabV0_ = big[:, o:o + B * 2 * 512]
        tabV0 = tabV0_.rearrange("p (b q j d) -> p b q j d", b=B, q=2, j=2)
        o += B * 2 * 512
        ab = big[:, o:o + 3072]
        o = 8 * W1 - B * FK * H1 * S2 - B * HP1 * D
        assert (R0 - SHARED_SLOTS) * (W0 + B0) + 3 * 2048 + 1536 + 2048 + 3072 <= o
        assert SHARED_SLOTS * (W0 + B0) <= 3 * 2048
        tabA = big[:, o:o + B * FK * H1 * S2].rearrange("p (b k n) -> p b k n", b=B, k=FK)
        o += B * FK * H1 * S2
        tabV = big[:, o:o + B * HP1 * D].rearrange("p (b h n) -> p b h n", b=B, h=HP1)
        o += B * HP1 * D
        assert o == 8 * W1

        ident = sb("ident", [P, P])
        ones_b = sb("ones_b", [P, P], BF16)
        tri_b = sb("tri_b", [P, P], BF16)
        mhalf = sb("mhalf", [P, 2])
        eps_t = sb("eps_t", [P, 2])
        stats = sb("stats", [P, 2, 6])
        mv = sb("mv", [P, 2, 2, 2])
        rs = sb("rs", [P, 2, 2])
        rms = sb("rms", [P, 2, 2])
        rtmp = sb("rtmp", [P, 1, 2])
        stats_r = sb("stats_r", [P, 2, 6])
        mv_r = sb("mv_r", [P, 2, 2, 2])
        rs_r = sb("rs_r", [P, 2, 2])
        WORK = 5376
        work = sb("work", [P, WORK])

        def carve(parts):
            at, got = 0, []
            for n in parts:
                got.append(work[:, at:at + n])
                at += n
            assert at <= WORK, at
            return got

        (w0q_, w0k_, w0v_, kblk0_, crep_, bqb_, bvb) = carve([512, 512, 512, 512, 1024, 256, 256])
        w0q = w0q_.rearrange("p (k n) -> p k n", k=2)
        w0k = w0k_.rearrange("p (k n) -> p k n", k=2)
        w0v = w0v_.rearrange("p (k n) -> p k n", k=2)
        kblk0 = kblk0_.rearrange("p (m c n) -> p m c n", m=2, c=2)
        crep = crep_.rearrange("p (k b j c s) -> p k b j c s", k=FK, b=B, j=J, c=C0)
        bqb = bqb_.rearrange("p (m n) -> p m n", m=2)
        ctxT = sb("ctxT", [P, FK, B * S2])
        b0c = sb("b0c", [P, 2, 2])

        xn_a = ab[:, 0:1024].rearrange("p (q n) -> p q n", q=2)
        xT_a = ab[:, 1024:2048].rearrange("p (q n) -> p q n", q=2)
        sc0 = ab[:, 2048:2304].rearrange("p (q n) -> p q n", q=2)
        aT0 = ab[:, 2304:2560].rearrange("p (q n) -> p q n", q=2)
        blkmask = ab[:, 2560:2816]
        gx = sb("gx", [P, 2, 512])
        scale_b = ab[:, 2816:3072]
        gateT = sb("gateT", [P, FK, E0 + E1])
        gate_b = sb("gate_b", [P, E0 + E1])
        sm0 = sb("sm0", [P, 4, 16])

        logits = sb("logits", [P, NT, E0])
        top = sb("top", [P, NT, 8])
        topi = sb("topi", [P, NT, 8], U32)
        wexp = sb("wexp", [P, NT, K0])
        wsum = sb("wsum", [P, 2, NT])
        wgt = [sb(f"wgt{l}", [P, NT, k]) for l, k in ((0, K0), (1, K1))]
        slot_i = [sb(f"slot_i{l}", [P, k, NT], I32) for l, k in ((0, K0), (1, K1))]
        info = [sb(f"info{l}", [1, 3, n], I32) for l, n in ((0, T0), (1, N1))]
        pidx = sb("pidx", [P, 1])
        iota_e = sb("iota_e", [P, E0])
        iota_p = sb("iota_p", [P, P])
        token_id = sb("token_id", [P, NT])

        (r_topf, r_one, r_mask, r_slot, r_tmp, r_small) = carve([128, 1024, 256, 512, 512, 1024])
        xn_r = work[:, 4320:5344].rearrange("p (q n) -> p q n", q=2)

        def routing(topf_, one_, mask_, slot_, tmp_, small):
            def at(lo, n):
                return small[:, lo:lo + n]
            return dict(
                topf=topf_.rearrange("p (t k) -> p t k", k=8), one=one_.bitcast(BF16),
                mask=mask_.bitcast(BF16), slot=slot_, tmp=tmp_, cnt_i=at(0, 32).bitcast(I32),
                tiles_f=at(32, 32), ends_f=at(64, 32), base_f=at(96, 32), ones_f=at(128, 32),
                cmp_f=at(160, 32), te_col=at(192, 2), te_row=at(194, 96)[0:1, :],
                fl_row=at(290, 96)[0:1, :], rk_row=at(386, 96)[0:1, :], one_row=at(482, 96)[0:1, :],
                slots_f=at(578, 64).rearrange("p (k t) -> p k t", t=NT), slot_hi=at(642, 64),
                slot_lo=at(706, 64), slot_sh=at(770, 64).bitcast(I32))

        n1 = NT * EC1
        r1 = gx[:, :, :].rearrange("p q n -> p (q n)")
        at1 = [128, K1 * n1 // 2, n1 // 2, n1, n1]
        r1_parts = [r1[:, sum(at1[:n]):sum(at1[:n + 1])] for n in range(5)]
        R = [routing(r_topf, r_one, r_mask, r_slot, r_tmp, r_small),
             routing(*r1_parts, work[:, 4352:4352 + 1024])]
        token_col = sb("token_col", [P, 4], I32)
        slot_token = [sb(f"slot_token{l}", [P, n], I32) for l, n in ((0, T0), (1, T1))]
        o = 2 * (W0 + B0)
        hot_hi = [big[:, o:o + K0 * NT * T0 // 2].bitcast(F16).rearrange("p (c n) -> p c n", n=T0)]
        o += K0 * NT * T0 // 2
        hot_lo = [[v.bitcast(F16).rearrange("p (c n) -> p c n", n=P)
                   for v in [big[:, o + k * NT * P // 2:o + (k + 1) * NT * P // 2] for k in range(K0)]]]
        assert o + K0 * NT * P // 2 <= (R0 - SHARED_SLOTS) * (W0 + B0)

        (xr0_, xT0_, hb_, hs_, hT_, y0_) = carve([1024, 512, 512, 512, 512, 1024])
        xr0 = xr0_.rearrange("p (q n) -> p q n", q=4)
        xT0 = xT0_.rearrange("p (q k n) -> p q k n", q=2, k=2)
        hs0 = hs_.rearrange("p (q n) -> p q n", q=2)
        hT0 = hT_.rearrange("p (q k n) -> p q k n", q=2, k=2)
        y0 = y0_.rearrange("p (q k n) -> p q k n", q=2, k=2)

        (xn1_, xT1_, s1_, aT1_, g1_, mk_) = carve([512, 512, 2048, 1024, 1024, 128])
        xn1 = xn1_.rearrange("p (q n) -> p q n", q=2)
        xT1 = xT1_.rearrange("p (q k n) -> p q k n", q=2, k=2)
        sc1 = s1_.rearrange("p (q n) -> p q n", q=2)
        aT1 = aT1_.rearrange("p (h n) -> p h n", h=HP1)
        msk = mk_.rearrange("p (q n) -> p q n", q=2)
        sm1 = sb("sm1", [P, 2, 3, H1])
        xn_f = gx[:, :, D:2 * D]

        (xr1_, xTe_, si_, hh_, hTe_, y1_) = carve([512, 512, 704, 704, 768, 512])
        xr1 = xr1_.rearrange("p (q n) -> p q n", q=2)
        xTe = xTe_.rearrange("p (q k n) -> p q k n", q=2, k=2)
        silu = si_.rearrange("p (q n) -> p q n", q=2)
        hh = hh_.rearrange("p (q n) -> p q n", q=2)
        hTe = hTe_.rearrange("p (q s n) -> p q s n", q=2, s=3)
        y1 = y1_.rearrange("p (q n) -> p q n", q=2)
        gat1 = big[:, W1:W1 + NT * K1 * D].rearrange("p (t k n) -> p t k n", t=NT, k=K1)
        gat_b = sb("gat_b", [P, 4 * D])
        gat0 = [g1_.rearrange("p (k n) -> p k n", k=K0), gat_b[:, :].rearrange("p (k n) -> p k n", k=K0)]

        hot_hi.append(work[:, 3744:3744 + K1 * NT * T1 // 2].bitcast(F16).rearrange("p (c n) -> p c n", n=T1))
        hot_lo.append([v.bitcast(F16).rearrange("p (c n) -> p c n", n=P)
                       for v in (gat_b[:, :], gx[:, :, :].rearrange("p q n -> p (q n)"))])

        xn_u = gat_b[:, :].rearrange("p (q n) -> p q n", q=2)
        glu, lin, sig = (v.rearrange("p (q n) -> p q n", q=2)
                         for v in (gat_b[:, 0:2 * F0], gat_b[:, 2 * F0:4 * F0], gx[:, 0, 0:2 * F0]))

        ps = [ctx.enter_context(nc.psum_tensor(f"ps{i}", [P, 512], F32)) for i in range(8)]

        n0, b1 = NT * E0, ps[0][:, D:2 * D]
        earlier = [ps[4][:, 0:n0], b1[:, 0:n1]]
        counts = [ps[5][:, 0:E0], b1[:, n1:n1 + EC1]]
        expert_of = [ps[6][0:1, 0:T0], b1[0:1, 0:T1]]
        token_of = [ps[7][:, 0:T0], b1[:, 0:T1]]

        xs = [nc.dram_tensor(f"rows_in{l}", (NT * P, D), F32, kind="Internal").ap() for l in range(2)]
        ys = [nc.dram_tensor(f"rows_out{l}", (n * P, D), F32, kind="Internal").ap() for l, n in ((0, T0), (1, T1))]

        s_x = sem("x_loaded")
        s_w0 = sem("layer0_attention_weights_loaded")
        s_rt = sem("router_weights_loaded")
        s_iota = sem("token_numbers_set")
        s_wkq = sem("layer1_wk_wq_loaded")
        s_wv = sem("layer1_wv_loaded")
        s_wo = sem("layer1_wo_loaded")
        s_const = sem("constants_set")
        s_pool = sem("pool_chain")
        s_dve = sem("dve_chain")
        s_act = sem("act_chain")
        s_blk0z = sem("layer0_blocks_zeroed")
        s_bn = sem("row_statistics")
        s_bqb = sem("query_bias_spread")
        s_crep = sem("context_columns_repeated")
        s_p0 = sem("prep0_products")
        s_p0e = sem("prep0_evacuated")
        s_var = sem("variances_ready")
        s_rstd = sem("rstd_ready")
        s_xn = sem("pair_normalised")
        s_xt = sem("pair_transposed")
        s_xte = sem("pair_transposed_copied")
        s_sc = sem("pair_scores")
        s_scb = sem("pair_scores_shifted")
        s_exp = sem("pair_exponentials")
        s_at = sem("pair_weights")
        s_att = sem("pair_weights_transposed")
        s_atte = sem("pair_weights_transposed_copied")
        s_ao = sem("pair_attended")
        s_aoe = sem("pair_residual_added")
        s_gbn = sem("router_row_statistics")
        s_gvar = sem("router_variances_ready")
        s_grstd = sem("router_rstd_ready")
        s_gn = sem("router_rows_normalised")
        s_un = sem("router_rows_unscaled")
        s_xl = sem("normalised_rows_added")
        s_nc = sem("normalised_rows_kept")
        s_gt = sem("router_rows_transposed")
        s_gte = sem("router_rows_transposed_copied")
        s_gl = sem("router_logits")
        s_gle = sem("router_logits_copied")
        s_rvar = sem("l1_router_variances")
        s_rbn = sem("l1_router_row_statistics")
        s_rrstd = sem("l1_router_rstd_ready")
        s_rn = sem("l1_router_rows_normalised")
        s_rk = sem("l1_router_rows_kept")
        s_rtr = sem("l1_router_rows_transposed")
        s_rte = sem("l1_router_rows_transposed_copied")
        s_rl = sem("l1_router_logits")
        s_rle = sem("l1_router_logits_copied")
        s_pmax = sem("router_logits_shifted")
        s_pexp = sem("router_exponentials")
        s_wd = sem("router_weight_differences")
        s_we = sem("router_weight_exponentials")
        s_mask = sem("assignment_masks")
        s_rank = sem("assignment_ranks")
        s_rread = sem("routing_bank_read")
        s_shared = sem("shared_places_set")
        s_te = sem("tile_expert_column")
        s_ter = sem("tile_expert_row")
        s_slot = sem("slots_ready")
        s_info = sem("tile_info_ready")
        s_rows = [sem("token_rows_stored0"), sem("token_rows_stored1")]
        s_hot = sem("slots_one_hot")
        s_inv = sem("slot_tokens_summed")
        s_fr = [sem("routed_rows_gathered_a"), sem("routed_rows_gathered_b")]
        s_col = sem("slot_tokens_in_place")
        s_tok = sem("slot_tokens_ready")
        s_l1p = sem("layer1_table_products")
        s_l1e = sem("layer1_table_products_copied")
        s_bz = sem("layer1_blocks_zeroed")
        s_ew = [sem("expert_weights_a"), sem("expert_weights_b")]
        s_ex = [sem(f"expert_rows_{q}") for q in range(4)]
        s_eX = sem("expert_rows_transposed")
        s_eXe = sem("expert_rows_transposed_copied")
        s_eH = sem("expert_hidden_products")
        s_ehb = sem("expert_hidden_biased")
        s_eglu = sem("expert_glu_ready")
        s_elin = sem("expert_linear_ready")
        s_egate = sem("expert_gated")
        s_esig = sem("expert_sigmoid_ready")
        s_ehs = sem("expert_hidden_ready")
        s_eHT = sem("expert_hidden_transposed")
        s_eHTe = sem("expert_hidden_transposed_copied")
        s_eO = sem("expert_out_products")
        s_ey = sem("expert_rows_out_ready")
        s_est = [sem("expert_rows_stored_a"), sem("expert_rows_stored_b")]
        s_gath = [sem("rows_gathered0_a"), sem("rows_gathered0_b")]
        s_comb4 = sem("rows_combined0")
        s_mk = [sem("mask_loaded_a"), sem("mask_loaded_b")]
        s_1n = sem("l1_tile_normalised")
        s_1t = sem("l1_tile_transposed")
        s_1te = sem("l1_tile_transposed_copied")
        s_1s = sem("l1_scores")
        s_1m = sem("l1_scores_masked")
        s_1b = sem("l1_scores_shifted")
        s_1x = sem("l1_exponentials")
        s_1w = sem("l1_weights")
        s_1wt = sem("l1_weights_transposed")
        s_1wte = sem("l1_weights_transposed_copied")
        s_1o = sem("l1_attended")
        s_1r = sem("l1_residual_added")
        s_w1 = sem("layer1_experts_loaded_a")
        s_w1b = sem("layer1_experts_loaded_b")
        s_fx = [sem("routed_rows_a"), sem("routed_rows_b")]
        s_fX = sem("ffn_rows_transposed")
        s_fXe = sem("ffn_rows_transposed_copied")
        s_fG = sem("ffn_gate_up_products")
        s_fsi = sem("ffn_silu_ready")
        s_fh = sem("ffn_hidden_ready")
        s_fHT = sem("ffn_hidden_transposed")
        s_fHTe = sem("ffn_hidden_transposed_copied")
        s_fO = sem("ffn_out_products")
        s_fy = sem("ffn_out_taken")
        s_fst = [sem("routed_rows_stored_a"), sem("routed_rows_stored_b")]
        s_g1 = [sem("rows_gathered1_a"), sem("rows_gathered1_b")]
        s_half = sem("first_routed_row_added")
        s_past = sem("waits_passed")
        s_fin = sem("tile_finished")
        s_out = sem("output_stored")

        block = ctx.enter_context(nc.Block())

        x_rows, out_rows = (v.rearrange("b (h p j) d -> (b h) j p d", h=2, j=J) for v in (a["x"], out))
        mask_rows = a["mask"].rearrange("b (h p j) d -> (b h) j p d", h=2, j=J)

        def dram_tile(v, i):
            if isinstance(i.t, int):
                return v[i.t // 4, i.t % 4]
            return v[span(i.m // 2), span(2 * (i.m % 2) + i.q)].rearrange("a c p d -> (a c p) d")

        def ring_slot(eng, t):
            return eng.value_load(info[0][0:1, 1, span(t)], min_val=0, max_val=R0 - 1)

        @block.sync
        def _(sp):
            sp.dma_start(ctxT[:, :, :], a["ctxT"]).then_inc(s_w0, 16)
            sp.dma_start(w0k, a["Wk0T"]).then_inc(s_w0, 16)
            sp.dma_start(w0q, a["Wq0"]).then_inc(s_w0, 16)
            sp.dma_start(w0v, a["Wv0T"]).then_inc(s_w0, 16)
            sp.dma_start(b0c[:, :, :], a["bkq"]).then_inc(s_w0, 16)
            sp.dma_start(bvb, a["bv"].to_broadcast([P, D])).then_inc(s_w0, 16)
            for g in range(NT // J):
                sp.dma_start(xres[:, J * g:J * g + J, :],
                             x_rows[g].rearrange("j p d -> p j d")).then_inc(s_x, 16)
            sp.dma_start(gateT[:, :, :], a["gateT"]).then_inc(s_rt, 16)
            sp.dma_start(gate_b[:, :], a["gate_b"].to_broadcast([P, E0 + E1])).then_inc(s_rt, 16)
            sp.dma_start(scale_b, a["norm_scale"].to_broadcast([P, D])).then_inc(s_rt, 16)
            sp.dma_start(att_in_v, a["wk1"]).then_inc(s_wkq, 16)
            sp.dma_start(att_w_v, a["wq1T"]).then_inc(s_wkq, 16)

            def keep_rows(l, kept, each):
                rows = xs[l].rearrange("(t p) d -> p t d", p=P)

                def keep(i):
                    sp.wait_ge(kept, each * (i.t + 1))
                    sp.dma_start(rows[:, span(2 * i.t, 2), :], normed[:, span(2 * i.t, 2), :]
                                 ).then_inc(s_rows[l], 16)

                over_tiles(sp, 0, NPAIR, keep)

            keep_rows(0, s_nc, 1)
            sp.wait_ge(s_l1p, 2)
            sp.dma_start(att_in_v, a["wv1"]).then_inc(s_wv, 16)
            sp.wait_ge(s_l1p, 10)
            sp.dma_start(att_w_v, a["wo1"]).then_inc(s_wo, 16)

            sp.wait_ge(s_info, 1)

            def weights(i):
                e = sp.value_load(info[0][0:1, 0, span(i.t)], min_val=0, max_val=E0 - 1)
                r = ring_slot(sp, i.t)
                new = sp.value_load(info[0][0:1, 2, span(i.t)], min_val=0, max_val=1)
                wait(sp, s_ey, i.t - R0 + 1)
                alone(sp, s_past)
                wait(sp, s_ew[i.p], 16 * i.half)
                sp.dma_start(ring[:, span(r), :].rearrange("p a w -> p (a w)"),
                             a["w_e0"][span(e)].rearrange("a p w -> (a p) w"),
                             cond=(new != 0)).then_inc(s_ew[i.p], 16)

            for t in range(AHEAD):
                weights(Tile(t // 4, t % 4, 4))
            sp.wait_ge(s_l1p, 20)
            sp.wait_ge(s_inv, 1)
            over_tiles(sp, AHEAD, T0, weights, lead=R0, tail=0, u=4)

            def mask_tile(i):
                wait(sp, s_1m, i.t - 1)
                sp.dma_start(msk[:, i.q, :], dram_tile(mask_rows, i)).then_inc(s_mk[i.q], 16)

            sp.wait_ge(s_ey, T0)
            mask_tile(Tile(0, 0))
            mask_tile(Tile(0, 1))
            for t in range(2, NT):
                mask_tile(Tile(t // 2, t % 2))
                if t - 2 < EARLY:
                    sp.dma_start(w1s[:, t - 2, :], a["w_e1"][t - 2]).then_inc(s_w1, 16)
            keep_rows(1, s_rk, 2)
            def rows1(source):
                def body(i):
                    wait(sp, s_fX, i.t - 1)
                    sp.dma_start(xr1[:, i.q, :], source(i)).then_inc(s_fx[i.q], 16)
                return body

            def token_rows(first):
                return rows1(lambda i: normed[:, span(i.plus(first).t), :].rearrange("p a d -> p (a d)"))

            sp.wait_ge(s_1t, NT)
            for t in range(SHARED_A):
                token_rows(0)(Tile(t // 2, t % 2))
                if t in (1, 3):
                    sp.wait_ge(s_1r, NT)
                    e = EARLY + t // 2
                    sp.dma_start(w1s[:, e, :], a["w_e1"][e]).then_inc(s_w1b, 16)
            over_tiles(sp, MID1, N1, token_rows(-T1))

            def output(i):
                sp.wait_ge(s_fin, i.t + 1)
                sp.dma_start(dram_tile(out_rows, i),
                             xres[:, span(i.t), :].rearrange("p a d -> p (a d)")).then_inc(s_out, 16)

            over_tiles(sp, 0, NT, output)
            sp.wait_ge(s_out, 16 * NT)

        @block.gpsimd
        def _(pool):
            chain = Chain(pool, s_pool)
            chain(pool.memset(ident[:, :], 0.0))
            chain(pool.memset(tri_b[:, :], 1.0))
            chain(pool.memset(blkmask, 1.0))
            pool.memset(kblk0_, 0.0).then_inc(s_blk0z, 1)
            pool.memset(tabV0_, 0.0).then_inc(s_blk0z, 1)
            chain.wait()
            pool.affine_select(out=ident[:, :], in_=ident[:, :], compare_op=ALU.not_equal, fill=1.0, base=0,
                               pattern=[[-1, P]], channel_multiplier=1).then_inc(s_const, 1)
            pool.affine_select(out=tri_b[:, :], in_=tri_b[:, :], compare_op=ALU.is_ge, fill=0.0, base=-1,
                               pattern=[[1, P]], channel_multiplier=-1).then_inc(s_const, 1)
            halves = [blkmask[64 * h:64 * h + 64, :].rearrange("p (c d) -> p c d", c=C0) for h in range(2)]
            pool.wait_ge(s_const, 2)
            for m in halves:
                chain(pool.affine_select(out=m, in_=m, compare_op=ALU.is_ge, fill=0.0, base=0,
                                         pattern=[[-KEYS0, C0], [0, DH]], channel_multiplier=1))
                chain.wait()
            for n, m in enumerate(halves):
                pool.affine_select(out=m, in_=m, compare_op=ALU.is_ge, fill=0.0, base=KEYS0 - 1,
                                   pattern=[[KEYS0, C0], [0, DH]], channel_multiplier=-1).then_inc(s_const, 1)
                pool.wait_ge(s_const, 3 + n)
            pool.memset(ones_b[:, :], 1.0).then_inc(s_const, 1)
            pool.memset(mhalf[:, :], -0.5).then_inc(s_const, 1)
            pool.memset(eps_t[:, :], EPS).then_inc(s_const, 1)
            pool.memset(blk1, 0.0).then_inc(s_bz, 1)
            pool.iota(pidx[:, :], pattern=[[0, 1]], base=0, channel_multiplier=1,
                      allow_small_or_imprecise_dtypes=True).then_inc(s_iota, 1)
            pool.iota(iota_e[:, :], pattern=[[1, E0]], base=0, channel_multiplier=0,
                      allow_small_or_imprecise_dtypes=True).then_inc(s_iota, 1)
            pool.iota(iota_p[:, :], pattern=[[1, P]], base=0, channel_multiplier=0,
                      allow_small_or_imprecise_dtypes=True).then_inc(s_iota, 1)
            pool.iota(token_id[:, :], pattern=[[P, NT]], base=0, channel_multiplier=1,
                      allow_small_or_imprecise_dtypes=True).then_inc(s_iota, 1)
            pool.wait_ge(s_const, 7)

            def factor(base, i, width, count):
                q, w = i.q, slice(0, width)
                chain.n = count
                pool.wait_ge(s_var, base + i.t + 1)
                chain(pool.tensor_tensor(rtmp[:, 0, w], mv[:, q, w, 1], eps_t[:, w], ALU.add))
                chain.wait()
                pool.tensor_tensor(rs[:, q, w], rtmp[:, 0, w], mhalf[:, w], ALU.pow).then_inc(s_rstd, 1)
                pool.wait_ge(s_rstd, base + i.t + 1)

            def router_factors(i):
                q, t = i.q, rtmp[:, 0, :]
                v, r = mv_r[:, q, :, 1], rs_r[:, q, :]
                pool.wait_ge(s_gvar, i.t + 1)
                chain(pool.tensor_tensor(t, v, eps_t[:, :], ALU.add))
                chain.wait()
                chain(pool.tensor_tensor(r, t, mhalf[:, :], ALU.pow))
                chain.wait()
                chain(pool.tensor_tensor(t, v, r, ALU.mult))
                chain.wait()
                chain(pool.tensor_tensor(t, t, r, ALU.mult))
                chain.wait()
                chain(pool.tensor_tensor(t, t, eps_t[:, :], ALU.add))
                chain.wait()
                pool.tensor_tensor(rms[:, q, :], t, mhalf[:, :], ALU.pow).then_inc(s_grstd, 1)
                pool.wait_ge(s_grstd, i.t + 1)

            def gather_rows(l, sem_, buf, i):
                place = token_col[:, i.q:i.q + 1]
                pool.tensor_copy(out=place, in_=slot_token[l][:, span(i.t)]).then_inc(s_col, 1)
                pool.wait_ge(s_col, l * T0 + i.t + 1)
                alone(pool, s_past)
                pool.indirect_dma_start(
                    out=buf, out_offset=None, in_=xs[l],
                    in_offset=bass.IndirectOffsetOnAxis(ap=place.bitcast(U32), axis=0)).then_inc(sem_, 16)

            for t in range(NPAIR + 3):
                i = Tile(t // 2, t % 2)
                if i.exists(0, NPAIR):
                    factor(0, i, 2, chain.n)
                if i.plus(-3).exists(0, NPAIR):
                    router_factors(i.plus(-3))
            pool.wait_ge(s_tok, 1)
            pool.wait_ge(s_rows[0], 16 * NPAIR)

            def rows0(i):
                if i.exists(0, T0):
                    wait(pool, s_eX, i.t - 3)
                    gather_rows(0, s_ex[i.q], xr0[:, i.q, :], i)
                j = i.plus(-LAG0)
                if j.exists(0, T0) and j.p == 0:
                    pool.wait_ge(s_ey, j.t + 2)
                    pool.dma_start(ys[0][span(j.t * P, 2 * P), :].rearrange("(k p) d -> p k d", k=2),
                                   y0[:, j.pair]).then_inc(s_est[j.pair], 16)

            over_tiles(pool, 0, T0 + LAG0, rows0, lead=LAG0, tail=LAG0, u=4)
            for q in range(2):
                pool.wait_ge(s_est[q], 16 * T0 // 4)

            def gather0(i):
                if i >= 2:
                    pool.wait_ge(s_comb4, K0 * (i - 1))
                for k in range(K0):
                    pool.indirect_dma_start(
                        out=gat0[i % 2][:, k, :], out_offset=None, in_=ys[0],
                        in_offset=bass.IndirectOffsetOnAxis(ap=slot_i[0][:, k, i:i + 1].bitcast(U32), axis=0)
                    ).then_inc(s_gath[i % 2], 16)

            def router_factor(i):
                q = i % 2
                pool.wait_ge(s_rvar, i + 1)
                chain(pool.tensor_tensor(rtmp[:, 0, 1:2], mv[:, q, 1, 1:2], eps_t[:, 1:2], ALU.add))
                chain.wait()
                pool.tensor_tensor(rs[:, q, 1:2], rtmp[:, 0, 1:2], mhalf[:, 1:2], ALU.pow).then_inc(s_rrstd, 1)
                pool.wait_ge(s_rrstd, i + 1)

            gather0(0)
            for i in range(NT):
                if i + 1 < NT:
                    gather0(i + 1)
                factor(NPAIR, Tile(i // 2, i % 2), 1, chain.n)
                if i >= LAGR:
                    router_factor(i - LAGR)
            for i in range(NT - LAGR, NT):
                router_factor(i)
            pool.wait_ge(s_tok, 2)
            pool.wait_ge(s_rows[1], 16 * NPAIR)

            def rows1(i):
                if i.exists(0, T1):
                    pool.wait_ge(s_fX, SHARED_A + i.t - 1)
                    gather_rows(1, s_fr[i.q], xr1[:, i.q, :], i)
                j = i.plus(-LAG1)
                if j.exists(0, T1):
                    pool.wait_ge(s_fy, SHARED_A + j.t + 1)
                    pool.dma_start(ys[1][span(j.t * P, P), :], y1[:, j.q, :]).then_inc(s_fst[j.q], 16)

            over_tiles(pool, 0, T1 + LAG1, rows1, lead=LAG1, tail=LAG1)
            for q in range(2):
                pool.wait_ge(s_fst[q], 16 * T1 // 2)
            for i in range(NT):
                if i >= 2:
                    pool.wait_ge(s_g1[i % 2], 16 * K1 * (i // 2))
                for k in range(K1):
                    pool.indirect_dma_start(
                        out=gat1[:, i, k, :], out_offset=None, in_=ys[1],
                        in_offset=bass.IndirectOffsetOnAxis(ap=slot_i[1][:, k, i:i + 1].bitcast(U32), axis=0)
                    ).then_inc(s_g1[i % 2], 16)

        @block.scalar
        def _(act):
            def copy(out_, in_, sem_, scale=1.0):
                act.activation(out_, in_, ACT.Copy, scale=scale).then_inc(sem_, 1)

            def exps0(i):
                act.wait_ge(s_scb, i.t + 1)
                act.activation(sc0[:, i.q, :], sc0[:, i.q, :], ACT.Exp).then_inc(s_exp, 1)

            def rows_t0(i):
                act.wait_ge(s_xt, i.t + 1)
                wait(act, s_sc, i.t - 1)
                copy(xT_a[:, i.q, :], ps[i.q][:, :], s_xte)

            def weights_t0(i):
                act.wait_ge(s_att, i.t + 1)
                wait(act, s_ao, i.t - 1)
                copy(aT0[:, i.q, :], ps[4][:, 0:P], s_atte)

            rows_t0(Tile(0, 0))

            def router0(i):
                act.wait_ge(s_gt, i.t + 1)
                wait(act, s_gl, i.t - 1)
                copy(gx[:, i.q, :], ps[7][:, :], s_gte)
                copy(normed[:, span(2 * i.t, 2), :], xn_r[:, i.q, :].rearrange("p (a d) -> p a d", a=2), s_nc)

            def attend0(i):
                if i.exists(0, NPAIR):
                    exps0(i)
                if i.plus(1).exists(0, NPAIR):
                    rows_t0(i.plus(1))
                if i.exists(0, NPAIR):
                    weights_t0(i)
                if i.plus(-2).exists(0, NPAIR):
                    router0(i.plus(-2))

            over_tiles(act, 0, NPAIR + 2, attend0, lead=6, tail=4)

            act.wait_ge(s_wd, 1)
            act.activation(wexp[:, :, :], wexp[:, :, :], ACT.Exp).then_inc(s_we, 1)

            def blocks(base):
                for g in range(2):
                    act.wait_ge(s_l1p, base + g + 1)
                    for h in range(2):
                        r = slice(64 * h, 64 * h + 64)
                        dst = blk1_v[r, 4 * g:4 * g + 4, :, h, :]
                        src = ps[g][r, :].rearrange("p (h b s) -> p h b s", h=4, b=B)
                        ins = act.activation(dst, src, ACT.Copy, scale=DH ** -0.5 if base == 0 else 1.0)
                    ins.then_inc(s_l1e, 1)

            act.wait_ge(s_bz, 1)
            blocks(0)
            for n in range(8):
                act.wait_ge(s_l1p, 3 + n)
                k, g = n // 4, n % 4
                copy(tabA[:, :, k, 256 * g:256 * g + 256].rearrange("p b (h n) -> p h b n", h=2),
                     ps[2 + n % 2][:, :].rearrange("p (h b n) -> p h b n", h=2, b=B), s_l1e)
            blocks(10)
            for n in range(8):
                act.wait_ge(s_l1p, 13 + n)
                b, g = n // 4, n % 4
                copy(tabV[:, b, 2 * g:2 * g + 2, :], ps[2 + n % 2][:, :].rearrange("p (h n) -> p h n", h=2), s_l1e)

            act.wait_ge(s_info, 1)

            def rows_e0(i):
                act.wait_ge(s_eX, i.t + 1)
                wait(act, s_eH, i.t - 1)
                copy(xT0[:, i.p, :, :], ps[i.p][:, 0:D].rearrange("p (k n) -> p k n", k=FK), s_eXe)

            def hidden_t0(i):
                act.wait_ge(s_eHT, i.t + 1)
                wait(act, s_eO, i.t - 1)
                copy(hT0[:, i.p, :, :], ps[4][:, 0:D].rearrange("p (k n) -> p k n", k=2), s_eHTe)

            def sigmoid0(i):
                act.wait_ge(s_eglu, i.t + 1)
                wait(act, s_ehs, i.t - 1)
                act.activation(sig[:, i.p], glu[:, i.p], ACT.Sigmoid, scale=ALPHA).then_inc(s_esig, 1)

            rows_e0(Tile(0, 0, 4))

            def expert0(i):
                if i.plus(-2).exists(0, T0):
                    hidden_t0(i.plus(-2))
                if i.plus(-1).exists(0, T0):
                    sigmoid0(i.plus(-1))
                if i.plus(1).exists(0, T0):
                    rows_e0(i.plus(1))

            over_tiles(act, 0, T0 + 2, expert0, lead=4, tail=4, u=4)

            def exps1(i, first, last):
                act.wait_ge(s_1b, i.t + 1)
                for h in range(first, last):
                    s = sc1[:, i.q, h * S2:h * S2 + S2]
                    ins = act.activation(s, s, ACT.Exp, bias=sm1[:, i.q, 0, h:h + 1],
                                         accum_out=sm1[:, i.q, 1, h:h + 1])
                if last == H1:
                    ins.then_inc(s_1x, 1)

            def rows_t1(i):
                act.wait_ge(s_1t, i.t + 1)
                wait(act, s_1s, i.t - 1)
                copy(xT1[:, i.q, :, :], ps[0][:, 0:D].rearrange("p (k n) -> p k n", k=FK), s_1te)

            def weights_t1(i):
                act.wait_ge(s_1wt, i.t + 1)
                wait(act, s_1o, i.t)
                for g in range(2):
                    ins = act.activation(aT1[:, 4 * g:4 * g + 4, :],
                                         ps[5 + g][:, :].rearrange("p (h n) -> p h n", h=4), ACT.Copy)
                ins.then_inc(s_1wte, 1)

            def router1(i):
                act.wait_ge(s_rtr, i.t + 1)
                wait(act, s_rl, i.t - 1)
                copy(gx[:, i.q, 0:D], ps[0][:, D:2 * D], s_rte)
                copy(normed[:, span(i.t), :].rearrange("p a d -> p (a d)"), xn_f[:, i.q, :], s_rk)

            def attend1(i):
                if i.plus(2).exists(0, NT):
                    rows_t1(i.plus(2))
                if i.plus(-2).exists(0, NT):
                    router1(i.plus(-2))
                if i.plus(1).exists(0, NT):
                    exps1(i.plus(1), 0, H1 // 2)
                if i.exists(0, NT):
                    weights_t1(i)
                if i.plus(1).exists(0, NT):
                    exps1(i.plus(1), H1 // 2, H1)

            rows_t1(Tile(0, 0))
            attend1(Tile(-1, 1))
            over_tiles(act, 0, NT + 2, attend1, lead=4, tail=4)
            act.wait_ge(s_pmax, 1)
            act.activation(logits[:, :, 0:E1], logits[:, :, 0:E1], ACT.Exp).then_inc(s_pexp, 1)


            def rows_e1(i):
                act.wait_ge(s_fX, i.t + 1)
                wait(act, s_fG, 2 * (i.t - 1))
                copy(xTe[:, i.q, :, :], ps[0][:, 0:D].rearrange("p (k n) -> p k n", k=FK), s_fXe)

            def hidden_t1(i, c):
                u = 2 * i.t + c
                act.wait_ge(s_fHT, u + 1)
                wait(act, s_fO, u - 1)
                copy(hTe[:, c, :, :], ps[5][:, 0:3 * P].rearrange("p (s n) -> p s n", s=3), s_fHTe)

            def silu1(i, c):
                u = 2 * i.t + c
                act.wait_ge(s_fG, u + 1)
                wait(act, s_fh, u - 1)
                act.activation(silu[:, c, :], ps[1 + 2 * c][:, 0:FC1], ACT.Silu).then_inc(s_fsi, 1)

            rows_e1(Tile(0, 0))

            def expert1(i):
                if i.exists(0, N1):
                    silu1(i, 0)
                if i.plus(-1).exists(0, N1):
                    hidden_t1(i.plus(-1), 1)
                if i.plus(1).exists(0, N1):
                    rows_e1(i.plus(1))
                if i.exists(0, N1):
                    silu1(i, 1)
                    hidden_t1(i, 0)

            over_tiles(act, 0, N1, expert1)
            expert1(Tile(N1 // 2, 0))

        @block.vector
        def _(dve):
            chain = Chain(dve, s_dve)
            TT, TS, STT, CP = dve.tensor_tensor, dve.tensor_scalar, dve.scalar_tensor_tensor, dve.tensor_copy

            def over(ap, n):
                return ap.unsqueeze(len(ap.shape)).broadcast_to([*ap.shape, n])

            def spread(ap, n):
                return ap.unsqueeze(1).broadcast_to([ap.shape[0], n, ap.shape[1]])

            dve.wait_ge(s_w0, 16 * 6)
            for m in range(2):
                ins = CP(bqb[:, m, :], b0c[:, 1, m:m + 1].broadcast_to([P, P]))
            ins.then_inc(s_bqb, 1)
            for k in range(FK):
                for b in range(B):
                    for c in range(C0):
                        ins = CP(crep[:, k, b, :, c, :],
                                 ctxT[:, k, b * S2:b * S2 + S2].rearrange("p (s j) -> p j s", j=J))
            ins.then_inc(s_crep, 1)
            dve.wait_ge(s_p0, 1)
            dve.wait_ge(s_blk0z, 2)
            for m in range(2):
                for h in range(2):
                    r = slice(64 * h, 64 * h + 64)
                    ins = TS(kblk0[r, m, h, :], ps[0][r, m * P:m * P + P], b0c[r, 0, m:m + 1], None, ALU.add)
            ins.then_inc(s_p0e, 1)
            dve.wait_ge(s_p0, 2)
            for k in range(3):
                src = ps[1 + k][:, :].rearrange("p (c b s j) -> p b j c s", c=C0, b=B, j=J)
                for b in range(B):
                    ins = TS(tabA0[:, k, b], src[:, b], DH ** -0.5, None, ALU.mult)
            ins.then_inc(s_p0e, 1)
            dve.wait_ge(s_p0, 3)
            vals = ab[:, 0:1024].rearrange("p (n d) -> p n d", n=4)
            for n in range(4):
                chain(TT(vals[:, n, :], ps[4 + n // 2][:, 256 * (n % 2):256 * (n % 2) + 256], bvb, ALU.add))
            chain.wait()
            dve.wait_ge(s_const, 7)
            for n in range(4):
                for j in range(2):
                    r = slice(64 * j, 64 * j + 64)
                    ins = TT(tabV0[r, n // 2, n % 2, j, :], vals[r, n, :], blkmask[r, :], ALU.mult)
            ins.then_inc(s_p0e, 1)

            def statistics(base, var_base, t, q, rows):
                wait(dve, s_var, var_base + t)
                alone(dve, s_past)
                for k, x in enumerate(rows):
                    dve.bn_stats(stats[:, k, :], x).then_inc(s_bn, 1)
                dve.wait_ge(s_bn, base + len(rows) * (t + 1))
                alone(dve, s_past)
                for k in range(len(rows)):
                    ins = dve.bn_aggr(mv[:, q, k, :], stats[:, k, :])
                ins.then_inc(s_var, 1)

            def row(i, k=0):
                return xres[:, span(2 * i.t + k), :].rearrange("p a d -> p (a d)")

            def pair(v, i):
                return v[:, span(2 * i.t, 2), :]

            def pair_stats(i, base=0, var_base=0):
                statistics(base, var_base, i.t, i.q, [row(i, 0), row(i, 1)])

            dve.wait_ge(s_x, 16 * (NT // J))

            def normalise0(i):
                dve.wait_ge(s_rstd, i.t + 1)
                wait(dve, s_xt, i.t - 1)
                for k in range(2):
                    ins = TS(xn_a[:, i.q, k * D:k * D + D], row(i, k), mv[:, i.q, k, 0:1],
                             rs[:, i.q, k:k + 1], ALU.subtract, ALU.mult)
                ins.then_inc(s_xn, 1)

            def shift0(i):
                s = sc0[:, i.q, :]
                sg = s.rearrange("p (g n) -> p g n", n=KEYS0)
                dve.wait_ge(s_sc, i.t + 1)
                bias = tabA0[:, 2].rearrange("p b j c s -> p b (j c s)")[:, span(i.m // 2), P * i.q:P * i.q + P]
                chain(TT(s, ps[2 + i.q][:, 0:P], bias.rearrange("p a n -> p (a n)"), ALU.add))
                chain.wait()
                chain(dve.tensor_reduce(sm0[:, 0, 0:8], sg, AX.X, ALU.max))
                chain.wait()
                TT(sg, sg, over(sm0[:, 0, 0:8], KEYS0), ALU.subtract).then_inc(s_scb, 1)

            def weights0(i):
                sg = sc0[:, i.q, :].rearrange("p (g n) -> p g n", n=KEYS0)
                dve.wait_ge(s_exp, i.t + 1)
                chain(dve.tensor_reduce(sm0[:, 1, 0:8], sg, AX.X, ALU.add))
                chain.wait()
                chain(dve.reciprocal(sm0[:, 2, 0:8], sm0[:, 1, 0:8]))
                chain.wait()
                TT(sg, sg, over(sm0[:, 2, 0:8], KEYS0), ALU.mult).then_inc(s_at, 1)

            def residual0(i):
                dve.wait_ge(s_ao, i.t + 1)
                TT(pair(xres, i), pair(xres, i), ps[5 + i.q][:, :].rearrange("p (a d) -> p a d", a=2),
                   ALU.add).then_inc(s_aoe, 1)

            pair_stats(Tile(0, 0))
            dve.wait_ge(s_p0e, 2)
            normalise0(Tile(0, 0))
            pair_stats(Tile(0, 1))
            c0 = chain.n

            def router_statistics0(i):
                dve.wait_ge(s_aoe, i.t + 1)
                wait(dve, s_gvar, i.t)
                for k in range(2):
                    dve.bn_stats(stats_r[:, k, :], row(i, k)).then_inc(s_gbn, 1)
                dve.wait_ge(s_gbn, 2 * (i.t + 1))
                for k in range(2):
                    ins = dve.bn_aggr(mv_r[:, i.q, k, :], stats_r[:, k, :])
                ins.then_inc(s_gvar, 1)

            def router_normalise0(i):
                dve.wait_ge(s_grstd, i.t + 1)
                wait(dve, s_gt, i.t - 1)
                wait(dve, s_nc, i.t - 1)
                for k in range(2):
                    ins = TS(xn_u[:, i.q, k * D:k * D + D], row(i, k), mv_r[:, i.q, k, 0:1],
                             rs_r[:, i.q, k:k + 1], ALU.subtract, ALU.mult)
                ins.then_inc(s_un, 1)
                dve.wait_ge(s_un, i.t + 1)
                for k in range(2):
                    ins = STT(out=xn_r[:, i.q, k * D:k * D + D], in0=xn_u[:, i.q, k * D:k * D + D],
                              scalar=rms[:, i.q, k:k + 1], in1=scale_b, op0=ALU.mult, op1=ALU.mult)
                ins.then_inc(s_gn, 1)
                TT(pair(xres, i), pair(xres, i), xn_u[:, i.q, :].rearrange("p (a d) -> p a d", a=2),
                   ALU.add).then_inc(s_xl, 1)

            def router_logits0(i):
                dve.wait_ge(s_gl, i.t + 1)
                dve.wait_ge(s_sc, at_most(i.t + 5, NPAIR))
                TT(logits[:, span(2 * i.t, 2), 0:E0],
                   ps[2 + i.q][:, P:P + 2 * E0].rearrange("p (a e) -> p a e", a=2),
                   spread(gate_b[:, 0:E0], 2), ALU.add).then_inc(s_gle, 1)

            def attend0(i):
                chain.step(c0, 4, i.t)
                if i.exists(0, NPAIR):
                    shift0(i)
                if i.plus(-4).exists(0, NPAIR):
                    router_logits0(i.plus(-4))
                if i.plus(1).exists(0, NPAIR):
                    normalise0(i.plus(1))
                if i.plus(2).exists(0, NPAIR):
                    pair_stats(i.plus(2))
                if i.exists(0, NPAIR):
                    weights0(i)
                    chain.stepped()
                if i.plus(-2).exists(0, NPAIR):
                    router_normalise0(i.plus(-2))
                if i.plus(-1).exists(0, NPAIR):
                    residual0(i.plus(-1))
                    router_statistics0(i.plus(-1))

            dve.wait_ge(s_rt, 16 * 3)
            over_tiles(dve, 0, NPAIR + 4, attend0, lead=6, tail=6)
            dve.wait_ge(s_gle, NPAIR)

            shapes = [(E0, E0, K0, T0), (EC1, E1, K1, T1)]

            def choose(l):
                columns = shapes[l][0]
                for i in range(NT):
                    chain(dve.max(top[:, i, :], logits[:, i, 0:columns]))
                chain.wait()
                for i in range(NT):
                    chain(dve.max_index(topi[:, i, :], top[:, i, :], logits[:, i, 0:columns]))

            def by_expert(l, name):
                n, columns = (shapes[l][2], shapes[l][0]) if name == "one" else (1, shapes[l][0])
                v = R[l][name][:, 0:n * NT * columns]
                if name == "one":
                    return v.rearrange("p (k t e) -> p k t e", k=n, t=NT)
                return v.rearrange("p (t e) -> p t e", t=NT)

            def masks(l):
                columns, _, chosen, _ = shapes[l]
                topf, one, mask = R[l]["topf"], by_expert(l, "one"), by_expert(l, "mask")
                dve.wait_ge(s_iota, 4)
                chain.wait()
                chain(CP(topf, topi[:, :, :]))
                chain.wait()
                for k in range(chosen):
                    chain(TT(one[:, k], spread(iota_e[:, 0:columns], NT), over(topf[:, :, k], columns),
                             ALU.is_equal))
                chain.wait()
                for k in range(1, chosen):
                    ins = TT(mask, one[:, 0] if k == 1 else mask, one[:, k], ALU.add)
                    if k < chosen - 1:
                        chain(ins)
                        chain.wait()
                ins.then_inc(s_mask, 1)

            def ranked(l):
                columns = shapes[l][0]
                E = slice(0, columns)
                cnt_i, ones_f, tiles_f, ends_f, base_f = (
                    R[l][n][:, E] for n in ("cnt_i", "ones_f", "tiles_f", "ends_f", "base_f"))
                dve.wait_ge(s_rank, l + 1)
                chain(TS(cnt_i, counts[l], float(P - 1), None, ALU.add))
                chain.wait()
                chain(TS(cnt_i, cnt_i, 7, None, ALU.logical_shift_right))
                chain(dve.memset(ones_f, 1.0))
                chain.wait()
                chain(CP(tiles_f, cnt_i))
                chain.wait()
                chain(dve.tensor_tensor_scan(ends_f, ones_f, tiles_f, 0.0, ALU.mult, ALU.add))
                chain.wait()
                chain(TT(base_f, ends_f, tiles_f, ALU.subtract))
                chain.wait()
                chain(TS(base_f, base_f, float(P), None, ALU.mult))
                chain.wait()
                TT(by_expert(l, "slot"), earlier[l].rearrange("p (t e) -> p t e", t=NT), spread(base_f, NT),
                   ALU.add).then_inc(s_rread, 1)

            def slots(l):
                chosen = shapes[l][2]
                slots_f, tmp = R[l]["slots_f"], by_expert(l, "tmp")
                dve.wait_ge(s_rread, 2 * l + 1)
                for k in range(chosen):
                    chain.wait()
                    chain(TT(tmp, by_expert(l, "one")[:, k], by_expert(l, "slot"), ALU.mult))
                    chain.wait()
                    chain(dve.tensor_reduce(slots_f[:, k, :], tmp, AX.X, ALU.add))
                chain.wait()
                chain(CP(slot_i[l][:, :, :], slots_f[:, 0:chosen, :]))

            def tile_experts(l):
                columns, real, _, tiles = shapes[l]
                te_col, cmp_f = R[l]["te_col"][0:tiles, 0:1], R[l]["cmp_f"][0:tiles, 0:columns]
                chain(TS(cmp_f, R[l]["ends_f"][0:tiles, 0:columns], pidx[0:tiles, :], None, ALU.is_le))
                chain.wait()
                chain(dve.tensor_reduce(te_col, cmp_f, AX.X, ALU.add))
                chain.wait()
                TS(te_col, te_col, float(real - 1), None, ALU.min).then_inc(s_te, 1)

            def slot_parts(l):
                n = shapes[l][2] * NT
                flat = slot_i[l][:, :, :].rearrange("p k t -> p (k t)")
                slot_sh, slot_hi, slot_lo = (R[l][m][:, 0:n] for m in ("slot_sh", "slot_hi", "slot_lo"))
                chain(TS(slot_sh, flat, 7, None, ALU.logical_shift_right))
                chain.wait()
                chain(CP(slot_hi, slot_sh))
                chain.wait()
                chain(TS(slot_sh, flat, P - 1, None, ALU.bitwise_and))
                chain.wait()
                chain(CP(slot_lo, slot_sh))
                chain.wait()

            def tile_info(l):
                tiles = shapes[l][3]
                te = R[l]["te_row"][:, 0:tiles]
                dve.wait_ge(s_ter, l + 1)
                if l == 1:
                    CP(te, expert_of[l]).then_inc(s_rread, 1)
                    dve.wait_ge(s_rread, 4)
                    TS(info[1][:, 0, SHARED_A:MID1], te, 1.0, None, ALU.add).then_inc(s_info, 1)
                    return
                fl, rk, on = (R[l][m][:, 0:tiles] for m in ("fl_row", "rk_row", "one_row"))
                chain(dve.memset(fl[:, 0:1], 1.0))
                chain(dve.memset(on, 1.0))
                CP(te, expert_of[l]).then_inc(s_rread, 1)
                dve.wait_ge(s_rread, 2)
                chain.wait()
                chain(TT(fl[:, 1:tiles], te[:, 1:tiles], te[:, 0:tiles - 1], ALU.not_equal))
                chain.wait()
                chain(dve.tensor_tensor_scan(rk, on, fl, -1.0, ALU.mult, ALU.add))
                chain(CP(info[0][:, 0, :], te))
                chain(CP(info[0][:, 2, :], fl))
                chain.wait()
                chain(CP(info[0][:, 1, :], rk))
                chain.wait()
                TS(info[0][:, 1, :], info[0][:, 1, :], R0 - 1, None, ALU.bitwise_and).then_inc(s_info, 1)

            def one_hot(l, lo, hi):
                slot_hi, slot_lo = R[l]["slot_hi"], R[l]["slot_lo"]
                for c in range(lo, hi):
                    TS(hot_hi[l][:, c, :], iota_p[:, 0:shapes[l][3]], slot_hi[:, c:c + 1],
                       token_id[:, c % NT:c % NT + 1], ALU.is_equal, ALU.mult)
                    TS(hot_lo[l][c // NT][:, c % NT, :], iota_p[:, :], slot_lo[:, c:c + 1], None,
                       ALU.is_equal).then_inc(s_hot, 1)

            def tokens(l):
                dve.wait_ge(s_inv, l + 1)
                CP(slot_token[l][:, :], token_of[l]).then_inc(s_tok, 1)

            chain.n = c0 + 4 * NPAIR

            choose(0)
            TT(wexp[:, :, :], top[:, :, 0:K0], over(top[:, :, 0], K0), ALU.subtract).then_inc(s_wd, 1)
            masks(0)
            ranked(0)
            slots(0)
            tile_experts(0)
            tile_info(0)
            slot_parts(0)
            one_hot(0, 0, K0 * NT)
            tokens(0)
            dve.wait_ge(s_we, 1)
            chain(dve.tensor_reduce(wsum[:, 0, :], wexp[:, :, :], AX.X, ALU.add))
            chain.wait()
            chain(dve.reciprocal(wsum[:, 1, :], wsum[:, 0, :]))
            chain.wait()
            chain(TT(wgt[0][:, :, :], wexp[:, :, :], over(wsum[:, 1, :], K0), ALU.mult))

            slot_at = Registers(lambda t: ring_slot(dve, t))

            def biases(i, lo, n):
                return ring[:, span(slot_at[i]), W0 + lo:W0 + lo + n].rearrange("p a n -> p (a n)")

            def bias0(i):
                dve.wait_ge(s_eH, i.t + 1)
                TT(hb_, ps[2 + i.p][:, :], biases(i, 0, 2 * F0), ALU.add).then_inc(s_ehb, 1)

            def clip0(i):
                dve.wait_ge(s_ehb, i.t + 1)
                wait(dve, s_ehs, i.t - 1)
                TS(glu[:, i.p], hb_[:, 0:F0], LIMIT, None, ALU.min).then_inc(s_eglu, 1)
                TS(lin[:, i.p], hb_[:, F0:2 * F0], LIMIT, -LIMIT, ALU.min, ALU.max).then_inc(s_elin, 1)

            def gate0(i):
                dve.wait_ge(s_elin, i.t + 1)
                STT(out=lin[:, i.p], in0=lin[:, i.p], scalar=1.0, in1=glu[:, i.p], op0=ALU.add,
                    op1=ALU.mult).then_inc(s_egate, 1)

            def hidden0(i):
                dve.wait_ge(s_egate, i.t + 1)
                dve.wait_ge(s_esig, i.t + 1)
                wait(dve, s_eHT, i.t - 1)
                TT(hs0[:, i.p, :], lin[:, i.p], sig[:, i.p], ALU.mult).then_inc(s_ehs, 1)

            def rows_out0(i):
                bias = biases(i, 2 * F0, D)
                dve.wait_ge(s_eO, i.t + 1)
                wait(dve, s_est[i.pair], 16 * i.m)
                TT(y0[:, i.pair, i.p, :], ps[5 + i.p][:, 0:D], bias, ALU.add).then_inc(s_ey, 1)

            def expert0(i):
                slot_at.begin(i)
                last = i.plus(-1)
                if last.exists(0, T0):
                    gate0(last)
                if i.exists(0, T0):
                    slot_at.load(i)
                if last.exists(0, T0):
                    hidden0(last)
                if i.exists(0, T0):
                    bias0(i)
                if i.plus(-2).exists(0, T0):
                    slot_at.load(i.plus(-2))
                if i.exists(0, T0):
                    clip0(i)
                if i.plus(-2).exists(0, T0):
                    rows_out0(i.plus(-2))

            over_tiles(dve, 0, T0 + 2, expert0, lead=4, tail=4, u=4)

            c1 = chain.n
            BN1 = 2 * NPAIR

            def row1(i):
                return xres[:, span(i.t), :].rearrange("p a d -> p (a d)")

            def combine0(i):
                dve.wait_ge(s_gath[i.q], 16 * K0 * (i.m + 1))
                for k in range(K0):
                    w = wgt[0][:, span(i.t), k:k + 1].rearrange("p a k -> p (a k)")
                    ins = STT(out=row1(i), in0=gat0[i.q][:, k, :], scalar=w, in1=row1(i),
                              op0=ALU.mult, op1=ALU.add)
                    ins.then_inc(s_comb4, 1)
                    dve.wait_ge(s_comb4, K0 * i.t + k + 1)
                statistics(BN1, NPAIR, i.t, i.q, [row1(i)])

            def normalise1(i):
                dve.wait_ge(s_rstd, NPAIR + i.t + 1)
                wait(dve, s_1t, i.t - 1)
                TS(xn1[:, i.q, :], row1(i), mv[:, i.q, 0, 0:1], rs[:, i.q, 0:1],
                   ALU.subtract, ALU.mult).then_inc(s_1n, 1)

            def shift1(i):
                s = sc1[:, i.q, :].rearrange("p (h n) -> p h n", h=H1)
                dve.wait_ge(s_1s, i.t + 1)
                dve.wait_ge(s_mk[i.q], 16 * (i.m + 1))
                for g in range(2):
                    ins = TT(s[:, 8 * g:8 * g + 8, :], ps[1 + 2 * i.q + g][:, :].rearrange("p (h n) -> p h n", h=8),
                             spread(msk[:, i.q, :], 8), ALU.add)
                ins.then_inc(s_1m, 1)
                dve.wait_ge(s_1m, i.t + 1)
                dve.tensor_reduce(sm1[:, i.q, 0, :], s, AX.X, ALU.max, negate=True).then_inc(s_1b, 1)

            def weights1(i):
                s = sc1[:, i.q, :].rearrange("p (h n) -> p h n", h=H1)
                dve.wait_ge(s_1x, i.t + 1)
                chain(dve.reciprocal(sm1[:, i.q, 2, :], sm1[:, i.q, 1, :]))
                chain.wait()
                TT(s, s, over(sm1[:, i.q, 2, :], S2), ALU.mult).then_inc(s_1w, 1)

            def residual1(i):
                dve.wait_ge(s_1o, i.t + 1)
                TT(row1(i), row1(i), ps[7][:, 0:D], ALU.add).then_inc(s_1r, 1)

            def router_statistics(i):
                dve.wait_ge(s_1r, i.t + 1)
                wait(dve, s_rvar, i.t)
                alone(dve, s_past)
                dve.bn_stats(stats[:, 1, :], row1(i)).then_inc(s_rbn, 1)
                dve.wait_ge(s_rbn, i.t + 1)
                alone(dve, s_past)
                dve.bn_aggr(mv[:, i.q, 1, :], stats[:, 1, :]).then_inc(s_rvar, 1)

            def router_normalise(i):
                dve.wait_ge(s_rrstd, i.t + 1)
                wait(dve, s_rtr, i.t - 1)
                wait(dve, s_rk, i.t - 1)
                TS(xn_f[:, i.q, :], row1(i), mv[:, i.q, 1, 0:1], rs[:, i.q, 1:2],
                   ALU.subtract, ALU.mult).then_inc(s_rn, 1)

            def router_logits(i):
                dve.wait_ge(s_rl, i.t + 1)
                TT(logits[:, span(i.t), 0:E1].rearrange("p a e -> p (a e)"), ps[7][:, D:D + E1],
                   gate_b[:, E0:E0 + E1], ALU.add).then_inc(s_rle, 1)

            def attend1(i):
                chain.step(c1, 1, i.t)
                if i.plus(2).exists(0, NT):
                    normalise1(i.plus(2))
                if i.plus(-2).exists(0, NT):
                    router_normalise(i.plus(-2))
                if i.plus(1).exists(0, NT):
                    shift1(i.plus(1))
                if i.exists(0, NT):
                    weights1(i)
                    chain.stepped()
                if i.plus(4).exists(0, NT):
                    combine0(i.plus(4))
                if i.plus(-1).exists(0, NT):
                    residual1(i.plus(-1))
                    router_statistics(i.plus(-1))
                if i.plus(-3).exists(0, NT):
                    router_logits(i.plus(-3))

            combine0(Tile(0, 0))
            normalise1(Tile(0, 0))
            combine0(Tile(0, 1))
            normalise1(Tile(0, 1))
            combine0(Tile(1, 0))
            shift1(Tile(0, 0))
            combine0(Tile(1, 1))
            over_tiles(dve, 0, NT + 4, attend1, lead=4, tail=8)

            dve.wait_ge(s_rle, NT)
            chain.n = c1 + NT
            lg = logits[:, :, 0:E1]
            chain(dve.tensor_reduce(wsum[:, 0, :], lg, AX.X, ALU.max))
            chain.wait()
            TT(lg, lg, over(wsum[:, 0, :], E1), ALU.subtract).then_inc(s_pmax, 1)
            chain(dve.memset(logits[:, :, E1:EC1], -1.0))
            chain(dve.memset(info[1][:, :, 0:SHARED_A], 0))
            chain(dve.memset(info[1][:, :, MID1:N1], 0))
            dve.wait_ge(s_pexp, 1)
            chain.wait()
            dve.sem_inc(s_shared, 1)
            def probabilities():
                chain(dve.tensor_reduce(wsum[:, 0, :], lg, AX.X, ALU.add))
                chain.wait()
                chain(dve.reciprocal(wsum[:, 1, :], wsum[:, 0, :]))
                chain.wait()
                chain(TT(lg, lg, over(wsum[:, 1, :], E1), ALU.mult))
                chain.wait()

            def chosen_weights():
                chain(dve.tensor_reduce(wsum[:, 0, :], top[:, :, 0:K1], AX.X, ALU.add))
                chain.wait()
                chain(dve.reciprocal(wsum[:, 1, :], wsum[:, 0, :]))
                chain.wait()
                chain(TT(wgt[1][:, :, :], top[:, :, 0:K1], over(wsum[:, 1, :], K1), ALU.mult))

            def routing_beside(t, half):
                n = K1 * NT // 4
                if (t, half) == (0, 0):
                    probabilities()
                elif (t, half) == (0, 1):
                    choose(1)
                elif (t, half) == (1, 0):
                    chosen_weights()
                elif (t, half) == (1, 1):
                    masks(1)
                elif (t, half) == (2, 1):
                    ranked(1)
                elif (t, half) == (3, 0):
                    slots(1)
                elif (t, half) == (3, 1):
                    tile_experts(1)
                    slot_parts(1)
                elif (t, half) == (4, 0):
                    one_hot(1, 0, n)
                elif (t, half) == (4, 1):
                    tile_info(1)
                    one_hot(1, n, 2 * n)
                elif (t, half) == (5, 0):
                    one_hot(1, 2 * n, 3 * n)
                elif (t, half) == (5, 1):
                    one_hot(1, 3 * n, 4 * n)
                elif (t, half) == (7, 1):
                    tokens(1)

            def hidden1(i, c):
                u = 2 * i.t + c
                dve.wait_ge(s_fsi, u + 1)
                wait(dve, s_fHT, u - 1)
                TT(hh[:, c, :], silu[:, c, :], ps[2 + 2 * c][:, 0:FC1], ALU.mult).then_inc(s_fh, 1)

            def take1(i, kind):
                dve.wait_ge(s_fO, 2 * i.t + 2)
                o = ps[6 + i.q][:, 0:D]
                if kind == "routed":
                    j = i.plus(-SHARED_A)
                    wait(dve, s_fst[i.q], 16 * j.m)
                    CP(y1[:, i.q, :], o).then_inc(s_fy, 1)
                else:
                    j = i if kind == "first" else i.plus(-T1)
                    TT(row1(j), row1(j), o, ALU.add).then_inc(s_fy, 1)

            def finish(i):
                dve.wait_ge(s_g1[i.q], 16 * K1 * (i.m + 1))
                for k in range(K1):
                    w = wgt[1][:, span(i.t), k:k + 1].rearrange("p a k -> p (a k)")
                    g = gat1[:, span(i.t), k, :].rearrange("p a d -> p (a d)")
                    STT(out=row1(i), in0=g, scalar=w, in1=row1(i), op0=ALU.mult, op1=ALU.add)                        .then_inc(s_half if k == 0 else s_fin, 1)
                    if k == 0:
                        dve.wait_ge(s_half, i.t + 1)

            def expert1(i, before):
                first = isinstance(i.t, int) and i.t < SHARED_A
                hidden1(i, 0)
                if first:
                    routing_beside(i.t, 0)
                hidden1(i, 1)
                if i.plus(-1).exists(0, N1):
                    take1(i.plus(-1), before)
                if first:
                    routing_beside(i.t, 1)

            def routed(i):
                first = isinstance(i.t, int) and i.t == SHARED_A
                expert1(i, "first" if first else "routed")

            for t in range(SHARED_A):
                expert1(Tile(t // 2, t % 2), "first")
            over_tiles(dve, SHARED_A, MID1, routed)
            dve.wait_ge(s_fy, SHARED_A)
            done = 0
            for t in range(MID1, N1 + 1):
                i = Tile(t // 2, t % 2)
                if t < N1:
                    expert1(i, "routed" if t == MID1 else "last")
                else:
                    take1(i.plus(-1), "last")
                for j in range(done, NT if t == N1 else 3 * max(0, t - MID1 - 1)):
                    if j >= SHARED_A:
                        dve.wait_ge(s_fy, j + T1 + 1)
                    finish(Tile(j // 2, j % 2))
                    done = j + 1

        @block.tensor
        def _(pe):
            MM = pe.matmul

            def transposes(dst, rows, n):
                for k in range(n):
                    ins = pe.transpose(dst[:, k * P:k * P + P], rows[:, k * P:k * P + P], ident[:, :])
                return ins

            pe.wait_ge(s_w0, 16 * 6)
            for m in range(2):
                for k in range(FK):
                    ins = MM(ps[0][:, m * P:m * P + P], w0k[:, k, m * P:m * P + P], ctxT[:, k, :],
                             start=(k == 0), stop=(k == FK - 1))
            ins.then_inc(s_p0, 1)
            pe.wait_ge(s_p0e, 1)
            pe.wait_ge(s_bqb, 1)
            for k in range(3):
                for m in range(2):
                    w = w0q[:, m, k * P:k * P + P] if k < FK else bqb[:, m, :]
                    ins = MM(ps[1 + k][:, m * 256:m * 256 + 256], w,
                             kblk0[:, m, :, :].rearrange("p c n -> p (c n)"), start=True, stop=True)
            ins.then_inc(s_p0, 1)
            pe.wait_ge(s_crep, 1)
            for n in range(4):
                for k in range(FK):
                    c = crep[:, k, n // 2].rearrange("p j c s -> p (j c s)")
                    ins = MM(ps[4 + n // 2][:, 256 * (n % 2):256 * (n % 2) + 256],
                             c[:, P * (n % 2):P * (n % 2) + P], w0v[:, k, :],
                             start=(k == 0), stop=(k == FK - 1))
            ins.then_inc(s_p0, 1)

            def rows_t0(i):
                pe.wait_ge(s_xn, i.t + 1)
                wait(pe, s_xte, i.t - 1)
                transposes(ps[i.q], xn_a[:, i.q, :], 4).then_inc(s_xt, 1)

            def scores0(i):
                pe.wait_ge(s_xte, i.t + 1)
                wait(pe, s_scb, i.t - 1)
                for j in range(2):
                    for k in range(FK):
                        tab = tabA0[:, k].rearrange("p b j c s -> p b (j c s)")[
                            :, span(i.m // 2), P * i.q + 64 * j:P * i.q + 64 * j + 64]
                        ins = MM(ps[2 + i.q][:, 64 * j:64 * j + 64],
                                 xT_a[:, i.q, (2 * j + k) * P:(2 * j + k) * P + P],
                                 tab.rearrange("p a n -> p (a n)"), start=(k == 0), stop=(k == FK - 1))
                ins.then_inc(s_sc, 1)

            def weights_t0(i):
                pe.wait_ge(s_at, i.t + 1)
                wait(pe, s_atte, i.t)
                transposes(ps[4], sc0[:, i.q, :], 1).then_inc(s_att, 1)

            def values0(i):
                pe.wait_ge(s_atte, i.t + 1)
                wait(pe, s_aoe, i.t - 1)
                tab = tabV0.rearrange("p b q j d -> p b q (j d)")[:, span(i.m // 2), i.q, :]
                MM(ps[5 + i.q][:, :], aT0[:, i.q, :], tab.rearrange("p a n -> p (a n)"),
                   start=True, stop=True).then_inc(s_ao, 1)

            pe.wait_ge(s_const, 7)
            pe.wait_ge(s_p0e, 3)
            def router_rows0(i):
                pe.wait_ge(s_gn, i.t + 1)
                wait(pe, s_gte, i.t)
                transposes(ps[7], xn_r[:, i.q, :], 4).then_inc(s_gt, 1)

            def router_logits0(i):
                pe.wait_ge(s_gte, i.t + 1)
                wait(pe, s_gle, i.t - 1)
                pe.wait_ge(s_scb, at_most(i.t + 3, NPAIR))
                for j in range(2):
                    for k in range(FK):
                        n = 2 * j + k
                        ins = MM(ps[2 + i.q][:, P + E0 * j:P + E0 * j + E0], gx[:, i.q, n * P:n * P + P],
                                 gateT[:, k, 0:E0], start=(k == 0), stop=(k == FK - 1))
                ins.then_inc(s_gl, 1)

            rows_t0(Tile(0, 0))
            scores0(Tile(0, 0))

            def attend0(i):
                if i.plus(-3).exists(0, NPAIR):
                    router_logits0(i.plus(-3))
                if i.plus(1).exists(0, NPAIR):
                    rows_t0(i.plus(1))
                    scores0(i.plus(1))
                if i.exists(0, NPAIR):
                    weights_t0(i)
                    values0(i)
                if i.plus(-2).exists(0, NPAIR):
                    router_rows0(i.plus(-2))

            pe.wait_ge(s_rt, 16 * 3)
            over_tiles(pe, 0, NPAIR + 4, attend0, lead=6, tail=6)

            def ranks(l, columns):
                mask = R[l]["mask"]
                pe.wait_ge(s_mask, l + 1)
                MM(earlier[l], tri_b[:, :], mask[:, 0:NT * columns],
                   start=True, stop=False, skip_group_check=True)
                for n in range(1, NT):
                    MM(earlier[l][:, n * columns:NT * columns], ones_b[:, :], mask[:, 0:(NT - n) * columns],
                       start=False, stop=(n == NT - 1), skip_group_check=True)
                for n in range(NT):
                    ins = MM(counts[l], ones_b[:, :], mask[:, n * columns:(n + 1) * columns],
                             start=(n == 0), stop=(n == NT - 1))
                ins.then_inc(s_rank, 1)

            def expert_row(l, tiles):
                pe.wait_ge(s_te, l + 1)
                MM(expert_of[l], R[l]["te_col"][0:tiles, 0:1], ident[0:tiles, 0:tiles],
                   start=True, stop=True).then_inc(s_ter, 1)

            def slot_tokens(l, chosen):
                for c in range(chosen * NT):
                    pe.wait_ge(s_hot, l * K0 * NT + c + 1)
                    ins = MM(token_of[l], hot_lo[l][c // NT][:, c % NT, :], hot_hi[l][:, c, :],
                             start=(c == 0), stop=(c == chosen * NT - 1))
                ins.then_inc(s_inv, 1)

            ranks(0, E0)

            pe.wait_ge(s_gle, NPAIR)
            pe.wait_ge(s_aoe, NPAIR)
            pe.wait_ge(s_wkq, 16 * 2)

            def blocks(base):
                for hp in range(HP1):
                    g = hp // 4
                    if hp % 4 == 0 and base:
                        pe.wait_ge(s_l1e, 10)
                    for k in range(FK):
                        ins = MM(ps[g][:, (hp % 4) * P:(hp % 4) * P + P], att_in_v[:, k, hp * P:hp * P + P],
                                 ctxT[:, k, :], start=(k == 0), stop=(k == FK - 1))
                    if hp % 4 == 3:
                        ins.then_inc(s_l1p, 1)

            blocks(0)
            for n in range(8):
                k, g = n // 4, n % 4
                pe.wait_ge(s_l1e, max(2, n + 1))
                for h in range(2):
                    hp = 2 * g + h
                    ins = MM(ps[2 + n % 2][:, 256 * h:256 * h + 256], att_w_v[:, hp, k * P:k * P + P],
                             blk1_v[:, hp].rearrange("p b c s -> p (b c s)"), start=True, stop=True)
                ins.then_inc(s_l1p, 1)
            expert_row(0, T0)
            pe.wait_ge(s_wv, 16)
            blocks(10)
            pe.wait_ge(s_wo, 16)
            for n in range(8):
                b, g = n // 4, n % 4
                pe.wait_ge(s_l1e, max(12, n + 11))
                for h in range(2):
                    hp = 2 * g + h
                    ins = MM(ps[2 + n % 2][:, 256 * h:256 * h + 256],
                             blk1_v[:, hp, b].rearrange("p c s -> p (c s)"), att_w_v[:, hp, :],
                             start=True, stop=True)
                ins.then_inc(s_l1p, 1)
            pe.wait_ge(s_l1e, 20)
            slot_tokens(0, K0)

            pe.wait_ge(s_info, 1)

            def rows_e0(i):
                pe.wait_ge(s_ex[i.q], 16 * (i.m + 1))
                wait(pe, s_eXe, i.t - 1)
                transposes(ps[i.p], xr0[:, i.q, :], FK).then_inc(s_eX, 1)

            slot_at = Registers(lambda t: ring_slot(pe, t))

            def hidden0(i):
                r = slot_at[i]
                pe.wait_ge(s_eXe, i.t + 1)
                pe.wait_ge(s_ew[i.p], 16 * (i.half + 1))
                wait(pe, s_ehb, i.t - 1)
                for k in range(FK):
                    w = ring[:, span(r), k * 2 * F0:(k + 1) * 2 * F0].rearrange("p a n -> p (a n)")
                    ins = MM(ps[2 + i.p][:, :], xT0[:, i.p, k, :], w, start=(k == 0), stop=(k == FK - 1))
                ins.then_inc(s_eH, 1)

            def hidden_t0(i):
                pe.wait_ge(s_ehs, i.t + 1)
                wait(pe, s_eHTe, i.t)
                transposes(ps[4], hs0[:, i.p, :], F0 // P).then_inc(s_eHT, 1)

            def out0(i):
                r = slot_at[i]
                pe.wait_ge(s_eHTe, i.t + 1)
                wait(pe, s_ey, i.t - 1)
                for k in range(F0 // P):
                    lo = FK * 2 * F0 + k * D
                    w = ring[:, span(r), lo:lo + D].rearrange("p a n -> p (a n)")
                    ins = MM(ps[5 + i.p][:, 0:D], hT0[:, i.p, k, :], w, start=(k == 0), stop=(k == F0 // P - 1))
                ins.then_inc(s_eO, 1)

            def expert0(i):
                slot_at.begin(i)
                for j in (i.plus(-2), i):
                    if j.exists(0, T0):
                        slot_at.load(j)
                if i.plus(-2).exists(0, T0):
                    hidden_t0(i.plus(-2))
                if i.plus(1).exists(0, T0):
                    rows_e0(i.plus(1))
                if i.exists(0, T0):
                    hidden0(i)
                if i.plus(-2).exists(0, T0):
                    out0(i.plus(-2))

            rows_e0(Tile(0, 0, 4))
            over_tiles(pe, 0, T0 + 2, expert0, lead=4, tail=4, u=4)

            def rows_t1(i):
                pe.wait_ge(s_1n, i.t + 1)
                wait(pe, s_1te, i.t)
                transposes(ps[0], xn1[:, i.q, :], FK).then_inc(s_1t, 1)

            def scores1(i):
                pe.wait_ge(s_1te, i.t + 1)
                wait(pe, s_1m, i.t - 1)
                b = i.m // 4
                for g in range(2):
                    for k in range(FK):
                        tab = tabA[:, span(b), k, 512 * g:512 * g + 512].rearrange("p a n -> p (a n)")
                        ins = MM(ps[1 + 2 * i.q + g][:, :], xT1[:, i.q, k, :], tab,
                                 start=(k == 0), stop=(k == FK - 1))
                ins.then_inc(s_1s, 1)

            def weights_t1(i):
                pe.wait_ge(s_1w, i.t + 1)
                wait(pe, s_1wte, i.t)
                transposes(ps[5], sc1[:, i.q, 0:512], 4)
                transposes(ps[6], sc1[:, i.q, 512:1024], 4).then_inc(s_1wt, 1)

            def values1(i):
                pe.wait_ge(s_1wte, i.t + 1)
                wait(pe, s_1r, i.t)
                b = i.m // 4
                for hp in range(HP1):
                    tab = tabV[:, span(b), hp, :].rearrange("p a n -> p (a n)")
                    ins = MM(ps[7][:, 0:D], aT1[:, hp, :], tab, start=(hp == 0), stop=(hp == HP1 - 1))
                ins.then_inc(s_1o, 1)

            def router_rows1(i):
                pe.wait_ge(s_rn, i.t + 1)
                wait(pe, s_rte, i.t)
                pe.wait_ge(s_1te, at_most(i.t + 4, NT))
                transposes(ps[0][:, D:2 * D], xn_f[:, i.q, :], FK).then_inc(s_rtr, 1)

            def router_logits1(i):
                pe.wait_ge(s_rte, i.t + 1)
                wait(pe, s_rle, i.t)
                pe.wait_ge(s_1r, at_most(i.t + 2, NT))
                for k in range(FK):
                    ins = MM(ps[7][:, D:D + E1], gx[:, i.q, k * P:k * P + P], gateT[:, k, E0:E0 + E1],
                             start=(k == 0), stop=(k == FK - 1))
                ins.then_inc(s_rl, 1)

            def attend1(i):
                if i.plus(1).exists(0, NT):
                    scores1(i.plus(1))
                if i.plus(-2).exists(0, NT):
                    router_rows1(i.plus(-2))
                if i.plus(2).exists(0, NT):
                    rows_t1(i.plus(2))
                if i.plus(-3).exists(0, NT):
                    router_logits1(i.plus(-3))
                if i.plus(-1).exists(0, NT):
                    values1(i.plus(-1))
                if i.exists(0, NT):
                    weights_t1(i)

            rows_t1(Tile(0, 0))
            attend1(Tile(-1, 1))
            over_tiles(pe, 0, NT + 4, attend1, lead=4, tail=6)

            pe.wait_ge(s_shared, 1)
            pe.wait_ge(s_w1, 16 * EARLY)
            pe.wait_ge(s_1r, NT)
            pe.wait_ge(s_rle, NT)

            def rows_e1(i, kind):
                if kind == "routed":
                    pe.wait_ge(s_fr[i.q], 16 * (i.plus(-SHARED_A).m + 1))
                else:
                    pe.wait_ge(s_fx[i.q], 16 * ((i if kind == "first" else i.plus(-T1)).m + 1))
                wait(pe, s_fXe, i.t)
                if isinstance(i.t, int) and i.t in (4, 6, 9):
                    pe.wait_ge(*{4: (s_rread, 3), 6: (s_rread, 4), 9: (s_tok, 2)}[i.t])
                transposes(ps[0], xr1[:, i.q, :], FK).then_inc(s_fX, 1)

            place = Registers(lambda t: pe.value_load(info[1][0:1, 0, span(t)], min_val=0, max_val=E1))

            def gate_up(i, c):
                e = place[i]
                u = 2 * i.t + c
                if c == 0:
                    pe.wait_ge(s_fXe, i.t + 1)
                wait(pe, s_fh, u - 1)
                for g in range(2):
                    for k in range(FK):
                        lo = ((k * NC1 + c) * 2 + g) * FC1
                        w = w1s[:, span(e), lo:lo + FC1].rearrange("p a n -> p (a n)")
                        ins = MM(ps[1 + 2 * c + g][:, 0:FC1], xTe[:, i.q, k, :], w,
                                 start=(k == 0), stop=(k == FK - 1))
                ins.then_inc(s_fG, 1)

            def hidden_t1(i, c):
                u = 2 * i.t + c
                pe.wait_ge(s_fh, u + 1)
                wait(pe, s_fHTe, u)
                for n, (lo, width) in enumerate(SUB1):
                    ins = pe.transpose(ps[5][0:width, n * P:n * P + P], hh[:, c, lo:lo + width], ident[:, :])
                ins.then_inc(s_fHT, 1)

            def out1(i, c):
                e = place[i]
                u = 2 * i.t + c
                pe.wait_ge(s_fHTe, u + 1)
                if c == 0:
                    wait(pe, s_fy, i.t - 1)
                for n, (_, width) in enumerate(SUB1):
                    lo = GU1 + (c * 3 + n) * D
                    w = w1s[0:width, span(e), lo:lo + D].rearrange("p a n -> p (a n)")
                    ins = MM(ps[6 + i.q][:, 0:D], hTe[0:width, c, n, :], w,
                             start=(c == 0 and n == 0), stop=(c == 1 and n == 2))
                ins.then_inc(s_fO, 1)

            def expert1(i, kind_next):
                last = i.plus(-1)
                place.begin(i)
                for j in (last, i):
                    if j.exists(0, N1):
                        place.load(j)
                if i.exists(0, N1):
                    gate_up(i, 0)
                if last.exists(0, N1):
                    out1(last, 0)
                    hidden_t1(last, 1)
                if i.plus(1).exists(0, N1):
                    rows_e1(i.plus(1), kind_next)
                if i.exists(0, N1):
                    gate_up(i, 1)
                if last.exists(0, N1):
                    out1(last, 1)
                if i.exists(0, N1):
                    hidden_t1(i, 0)

            def segment(lo, hi, kind, after):
                def body(i):
                    last = isinstance(i.t, int) and i.t == hi - 1
                    expert1(i, after if last else kind)
                over_tiles(pe, lo, hi, body)

            rows_e1(Tile(0, 0), "first")
            for t in range(SHARED_A):
                if t == SHARED_A - 1:
                    pe.wait_ge(s_w1b, 16 * (8 - EARLY))
                expert1(Tile(t // 2, t % 2), "first" if t < SHARED_A - 1 else "routed")
                if t in (2, 4, 7):
                    pe.wait_ge(s_fXe, t + 2)
                if t == 2:
                    ranks(1, EC1)
                elif t == 4:
                    expert_row(1, T1)
                elif t == 7:
                    slot_tokens(1, K1)
            pe.wait_ge(s_info, 2)
            segment(SHARED_A, MID1, "routed", "last")
            segment(MID1, N1, "last", None)
            expert1(Tile(N1 // 2, 0), None)


_NAMES = ["x", "mask", "ctxT", "Wk0T", "Wq0", "Wv0T", "bkq", "bv", "gateT", "gate_b", "norm_scale",
          "wk1", "wq1T", "wv1", "wo1", "w_e0", "w_e1"]


def arrange(i):
    f = {k: np.asarray(v) for k, v in i.items()}

    def by_part(w):
        return w.reshape(-1, P, w.shape[-1]).transpose(1, 0, 2)

    r = {"x": f["x"], "mask": f["mask_Bx1xSxS2_ff0"][:, 0]}
    r["ctxT"] = by_part(f["ctx_1024"].reshape(B * S2, D).T)
    r["Wk0T"], r["Wv0T"] = by_part(f["L0_xattn_Wk"].T), by_part(f["L0_xattn_Wv"].T)
    r["Wq0"] = by_part(f["L0_xattn_Wq"])
    r["bkq"] = np.stack([f["L0_xattn_bk"].reshape(2, P), f["L0_xattn_bq"].reshape(2, P)]).transpose(2, 0, 1)
    r["bv"] = f["L0_xattn_bv"][None]
    r["gateT"] = by_part(np.concatenate([f["L0_ffn_gate_w"], f["L1_ffn_wr"]]).T)
    r["gate_b"] = np.concatenate([f["L0_ffn_gate_b"], f["L1_ffn_rb"]])[None]
    r["norm_scale"] = f["L0_ffn_norm_scale"][None]
    r["wk1"], r["wv1"] = (by_part(f[k].reshape(D, H1 * DH)) for k in ("L1_xattn_wk", "L1_xattn_wv"))
    r["wq1T"] = by_part(f["L1_xattn_wq"].reshape(D, H1 * DH).T)
    r["wo1"] = by_part(f["L1_xattn_wo"].reshape(H1 * DH, D))
    w1 = f["L0_ffn_w1"].reshape(E0, F0, 2, FK, P).transpose(0, 4, 3, 2, 1).reshape(E0, P, FK * 2 * F0)
    w2 = f["L0_ffn_w2"].reshape(E0, D, F0 // P, P).transpose(0, 3, 2, 1).reshape(E0, P, (F0 // P) * D)
    b1 = f["L0_ffn_b1"].reshape(E0, F0, 2).transpose(0, 2, 1).reshape(E0, 2 * F0)
    b = np.concatenate([b1, f["L0_ffn_b2"]], axis=1)
    r["w_e0"] = np.concatenate([w1, w2, np.broadcast_to(b[:, None], (E0, P, B0))], axis=2)
    g, u, d = (np.concatenate([f["L1_ffn_s" + k][None], f["L1_ffn_r" + k]]) for k in "gud")
    gu = np.stack([g, u]).reshape(2, 8, NC1, FC1, FK, P).transpose(1, 5, 4, 2, 0, 3).reshape(8, P, GU1)
    d = d.reshape(8, D, NC1, FC1).transpose(0, 2, 3, 1)
    dd = np.zeros((8, NC1, 3 * P, D), np.float32)
    dd[:, :, :FC1] = d
    dd = dd.reshape(8, NC1, 3, P, D).transpose(0, 3, 1, 2, 4).reshape(8, P, NC1 * 3 * D)
    r["w_e1"] = np.concatenate([gu, dd], axis=2)
    return {k: np.ascontiguousarray(r[k]) for k in _NAMES}


def kernel(**inputs):
    import concourse.bacc as _bacc
    from concourse.bass_utils import run_bass_kernel_spmd as _run

    nc = _bacc.Bacc("TRN2", target_bir_lowering=False, num_devices=1)
    arrays = arrange(inputs)
    aps = {k: nc.dram_tensor("in_" + k, v.shape, F32, kind="ExternalInput").ap() for k, v in arrays.items()}
    out = nc.dram_tensor("out", (B, S, D), F32, kind="ExternalOutput").ap()
    build(nc, aps, out)
    r = _run(nc, [{"in_" + k: v for k, v in arrays.items()}], core_ids=[0])
    return r.results[0]["out"]
```
